# Optimizing a Trainium2 kernel written in Bass

```python
import numpy as np
import jax
import jax.numpy as jnp

def _softmax(x, axis=-1):
    return jax.nn.softmax(x, axis=axis)

def _gelu(x):
    return jax.nn.gelu(x, approximate=True)

def _silu(x):
    return jax.nn.silu(x)

def _sigmoid(x):
    return jax.nn.sigmoid(x)

def _layernorm(x, axis=-1, eps=1e-05):
    m = jnp.mean(x, axis=axis, keepdims=True)
    v = jnp.var(x, axis=axis, keepdims=True)
    return (x - m) / jnp.sqrt(v + eps)

def _scatter_add(tgt, idx, src, axis=0):
    return tgt.at[idx].add(src)

def _segment_sum(src, seg, n):
    return jax.ops.segment_sum(src, seg, n)
kernel_name = 'mk_decoder_postln_d1_seqx_r8_32297d'

def setup_inputs(seed: int=0):
    np.random.seed(seed)
    _w = jnp.asarray

    def _rec_inputs():
        import jax
        import jax.numpy as jnp
        _rk = jax.random.key(seed)
        x = 7.22e-05 + 1 * jax.random.normal(jax.random.fold_in(_rk, 1), (32, 56, 128), jnp.float32)
        _lenS = 56 - jax.random.randint(jax.random.fold_in(_rk, 7), (32,), 0, max(1, 56 // 4) + 1, jnp.int32)
        _lenS2 = 1500 - jax.random.randint(jax.random.fold_in(_rk, 8), (32,), 0, max(1, 1500 // 4) + 1, jnp.int32)
        _ctx_768P = jax.random.normal(jax.random.fold_in(_rk, 11), (32, 16, 96), jnp.float32)
        _ctx_768c = jax.random.dirichlet(jax.random.fold_in(_rk, 511), 0.3 * jnp.ones((16,), jnp.float32), (32, 1500))
        _ctx_768t = jnp.einsum('bsk,bkd->bsd', _ctx_768c, _ctx_768P)
        _ctx_768t = _ctx_768t * jax.lax.rsqrt(jnp.mean(jnp.square(_ctx_768t)) + 1e-12) * 0.953939
        ctx_768 = -0.000191848 + 0.999787 * (_ctx_768t + 0.3 * jax.random.normal(jax.random.fold_in(_rk, 611), (32, 1500, 96), jnp.float32))
        return (x, ctx_768)
    x, ctx_768 = _rec_inputs()

    def _L0_attn_setup():
        import jax, jax.numpy as jnp
        import numpy as np
        B, S, D = (4, 256, 128)
        key = jax.random.key(seed)
        k1, k2, k3, k4 = jax.random.split(key, 4)
        x = jax.random.normal(k1, (B, S, D), dtype=jnp.float32)
        scale = 1.0 / np.sqrt(D)
        wq = jax.random.uniform(k2, (D, D), dtype=jnp.float32, minval=-scale, maxval=scale)
        wk = jax.random.uniform(k3, (D, D), dtype=jnp.float32, minval=-scale, maxval=scale)
        wv = jax.random.uniform(k4, (D, D), dtype=jnp.float32, minval=-scale, maxval=scale)
        return {'x': x, 'wq': wq, 'wk': wk, 'wv': wv}
    _L0_attn_all = _L0_attn_setup()
    _L0_attn_in = {k: v for k, v in _L0_attn_all.items() if k in ('wq', 'wk', 'wv')}
    del _L0_attn_all

    def _L0_xattn_setup():
        import jax, jax.numpy as jnp
        import numpy as np
        NUM_HEADS = 16
        CLAMP = 10000.0
        key = jax.random.key(seed)
        ks = jax.random.split(key, 8)
        B, Nq, Nkv, Cq, Ckv = (4, 256, 256, 128, 96)
        s_q = 1.0 / np.sqrt(Cq)
        s_kv = 1.0 / np.sqrt(Ckv)
        return {'query': jax.random.normal(ks[0], (B, Nq, Cq), jnp.float32), 'key_value': jax.random.normal(ks[1], (B, Nkv, Ckv), jnp.float32), 'Wq': jax.random.normal(ks[2], (Cq, Cq), jnp.float32) * s_q, 'bq': jnp.zeros((Cq,), jnp.float32), 'Wk': jax.random.normal(ks[3], (Ckv, Cq), jnp.float32) * s_kv, 'bk': jnp.zeros((Cq,), jnp.float32), 'Wv': jax.random.normal(ks[4], (Ckv, Cq), jnp.float32) * s_kv, 'bv': jnp.zeros((Cq,), jnp.float32), 'Wo': jax.random.normal(ks[5], (Cq, Cq), jnp.float32) * s_q, 'bo': jnp.zeros((Cq,), jnp.float32)}
    _L0_xattn_all = _L0_xattn_setup()
    _L0_xattn_in = {k: v for k, v in _L0_xattn_all.items() if k in ('Wq', 'bq', 'Wk', 'bk', 'Wv', 'bv', 'Wo', 'bo')}
    del _L0_xattn_all

    def _L0_ffn_setup():
        import jax, jax.numpy as jnp
        import numpy as np
        import math
        EMBED_DIM = 128
        FFN_DIM = 512
        N_EXPERTS = 8
        TOP_K = 2
        CAP_FACTOR = 1.25
        key = jax.random.key(seed)
        k0, k1, k2, k3 = jax.random.split(key, 4)
        B, S = (4, 256)
        x = jax.random.normal(k0, (B, S, EMBED_DIM), dtype=jnp.float32)
        Wr = jax.random.normal(k1, (EMBED_DIM, N_EXPERTS), dtype=jnp.float32) * 0.02
        W1 = jax.random.normal(k2, (N_EXPERTS, EMBED_DIM, FFN_DIM), dtype=jnp.float32) * 0.02
        W2 = jax.random.normal(k3, (N_EXPERTS, FFN_DIM, EMBED_DIM), dtype=jnp.float32) * 0.02
        return {'x': x, 'Wr': Wr, 'W1': W1, 'W2': W2}
    _L0_ffn_all = _L0_ffn_setup()
    _L0_ffn_in = {k: v for k, v in _L0_ffn_all.items() if k in ('Wr', 'W1', 'W2')}
    del _L0_ffn_all
    return {'x': x, 'ctx_768': ctx_768, 'L0_attn_wq': _L0_attn_in['wq'], 'L0_attn_wk': _L0_attn_in['wk'], 'L0_attn_wv': _L0_attn_in['wv'], 'L0_xattn_Wq': _L0_xattn_in['Wq'], 'L0_xattn_bq': _L0_xattn_in['bq'], 'L0_xattn_Wk': _L0_xattn_in['Wk'], 'L0_xattn_bk': _L0_xattn_in['bk'], 'L0_xattn_Wv': _L0_xattn_in['Wv'], 'L0_xattn_bv': _L0_xattn_in['bv'], 'L0_xattn_Wo': _L0_xattn_in['Wo'], 'L0_xattn_bo': _L0_xattn_in['bo'], 'L0_ffn_Wr': _L0_ffn_in['Wr'], 'L0_ffn_W1': _L0_ffn_in['W1'], 'L0_ffn_W2': _L0_ffn_in['W2']}

def reference(x, ctx_768, L0_attn_wq, L0_attn_wk, L0_attn_wv, L0_xattn_Wq, L0_xattn_bq, L0_xattn_Wk, L0_xattn_bk, L0_xattn_Wv, L0_xattn_bv, L0_xattn_Wo, L0_xattn_bo, L0_ffn_Wr, L0_ffn_W1, L0_ffn_W2):
    import jax
    import jax.numpy as jnp

    def _L0_attn_ref(x, wq, wk, wv):
        import jax, jax.numpy as jnp
        import numpy as np
        B, S, D = (4, 256, 128)
        d = wq.shape[0]
        q = x @ wq.T
        k = x @ wk.T
        v = x @ wv.T
        scores = jnp.einsum('bqd,bkd->bqk', q, k) / np.sqrt(float(d))
        a = jax.nn.softmax(scores, axis=-2)
        a = jnp.triu(a)
        attn = jnp.swapaxes(a, -2, -1) @ v
        return attn

    def _L0_xattn_ref(query, key_value, Wq, bq, Wk, bk, Wv, bv, Wo, bo):
        import jax, jax.numpy as jnp
        import numpy as np
        NUM_HEADS = 16
        CLAMP = 10000.0
        B, Nq, Cq = query.shape
        Nkv = key_value.shape[1]
        H = NUM_HEADS
        D = Cq // H
        scale = D ** (-0.5)
        q = (query @ Wq + bq).reshape(B, Nq, H, D).transpose(0, 2, 1, 3)
        k = (key_value @ Wk + bk).reshape(B, Nkv, H, D).transpose(0, 2, 1, 3)
        v = (key_value @ Wv + bv).reshape(B, Nkv, H, D).transpose(0, 2, 1, 3)
        attn = jnp.einsum('bhqd,bhkd->bhqk', q, k) * scale
        attn = jnp.clip(attn, -CLAMP, CLAMP)
        attn = jax.nn.softmax(attn, axis=-1)
        attn = jnp.where(jnp.any(jnp.isnan(attn)), jnp.asarray(1.0 / Nkv, attn.dtype), attn)
        x = jnp.einsum('bhqk,bhkd->bqhd', attn, v).reshape(B, Nq, Cq)
        return x @ Wo + bo

    def _L0_ffn_ref(x, Wr, W1, W2):
        import jax, jax.numpy as jnp
        import numpy as np
        import math
        EMBED_DIM = 128
        FFN_DIM = 512
        N_EXPERTS = 8
        TOP_K = 2
        CAP_FACTOR = 1.25
        B, S, D = x.shape
        t = B * S
        xf = x.reshape(t, D)
        probs = jax.nn.softmax(xf.astype(jnp.float32) @ Wr, axis=-1)
        topk_probs, topk_experts = jax.lax.top_k(probs, TOP_K)
        cap = max(math.ceil(t * TOP_K * CAP_FACTOR / N_EXPERTS), 1)
        y = jnp.zeros_like(xf)
        for e in range(N_EXPERTS):
            mask = topk_experts == e
            gate = jnp.sum(jnp.where(mask, topk_probs, 0.0), axis=-1)
            has = jnp.any(mask, axis=-1)
            g_masked = jnp.where(has, gate, -jnp.inf)
            vals, idx = jax.lax.top_k(g_masked, cap)
            g = jnp.where(jnp.isfinite(vals), vals, 0.0)
            xe = xf[idx]
            h = jax.nn.relu(xe @ W1[e]) @ W2[e]
            y = y.at[idx].add(g[:, None] * h)
        return y.reshape(B, S, D)
    x = _layernorm(x + _L0_attn_ref(x, L0_attn_wq, L0_attn_wk, L0_attn_wv), axis=-1)
    x = _layernorm(x + _L0_xattn_ref(x, ctx_768, L0_xattn_Wq, L0_xattn_bq, L0_xattn_Wk, L0_xattn_bk, L0_xattn_Wv, L0_xattn_bv, L0_xattn_Wo, L0_xattn_bo), axis=-1)
    x = _layernorm(x + _L0_ffn_ref(x, L0_ffn_Wr, L0_ffn_W1, L0_ffn_W2), axis=-1)
    return x

_drawn_inputs = setup_inputs


def setup_inputs(seed=0):
    import zlib

    import numpy as np

    out = dict(_drawn_inputs(seed))
    spreads = {'L0_xattn_bq': (0.0, 0.355),
     'L0_xattn_bk': (0.0, 0.8),
     'L0_xattn_bv': (0.0, 0.1),
     'L0_xattn_bo': (0.0, 0.1)}
    factors = {'L0_attn_wq': 2.86,
     'L0_attn_wk': 2.812,
     'L0_ffn_Wr': 3.915,
     'L0_ffn_W1': 4.146,
     'L0_ffn_W2': 3.473}
    for name, (base, spread) in spreads.items():
        noise = np.random.default_rng([zlib.crc32(name.encode()), seed]).standard_normal(out[name].shape)
        drawn = base * np.exp(spread * noise) if base else spread * noise
        out[name] = jnp.asarray(drawn.astype(out[name].dtype))
    for name, factor in factors.items():
        out[name] = (out[name] * factor).astype(out[name].dtype)
    return out
```

```python
import math
from contextlib import ExitStack

import concourse.bass as bass
from concourse import mybir

F32 = mybir.dt.float32
F32R = mybir.dt.float32r
I32 = mybir.dt.int32
ALU = mybir.AluOpType
ACT = mybir.ActivationFunctionType
AX = mybir.AxisListType

B, S, D = 32, 56, 128
NK, DC = 1500, 96
H, DH = 16, 8
NE, FF, TOPK = 8, 512, 2
CAP = max(math.ceil(B * S * TOPK * 1.25 / NE), 1)
EPS, CLAMP = 1e-5, 10000.0
TT = 2 * S
NT = B // 2
QT = 4
NQ = NT // QT
QC = QT * TT
CK = 125
NC = NK // CK
KB = 500
NB = NK // KB
G2 = H // 2
V_SLOTS = (9, 10, 11)
SLOTS = 4
FC = FF // 128
NEG = -3.0e38
HQ = H * S
RG = HQ // 128
HG = H // 4
AP_ = RG * NB
SUM = 0
V3, V1 = 3 * DH + 1, DH + 1
VC = 4 * (V3 + V1)
PLAIN = 9000.0
ARENA = 19700
PRIME = 4


def decoder_kernel(nc, x, ctx_in, wq, wk, wv, xWq, xbq, xWk, xbk, xWv, xbv, xWo, xbo, Wr, W1, W2, out):
    stack = ExitStack()

    def sb(name, shape, dt=F32):
        return stack.enter_context(nc.sbuf_tensor(name, shape, dt))

    def sem(name):
        return stack.enter_context(nc.semaphore(name))

    with stack:
        psum = stack.enter_context(nc.psum_tensor("psum", [128, 8, 512], F32))
        bank = [psum[:, i, :] for i in range(8)]
        ident = sb("ident", [128, 128])
        other_batch = sb("other_batch", [TT, TT])
        causal = sb("causal", [TT, TT])
        head_rows = sb("head_rows", [128, H])
        pair_rows = sb("pair_rows", [TT, 2])
        fold_q = sb("fold_q", [TT, S])
        expert_rows = sb("expert_rows", [128, 128])
        before_rows = sb("before_rows", [128, 128])
        ones = sb("ones", [128, 128])
        minus_half = sb("minus_half", [128, QT])
        index_prio = sb("index_prio", [TT, NE])
        perm = sb("perm", [128, SLOTS, 128])
        w_sb = {n: sb(n + "_sb", [128, 128]) for n in ("wq", "wk", "wv", "xWq", "xWo")}
        qk = sb("qk", [128, 128])
        wvT = sb("wvT", [128, 128])
        bq_col = sb("bq_col", [128, 1])
        WkA = sb("WkA", [DC + 1, 128])
        WvA = sb("WvA", [DC + 1, 128])
        WoP = sb("WoP", [128, SLOTS, 128])
        bo_row = sb("bo_row", [1, 128])
        Wr_sb = sb("Wr_sb", [128, NE])
        x1_all = sb("x1_all", [TT, NT, D])
        x2_all = x1_all
        Qt_all = sb("Qt_all", [128, B * S])
        OS_all = sb("OS_all", [128, SLOTS, B * S])
        hT = OS_all
        K_hi = sb("K_hi", [128, 2, NK], F32R)
        K_st = sb("K_st", [DC + 1, 2, HG, NK], F32R)
        Q_st = sb("Q_st", [DC + 1, 2, HG, 4, S], F32R)
        Q_bd = sb("Q_bd", [128, 2, H, S], F32R)
        max_row = sb("max_row", [RG, 128], F32R)
        four_heads = sb("four_heads", [DC, 4])
        sum_rows = sb("sum_rows", [128, 128])
        sum_row = sb("sum_row", [128, 1])
        arena = sb("arena", [128, ARENA])
        used = [0]

        def at(parts, *shape):
            n = math.prod(shape)
            o = used[0]
            used[0] += n
            assert used[0] <= ARENA, used[0]
            v = arena[0:parts, o:o + n]
            if len(shape) == 2:
                v = v.rearrange("p (a b) -> p a b", b=shape[1])
            elif len(shape) == 3:
                v = v.rearrange("p (a b c) -> p a b c", b=shape[1], c=shape[2])
            return v

        stats = at(TT, QT, 6)
        mv = at(TT, QT, 2)
        ve = at(TT, QT)
        rstd = at(TT, QT)
        pad = at(1, 1)
        Qs_all = at(DC, HG, B * S)
        start = used[0]
        xq = at(TT, QT, D)
        xT = at(128, QC)
        u_sb = at(128, QC)
        v_sb = at(TT, QT, D)
        s_sb = at(TT, QT, TT)
        e_sb = at(TT, QT, TT)
        aT = at(TT, QT, TT)
        nm = at(TT, QT)
        rs = at(TT, QT)
        ri = at(TT, QT)
        y = at(TT, QT, D)
        xn = at(TT, QT, D)
        OSq = at(128, SLOTS, QC)
        after3 = used[0]
        Q_hi = at(128, B * S)
        Q_lo = at(128, B * S)
        used[0] = start
        C2 = at(CK, NC, DC)
        ctxT2 = at(DC + 1, 2, NK)
        V2 = [at(CK, NC, VC) for _ in range(2)]
        P2 = [at(CK, HQ) for _ in range(2)]
        K_lo = at(128, NK)
        O_sb = at(128, SLOTS * S)
        R_sb = at(128, SLOTS * S)
        mx = at(128, RG, NB)
        m2x = at(128, RG)
        m_high = at(128, RG)
        m_low = at(128, RG)
        chk = at(128, 1)
        chk_sum = at(128, 1)
        bad = at(128, 2)
        used[0] = start
        C = at(CK, NC, DC)
        ctxT = at(DC + 1, NK)
        KT = at(128, NK)
        V = at(CK, NC, 128)
        Qbd = at(128, H, S)
        Sc = at(TT, NK)
        P = at(TT, NK)
        PT = at(CK, NC, TT)
        Om = at(TT, 128)
        OT = at(128, 2, S)
        c1 = at(TT, 1)
        c2 = at(TT, 1)
        rowmax = at(TT, 1)
        negmax = at(TT, 1)
        rowsum = at(TT, 1)
        rinv = at(TT, 1)
        numbers = at(TT, 1)
        nan_mask = at(TT, 1)
        nan_col = at(128, 1)
        nan_int = at(128, 1).bitcast(I32)
        OM_all = at(128, SLOTS, B)
        used[0] = after3
        x2T = at(128, NT * TT)
        pr = at(TT, NT, NE)
        pw = at(TT, NT, NE)
        eq = at(TT, NT, NE)
        hot = at(TT, NT, NE)
        mask = at(TT, NT, NE)
        m1 = at(TT, NT)
        m2 = at(TT, NT)
        gsel = at(TT, NE, NT)
        G = at(128, TT)
        gscr = at(128, TT)
        gtm = at(128, TT)
        eqm = at(128, TT)
        pref = at(128, TT)
        cand = at(128, 1)
        fac = at(128, 1)
        cnt = at(128, 2)
        room = at(128, 1)
        Gs = at(128, TT)
        gate = at(TT, NE, NT)
        gate_e = at(TT, 2, NT)
        w1 = at(128, 2, FF)
        w2 = at(128, 2, FC, 128)
        flag_int = sb("flag_int", [1, 1], I32)
        zrow = sb("zrow", [128, TT])
        thr = sb("thr", [128, 1])
        stepv = sb("stepv", [128, 1])

        dve_step = sem("dve_step")
        clamp_step = sem("clamp_step")
        pool_step = sem("pool_step")
        consts = sem("consts")
        weights = sem("weights")
        w_ps = sem("w_ps"); w_ev = sem("w_ev")

        S1 = {n: sem("s1_" + n) for n in ("x", "xTp", "xT", "up", "u", "vp", "v", "sp", "max", "e", "a", "aTp", "aT", "op",
                                          "y", "ve", "rstd", "xn", "x1", "xnTp", "xnT", "qp", "q")}
        S2 = {n: sem("s2_" + n) for n in ("c", "cTp", "cT", "kp", "k", "vp", "v", "qbd", "sp", "s", "m", "e", "pTp", "pT", "op", "om",
                                          "otp", "ot", "osp", "os", "nan", "nanrow", "nanall", "fix")}
        S3 = {n: sem("s3_" + n) for n in ("osq", "op", "y", "ve", "rstd", "xn", "xnTp", "xnT", "x2")}
        S4 = {n: sem("s4_" + n) for n in ("lg", "pr", "e", "g", "gTp", "cnt", "tot", "eqc", "eqp", "gs", "gsTp", "gate", "w", "up", "h", "dn", "acc",
                                          "ve", "rstd", "xn", "out")}

        F = {n: sem("f_" + n) for n in ("cTp", "cT", "kp", "k", "khi", "klo", "vp", "v", "qa", "qs", "ap", "am", "mx", "ab", "m", "mTp", "mr",
                                        "bp", "e", "pv", "o", "rp", "r", "os", "chk", "ready", "bad", "sum", "flag")}
        D_ = {n: sem("d_" + n) for n in ("c", "khi0", "khi1", "klo0", "klo1", "mrow", "q")}
        primed = [s_ for d in (S1, S2, S3, S4) for n, s_ in d.items() if n not in ("x", "c", "w", "out")] + list(F.values())

        def periods(eng, period):
            for b in range(-2, 2):
                period(b, b % 2, b // 2)
            with eng.Fori(1, B // 2 - 2) as i:
                for par in range(2):
                    period(i * 2 + par, par, i)
            for b in range(B - 4, B + 1):
                period(b, b % 2, b // 2)

        def pieces(c):
            if c < 6:
                return [(1, 9 + 2 * c), (1, 10 + 2 * c)]
            return [(2, n) for n in {6: (0,), 7: (1,), 8: (2, 3), 9: (4,), 10: (5, 6), 11: (7, 8)}[c]]

        def bank_of(n):
            return bank[(n + 1 if 1 <= n < 9 else n + 1 if n >= 9 else 0) % 2]

        def has(b, ahead):
            return not isinstance(b, int) or 0 <= b + ahead < B

        block = stack.enter_context(nc.Block())

        @block.sync
        def _(sp):
            for s_ in primed:
                sp.sem_inc(s_, PRIME)
            for t, src in ((w_sb["wq"], wq), (w_sb["wk"], wk), (w_sb["wv"], wv), (w_sb["xWq"], xWq), (w_sb["xWo"], xWo)):
                sp.dma_start(t[:], src).then_inc(weights, 16)
            sp.dma_start(bq_col[:], xbq.rearrange("(p a) -> p a", a=1)).then_inc(weights, 16)
            sp.dma_start(WkA[0:DC, :], xWk).then_inc(weights, 16)
            sp.dma_start(WkA[DC:DC + 1, :], xbk.rearrange("(a p) -> a p", a=1)).then_inc(weights, 16)
            sp.dma_start(WvA[0:DC, :], xWv).then_inc(weights, 16)
            sp.dma_start(WvA[DC:DC + 1, :], xbv.rearrange("(a p) -> a p", a=1)).then_inc(weights, 16)
            sp.dma_start(bo_row[:], xbo.rearrange("(a p) -> a p", a=1)).then_inc(weights, 16)
            sp.dma_start(Wr_sb[:], Wr).then_inc(weights, 16)
            xv = x.rearrange("(n t b) s d -> n (b s) t d", t=QT, b=2)
            with sp.Fori(0, NQ) as i:
                sp.wait_ge(S1["y"], i + PRIME)
                sp.dma_start(xq[:], xv[bass.ds(i, 1), :, :, :].rearrange("a p t d -> (a p) t d")).then_inc(S1["x"], 16)
            cv = ctx_in.rearrange("b (p c) d -> b p c d", c=NC)
            sp.wait_ge(F["ready"], 1 + PRIME)
            for q, part in enumerate((Q_hi, Q_lo, Q_hi)):
                for g in range(HG):
                    sp.dma_start(Qs_all[32 * q:32 * q + 32, g, :], part[32 * g:32 * g + 32, :]).then_inc(D_["q"], 16)
            sp.wait_ge(D_["q"], 16 * 3 * HG)
            sp.sem_inc(F["ready"], 1)

            def load_context(b):
                sp.dma_start(C2, cv[bass.ds(b, 1), :, :, :].rearrange("a p c d -> (a p) c d")).then_inc(D_["c"], 16)
            load_context(0)

            def period(b, par, half):
                if has(b, 1):
                    sp.wait_ge(F["klo"], (b + 2) * NB + PRIME)
                    if not isinstance(b, int) or b >= 1:
                        sp.wait_ge(F["bp"], b * NC + PRIME)
                    for q, part in ((2, K_lo), (0, K_hi[:, 1 - par]), (1, K_hi[:, 1 - par])):
                        for g in range(HG):
                            sp.dma_start(K_st[32 * q:32 * q + 32, 1 - par, g, :].bitcast(F32), part[32 * g:32 * g + 32, :].bitcast(F32))\
                              .then_inc(D_[f"{'klo' if q == 2 else 'khi'}{1 - par}"], 16)
                if has(b, 3):
                    sp.wait_ge(F["cTp"], (b + 3) * NB + PRIME)
                    load_context(b + 3)
                if has(b, 1):
                    sp.wait_ge(F["mr"], b + 2 + PRIME)
                    last_row = Q_st[DC:DC + 1, 1 - par].rearrange("a g h q -> a (g h q)")
                    for j in range(RG):
                        sp.dma_start(last_row[:, 128 * j:128 * j + 128].bitcast(F32), max_row[j:j + 1, :].bitcast(F32)).then_inc(D_["mrow"], 16)
            periods(sp, period)
            sp.wait_ge(F["flag"], 1 + PRIME)
            clamped = sp.value_load(flag_int[0:1, 0:1], min_val=0, max_val=1)
            with sp.If(clamped > 0), sp.Fori(0, B) as i:
                sp.wait_ge(S2["cTp"], i + PRIME)
                sp.dma_start(C[:], cv[bass.ds(i, 1), :, :, :].rearrange("a p c d -> (a p) c d")).then_inc(S2["c"], 16)
            sp.wait_ge(S3["osq"], 1 + PRIME)
            w1v = W1.rearrange("(n e) d f -> n d e f", e=2)
            w2v = W2.rearrange("(n e) (c p) d -> n p e c d", e=2, p=128)
            with sp.Fori(0, NE // 2) as i:
                sp.wait_ge(S4["dn"], i * (2 * NT) + PRIME)
                sp.dma_start(w1[:], w1v[bass.ds(i, 1), :, :, :].rearrange("a p e f -> (a p) e f")).then_inc(S4["w"], 16)
                for e in range(2):
                    sp.dma_start(w2[:, e], w2v[bass.ds(i, 1), :, e].rearrange("a p c d -> (a p) c d")).then_inc(S4["w"], 16)
            ov = out.rearrange("(n t b) s d -> n (b s) t d", t=QT, b=2)
            for i in range(NQ):
                sp.wait_ge(S4["xn"], i + 1 + PRIME)
                sp.dma_start(ov[i], x2_all[:, QT * i:QT * i + QT, :]).then_inc(S4["out"], 16)
            sp.wait_ge(S4["out"], 16 * NQ)

        @block.gpsimd
        def _(pool):
            g = nc.gpsimd
            n = [0]

            def step(ins):
                n[0] += 1
                ins.then_inc(pool_step, 1)
                pool.wait_ge(pool_step, n[0])

            def keep(t, pattern, base, mult, op=ALU.is_ge, fill=0.0):
                step(g.affine_select(out=t, in_=t, pattern=pattern, compare_op=op, fill=fill, base=base,
                                     channel_multiplier=mult))

            for t, v in ((ident, 0.0), (other_batch, 0.0), (causal, 1.0), (head_rows, 1.0), (pair_rows, 1.0), (fold_q, 0.0),
                         (expert_rows, 1.0), (before_rows, 1.0), (ones, 1.0), (minus_half, -0.5), (perm, 0.0), (zrow, 0.0),
                         (sum_rows, 0.0), (sum_row, 0.0), (thr, 1.0), (stepv, 0.5)):
                step(g.memset(t[:], v))
            keep(ident[:], [[-1, 128]], 0, 1, ALU.not_equal, 1.0)
            keep(other_batch[:, 0:S], [[0, S]], S - 1, -1, fill=NEG)
            keep(other_batch[:, S:TT], [[0, S]], -S, 1, fill=NEG)
            keep(causal[:], [[-1, TT]], 0, 1)
            keep(causal[:, 0:S], [[0, S]], S - 1, -1)
            keep(head_rows[:], [[-DH, H]], 0, 1)
            keep(head_rows[:], [[DH, H]], DH - 1, -1)
            keep(pair_rows[:, 0:1], [[0, 1]], S - 1, -1)
            keep(pair_rows[:, 1:2], [[0, 1]], -S, 1)
            keep(fold_q[:], [[-1, S]], 0, 1, ALU.not_equal, 1.0)
            keep(fold_q[:], [[-1, S]], -S, 1, ALU.not_equal, 1.0)
            ev = expert_rows[:].rearrange("p (e s) -> p e s", s=NT)
            keep(ev, [[-NT, NE], [0, NT]], 0, 1)
            keep(ev, [[NT, NE], [0, NT]], NT - 1, -1)
            bv = before_rows[:].rearrange("p (e s) -> p e s", s=NT)
            keep(bv, [[-NT, NE], [0, NT]], 0, 1)
            keep(bv, [[NT, NE], [1, NT]], -1, -1)
            for e in range(NE):
                step(g.memset(index_prio[:, e:e + 1], float(NE - e)))
            for s in range(SLOTS - 1):
                step(g.tensor_copy(perm[:, s, :].rearrange("p (g c) -> p g c", c=32)[:, :, 1 + DH * s:1 + DH * s + DH],
                                   ident[:, 0:96].rearrange("p (g c) -> p g c", c=24)[:, :, DH * s:DH * s + DH]))
            step(g.tensor_copy(perm[:, 3, :].rearrange("p (g c) -> p g c", c=32)[:, :, 1:V1],
                               ident[:, 96:128].rearrange("p (g c) -> p g c", c=DH)))
            keep(sum_rows[:].rearrange("p (g c) -> p g c", c=32), [[-32, 4], [0, 32]], -SUM, 1, ALU.not_equal, 1.0)
            for g4 in range(4):
                keep(sum_row[:], [[0, 1]], -SUM - 32 * g4, 1, ALU.not_equal, 1.0)
            for a3 in range(3):
                step(g.tensor_copy(four_heads[32 * a3:32 * a3 + 32, :], head_rows[32 * a3:32 * a3 + 32, 4 * a3:4 * a3 + 4]))
            g.memset(K_st[DC:DC + 1].rearrange("p a g k -> p (a g k)").bitcast(F32), 1.0).then_inc(consts, 1)
            with pool.Fori(0, NQ) as i:
                pool.wait_ge(S1["ve"], i + 1 + PRIME)
                g.tensor_tensor(rstd[:], ve[:], minus_half[0:TT], ALU.pow).then_inc(S1["rstd"], 1)
                pool.wait_ge(S1["x1"], i + 1 + PRIME)
            pool.wait_ge(F["ready"], 2 + PRIME)
            for par in range(2):
                step(g.memset(V2[par][:, :, 0:4 * V3].rearrange("p c (m r) -> p c m r", r=V3)[:, :, :, SUM], 1.0))
                step(g.memset(V2[par][:, :, 4 * V3:VC].rearrange("p c (m r) -> p c m r", r=V1)[:, :, :, SUM], 1.0))
            step(g.memset(ctxT2[DC:DC + 1], 1.0))
            pool.sem_inc(F["ready"], 1)

            def period(b, par, half):
                if has(b, 2):
                    if not isinstance(b, int) or b >= 0:
                        pool.wait_ge(F["ap"], (b + 1) * AP_ + PRIME)
                    g.tensor_tensor(Q_bd[:, par], Qt_all[:, bass.ds((b + 2) * S, S)].unsqueeze(1).to_broadcast([128, H, S]),
                                    head_rows[:].unsqueeze(2).to_broadcast([128, H, S]), ALU.mult).then_inc(F["qa"], 1)
                if has(b, 1):
                    if not isinstance(b, int) or b >= 1:
                        pool.wait_ge(F["bp"], b * NC + PRIME)
                    g.tensor_tensor(Q_st[0:DC, 1 - par], Qs_all[:, :, bass.ds((b + 1) * S, S)].unsqueeze(2).to_broadcast([DC, HG, 4, S]),
                                    four_heads[:].unsqueeze(1).unsqueeze(3).to_broadcast([DC, HG, 4, S]), ALU.mult).then_inc(F["qs"], 1)
                if has(b, 2):
                    for n in range(NB):
                        pool.wait_ge(F["khi"], b * NB + (2 * NB + n + 1) + PRIME)
                        low = K_lo[:, n * KB:n * KB + KB]
                        g.tensor_tensor(low.bitcast(F32R), low, K_hi[:, par, n * KB:n * KB + KB].bitcast(F32), ALU.subtract).then_inc(F["klo"], 1)
            periods(pool, period)
            pool.wait_ge(F["flag"], 1 + PRIME)
            with pool.Fori(0, NQ) as i:
                pool.wait_ge(S3["ve"], i + 1 + PRIME)
                g.tensor_tensor(rstd[:], ve[:], minus_half[0:TT], ALU.pow).then_inc(S3["rstd"], 1)
            with pool.Fori(0, NQ) as i:
                pool.wait_ge(S4["ve"], i + 1 + PRIME)
                g.tensor_tensor(rstd[:], ve[:], minus_half[0:TT], ALU.pow).then_inc(S4["rstd"], 1)

        @block.scalar
        def _(act):
            a = nc.scalar
            with act.Fori(0, NQ) as i:
                act.wait_ge(S1["xTp"], i + 1 + PRIME)
                a.copy(xT[:], bank[0][:, 0:QC]).then_inc(S1["xT"], 1)
                act.wait_ge(S1["up"], i + 1 + PRIME)
                a.copy(u_sb[:], bank[1][:, 0:QC]).then_inc(S1["u"], 1)
                act.wait_ge(S1["vp"], i + 1 + PRIME)
                a.copy(v_sb[:], bank[2][0:TT, :].rearrange("p (t d) -> p t d", t=QT)).then_inc(S1["v"], 1)
                act.wait_ge(S1["max"], i + 1 + PRIME)
                a.activation(e_sb[:], s_sb[:], ACT.Exp).then_inc(S1["e"], 1)
                act.wait_ge(S1["aTp"], i + 1 + PRIME)
                a.copy(aT[:], bank[4][0:TT, 0:QC].rearrange("p (t k) -> p t k", t=QT)).then_inc(S1["aT"], 1)
                act.wait_ge(S1["xn"], i + 1 + PRIME)
                a.copy(x1_all[:, bass.ts(i, QT), :], xn[:]).then_inc(S1["x1"], 1)
                act.wait_ge(S1["xnTp"], i + 1 + PRIME)
                a.copy(xT[:], bank[6][:, 0:QC]).then_inc(S1["xnT"], 1)
            act.wait_ge(F["ready"], 3 + PRIME)

            def period(b, par, half):
                for c in range(NC):
                    if c == 1 and has(b, -1):
                        act.wait_ge(F["pv"], b * NC + PRIME)
                        if not isinstance(b, int) or b >= 2:
                            act.wait_ge(F["os"], b - 1 + PRIME)
                        a.copy(O_sb, bank[6][:, 0:SLOTS * S]).then_inc(F["o"], 1)
                    if has(b, 0):
                        act.wait_ge(F["bp"], b * NC + (c + 1) + PRIME)
                        if not (isinstance(b, int) and b == 0 and c < 2):
                            act.wait_ge(F["pv"], b * NC + (c - 1) + PRIME)
                        a.activation(P2[c % 2].rearrange("p (n k) -> p n k", n=2), psum[0:CK, 2 + 2 * (c % 2):4 + 2 * (c % 2), 0:HQ // 2], ACT.Exp)\
                         .then_inc(F["e"], 1)
                    if c < 3 and has(b, 2):
                        act.wait_ge(F["cTp"], b * NB + (2 * NB + c + 1) + PRIME)
                        if not isinstance(b, int) or b >= 0:
                            act.wait_ge(F["vp"], (b + 1) * NB + PRIME)
                        a.copy(ctxT2[0:DC, par, c * KB:c * KB + KB], bank[7][0:DC, 0:KB]).then_inc(F["cT"], 1)
                    if 3 <= c < 6 and has(b, 2):
                        n = c - 3
                        act.wait_ge(F["kp"], b * NB + (2 * NB + n + 1) + PRIME)
                        if not isinstance(b, int) or b >= 0:
                            act.wait_ge(F["ap"], (b + 1) * AP_ + PRIME)
                            act.wait_ge(D_[f"khi{par}"], (half + 1) * (16 * 2 * HG))
                        if not isinstance(b, int) or b >= -1:
                            act.wait_ge(D_[f"klo{1 - par}"], (half + (par + 1)) * (16 * HG))
                        a.copy(K_lo[:, n * KB:n * KB + KB], bank[7][:, 0:KB]).then_inc(F["k"], 1)
                        act.wait_ge(F["k"], b * NB + (2 * NB + n + 1) + PRIME)
                        a.copy(K_hi[:, par, n * KB:n * KB + KB], K_lo[:, n * KB:n * KB + KB]).then_inc(F["khi"], 1)
                    if c in V_SLOTS and has(b, 1):
                        n = V_SLOTS.index(c)
                        act.wait_ge(F["vp"], b * NB + (NB + n + 1) + PRIME)
                        if not isinstance(b, int) or b >= 1:
                            act.wait_ge(F["pv"], b * NC + PRIME)
                        src = bank[7][0:CK, :].rearrange("p (c k) -> p c k", c=4)
                        three = V2[1 - par][:, 4 * n:4 * n + 4, 0:4 * V3].rearrange("p c (m r) -> p c m r", r=V3)
                        one = V2[1 - par][:, 4 * n:4 * n + 4, 4 * V3:VC].rearrange("p c (m r) -> p c m r", r=V1)
                        a.copy(three[:, :, :, 1:V3], src[:, :, 0:96].rearrange("p c (m r) -> p c m r", r=24))
                        a.copy(one[:, :, :, 1:V1], src[:, :, 96:128].rearrange("p c (m r) -> p c m r", r=DH)).then_inc(F["v"], 1)
            periods(act, period)
            act.wait_ge(F["flag"], 1 + PRIME)
            clamped = act.value_load(flag_int[0:1, 0:1], min_val=0, max_val=1)
            with act.If(clamped > 0), act.Fori(0, B) as i:
                for n in range(NB):
                    act.wait_ge(S2["cTp"], i + 1 + PRIME)
                    a.copy(ctxT[0:DC, n * KB:n * KB + KB], bank[n][0:DC, 0:KB]).then_inc(S2["cT"], 1)
                for n in range(NB):
                    act.wait_ge(S2["kp"], i + 1 + PRIME)
                    a.copy(KT[:, n * KB:n * KB + KB], bank[n][:, 0:KB]).then_inc(S2["k"], 1)
                for n in range(NB):
                    act.wait_ge(S2["vp"], i + 1 + PRIME)
                    a.copy(V[:, 4 * n:4 * n + 4, :], bank[3 + n][0:CK, :].rearrange("p (c d) -> p c d", c=4)).then_inc(S2["v"], 1)
                for j in range(G2):
                    act.wait_ge(S2["m"], i * G2 + j + 1 + PRIME)
                    act.wait_ge(S2["pTp"], i * G2 + j + PRIME)
                    a.activation(P[:], Sc[:], ACT.Exp, bias=negmax[:], accum_out=rowsum[:]).then_inc(S2["e"], 1)
                    for n in range(NB):
                        act.wait_ge(S2["pTp"], i * G2 + j + 1 + PRIME)
                        a.copy(PT[:, 4 * n:4 * n + 4, :], bank[3 + n][0:CK, 0:4 * TT].rearrange("p (c q) -> p c q", c=4)).then_inc(S2["pT"], 1)
                act.wait_ge(S2["otp"], i + 1 + PRIME)
                a.copy(OT[:], bank[7][:, 0:2 * S].rearrange("p (a q) -> p a q", a=2)).then_inc(S2["ot"], 1)
            with act.Fori(0, NQ) as i:
                act.wait_ge(S3["xnTp"], i + 1 + PRIME)
                a.copy(x2T[:, bass.ts(i, QC)], bank[6][:, 0:QC]).then_inc(S3["xnT"], 1)
            act.wait_ge(S4["pr"], 1 + PRIME)
            a.activation(pw[:], pr[:], ACT.Exp).then_inc(S4["e"], 1)
            with act.Fori(0, NE // 2) as i:
                for e in range(2):
                    for f in range(FC):
                        for q in range(NQ):
                            k = (e * FC + f) * NQ + q
                            act.wait_ge(S4["up"], i * (2 * FC * NQ) + k + 1 + PRIME)
                            a.activation(hT[:, f, q * QC:q * QC + QC], bank[q][:, 0:QC], ACT.Relu).then_inc(S4["h"], 1)

        @block.vector
        def _(dve):
            v = nc.vector
            done = [0]

            def tie(base, sem_=dve_step):
                def step(ins):
                    done[0] += 1
                    ins.then_inc(sem_, 1)
                    dve.wait_ge(sem_, base + done[0])
                return step

            def norm(step, S_, i, src, resid, dst, first_wait=None):
                ins = v.tensor_tensor(y[:], src, resid, ALU.add)
                ins.then_inc(S_["y"], 1)
                dve.wait_ge(S_["y"], i + 1 + PRIME)
                for t in range(QT):
                    last = v.bn_stats(stats[:, t, :], y[:, t, :])
                step(last)
                v.memset(pad[:], 0.0)
                for t in range(QT):
                    last = v.bn_aggr(mv[:, t, :], stats[:, t, :])
                step(last)
                v.tensor_scalar(ve[:], mv[:, :, 1], EPS, None, ALU.add).then_inc(S_["ve"], 1)
                dve.wait_ge(S_["rstd"], i + 1 + PRIME)
                for t in range(QT):
                    last = v.tensor_scalar(dst(t), y[:, t, :], mv[:, t, 0:1], rstd[:, t:t + 1], ALU.subtract, ALU.mult)
                last.then_inc(S_["xn"], 1)

            dve.wait_ge(w_ps, 1)
            v.tensor_copy(qk[:], bank[0][:, 0:128]).then_inc(w_ev, 1)
            v.tensor_copy(wvT[:], bank[1][:, 0:128]).then_inc(w_ev, 1)
            v.tensor_copy(WoP[:], bank[2][:].rearrange("p (s c) -> p s c", s=SLOTS)).then_inc(w_ev, 1)
            dve.wait_ge(weights, 16 * 12)
            step0 = tie(0)
            step0(v.tensor_scalar(bq_col[:], bq_col[:], DH ** -0.5, None, ALU.mult))

            K1 = 2 + 3 + 2
            base0 = done[0]
            with dve.Fori(0, NQ) as i:
                done[0] = base0
                step = tie(i * K1)
                dve.wait_ge(S1["sp"], i + 1 + PRIME)
                step(v.scalar_tensor_tensor(s_sb[:], bank[3][0:TT, 0:QC].rearrange("p (t q) -> p t q", t=QT), float(D) ** -0.5,
                                            other_batch[:].unsqueeze(1).to_broadcast([TT, QT, TT]), ALU.mult, ALU.add))
                step(v.reduce_max(nm[:], s_sb[:], AX.X))
                v.tensor_tensor(s_sb[:], s_sb[:], nm[:].unsqueeze(2).to_broadcast([TT, QT, TT]), ALU.subtract).then_inc(S1["max"], 1)
                dve.wait_ge(S1["e"], i + 1 + PRIME)
                step(v.reduce_sum(rs[:], e_sb[:], AX.X))
                step(v.reciprocal(ri[:], rs[:]))
                step(v.tensor_tensor(e_sb[:], e_sb[:], causal[:].unsqueeze(1).to_broadcast([TT, QT, TT]), ALU.mult))
                v.tensor_tensor(s_sb[:], e_sb[:], ri[:].unsqueeze(2).to_broadcast([TT, QT, TT]), ALU.mult).then_inc(S1["a"], 1)
                dve.wait_ge(S1["op"], i + 1 + PRIME)
                norm(step, S1, i, bank[5][0:TT, :].rearrange("p (t d) -> p t d", t=QT), xq[:], lambda t: xn[:, t, :])
                dve.wait_ge(S1["qp"], i + 1 + PRIME)
                v.tensor_scalar(Qt_all[:, bass.ts(i, QC)], bank[7][:, 0:QC], DH ** -0.5, bq_col[:], ALU.mult, ALU.add).then_inc(S1["q"], 1)
                assert done[0] - base0 == K1, done[0] - base0
            base1 = done[0] - base0
            done[0] = base0 + NQ * K1

            step = tie(0)
            dve.wait_ge(S1["q"], NQ + PRIME)
            step(v.tensor_copy(Q_hi.bitcast(F32R), Qt_all[:]))
            step(v.tensor_tensor(Q_lo.bitcast(F32R), Qt_all[:], Q_hi, ALU.subtract))
            dve.sem_inc(F["ready"], 1)
            dve.wait_ge(F["ready"], 3 + PRIME)
            step(v.memset(m_high, 0.0))
            step(v.memset(m_low, 0.0))
            step(v.memset(bank[6], 0.0))
            step(v.memset(chk_sum, 0.0))

            dve.sem_inc(F["ready"], 1)

            def period(b, par, half):
                for c in range(NC):
                    if c == 6 and has(b, 1):
                        dve.wait_ge(F["am"], (b + 2) * AP_ + PRIME)
                        if not isinstance(b, int) or b >= 0:
                            dve.wait_ge(F["mTp"], b + 1 + PRIME)
                            dve.wait_ge(F["ab"], (b + 1) * 2 + PRIME)
                        v.reduce_max(m2x, mx, AX.X).then_inc(F["mx"], 1)
                        dve.wait_ge(F["mx"], b + 2 + PRIME)
                        v.tensor_tensor(m_high, m_high, m2x, ALU.max).then_inc(F["ab"], 1)
                        v.tensor_tensor(m_low, m_low, m2x, ALU.min).then_inc(F["ab"], 1)
                    for ahead, n in pieces(c):
                        if not has(b, ahead):
                            continue
                        dve.wait_ge(F["ap"], b * AP_ + (ahead * AP_ + n + 1) + PRIME)
                        if n == 0 and (not isinstance(b, int) or b >= -1):
                            dve.wait_ge(F["mx"], b + 2 + PRIME)
                        v.reduce_max(mx[:, n // NB, n % NB:n % NB + 1], bank_of(n)[:, 0:KB], AX.X).then_inc(F["am"], 1)
                    if c == 7 and has(b, 1):
                        dve.wait_ge(F["mTp"], b + 2 + PRIME)
                        if not isinstance(b, int) or b >= 0:
                            dve.wait_ge(D_["mrow"], (b + 1) * (16 * RG))
                        v.tensor_scalar(max_row[:], bank[1][0:RG, 0:128], -1.0, None, ALU.mult).then_inc(F["mr"], 1)
                    if c in (6, 7) and has(b, -1):
                        if c == 6:
                            dve.wait_ge(F["rp"], b + PRIME)
                            if not isinstance(b, int) or b >= 2:
                                dve.wait_ge(F["os"], b - 1 + PRIME)
                        part = slice((c - 6) * (SLOTS * S // 2), (c - 5) * (SLOTS * S // 2))
                        v.reciprocal(R_sb[:, part], bank[7][:, part]).then_inc(F["r"], 1)
                    if c == 7 and has(b, -1):
                        dve.wait_ge(F["r"], 2 * b + PRIME)
                        if not isinstance(b, int) or b >= 2:
                            dve.wait_ge(F["chk"], b - 1 + PRIME)
                        v.scalar_tensor_tensor(OS_all[:, :, bass.ds((b - 1) * S, S)], O_sb.rearrange("p (s q) -> p s q", s=SLOTS), 1.0,
                                               R_sb.rearrange("p (s q) -> p s q", s=SLOTS), ALU.mult, ALU.mult, accum_out=chk).then_inc(F["os"], 1)
                        dve.wait_ge(F["os"], b + PRIME)
                        v.tensor_tensor(chk_sum, chk_sum, chk, ALU.add).then_inc(F["chk"], 1)
            periods(dve, period)
            dve.wait_ge(F["chk"], B + PRIME)
            dve.wait_ge(F["ab"], 2 * B + PRIME)
            step(v.tensor_scalar(m_low, m_low, -1.0, None, ALU.mult))
            step(v.tensor_tensor(m_high, m_high, m_low, ALU.max))
            step(v.reduce_max(bad[:, 0:1], m_high, AX.X))
            step(v.tensor_scalar(bad[:, 0:1], bad[:, 0:1], PLAIN, None, ALU.is_ge))
            step(v.tensor_scalar(bad[:, 1:2], chk_sum, 0.0, None, ALU.is_ge))
            step(v.tensor_scalar(bad[:, 1:2], bad[:, 1:2], -1.0, -1.0, ALU.add, ALU.mult))
            step(v.tensor_tensor(bad[:, 1:2], bad[:, 1:2], sum_row[:], ALU.mult))
            v.tensor_tensor(bad[:, 0:1], bad[:, 0:1], bad[:, 1:2], ALU.add).then_inc(F["bad"], 1)
            dve.wait_ge(F["sum"], 1 + PRIME)
            v.tensor_scalar(flag_int[:], bank[0][0:1, 0:1], 0.5, None, ALU.is_ge).then_inc(F["flag"], 1)
            dve.wait_ge(F["flag"], 1 + PRIME)
            clamped = dve.value_load(flag_int[0:1, 0:1], min_val=0, max_val=1)
            with dve.If(clamped > 0):
                outer, done[0] = done[0], 0
                step = tie(0, clamp_step)
                step(v.memset(ctxT[DC:DC + 1, :], 1.0))
                step(v.memset(numbers, float(NK)))

                K2 = G2 * 7
                base0 = done[0]
                with dve.Fori(0, B) as i:
                    done[0] = base0
                    step = tie(i * K2, clamp_step)
                    dve.wait_ge(S2["sp"], i * G2 + PRIME)
                    dve.wait_ge(S1["q"], NQ + PRIME)
                    v.tensor_tensor(Qbd[:], Qt_all[:, bass.ts(i, S)].unsqueeze(1).to_broadcast([128, H, S]),
                                    head_rows[:].unsqueeze(2).to_broadcast([128, H, S]), ALU.mult).then_inc(S2["qbd"], 1)
                    for j in range(G2):
                        n = i * G2 + j
                        dve.wait_ge(S2["sp"], n + 1 + PRIME)
                        dve.wait_ge(S2["e"], n + PRIME)
                        src = psum[0:TT, 0:NB, 0:KB]
                        step(v.tensor_scalar(view3(Sc, KB), src, 0.0, 0.0, ALU.is_ge, ALU.add, accum_out=c1[:]))
                        step(v.tensor_scalar(view3(Sc, KB), src, 0.0, 0.0, ALU.is_lt, ALU.add, accum_out=c2[:]))
                        step(v.tensor_scalar(view3(Sc, KB), src, CLAMP, -CLAMP, ALU.min, ALU.max, accum_out=rowmax[:]))
                        step(v.tensor_tensor(c1[:], c1[:], c2[:], ALU.add))
                        step(v.tensor_tensor(numbers[:], numbers[:], c1[:], ALU.min))
                        step(v.tensor_scalar(Sc[:], Sc[:], -CLAMP, None, ALU.max))
                        v.tensor_scalar(negmax[:], rowmax[:], -1.0, None, ALU.mult).then_inc(S2["m"], 1)
                        dve.wait_ge(S2["e"], n + 1 + PRIME)
                        step(v.reciprocal(rinv[:], rowsum[:]))
                        dve.wait_ge(S2["op"], n + 1 + PRIME)
                        v.scalar_tensor_tensor(Om[:, 16 * j:16 * j + 16].rearrange("p (a d) -> p a d", a=2),
                                               bank[6][0:TT, 0:16].rearrange("p (a d) -> p a d", a=2), rinv[:],
                                               pair_rows[:].unsqueeze(2).to_broadcast([TT, 2, DH]), ALU.mult, ALU.mult).then_inc(S2["om"], 1)
                    dve.wait_ge(S2["osp"], i + 1 + PRIME)
                    v.tensor_scalar(OS_all[:, :, bass.ts(i, S)], bank[6][:, 0:SLOTS * S].rearrange("p (s q) -> p s q", s=SLOTS), 1.0, None, ALU.mult).then_inc(S2["os"], 1)
                    v.tensor_scalar(OM_all[:, :, bass.ds(i, 1)], bank[6][:, SLOTS * S:2 * SLOTS * S].rearrange("p (s q) -> p s q", s=SLOTS)[:, :, 0:1], 1.0 / NK,
                                    None, ALU.mult).then_inc(S2["os"], 1)
                    assert done[0] - base0 == K2, done[0] - base0
                done[0] = base0 + B * K2
                step = tie(0, clamp_step)
                v.tensor_scalar(nan_mask[:], numbers[:], float(NK), None, ALU.is_lt).then_inc(S2["nanrow"], 1)
                dve.wait_ge(S2["nanall"], 1 + PRIME)
                step(v.tensor_scalar(nan_col[:], bank[0][:, 0:1], 0.5, None, ALU.is_ge))
                step(v.tensor_copy(nan_int[:], nan_col[:]))
                dve.wait_ge(S2["os"], 2 * B + PRIME)
                v.copy_predicated(OS_all[:].rearrange("p s (b q) -> p (s b) q", q=S), nan_int.unsqueeze(2).to_broadcast([128, SLOTS * B, S]),
                                  OM_all[:].rearrange("p s b -> p (s b)").unsqueeze(2).to_broadcast([128, SLOTS * B, S])).then_inc(S2["fix"], 1)
                dve.wait_ge(S2["fix"], 1 + PRIME)
                done[0] = outer

            K3 = 2
            base0 = done[0]
            with dve.Fori(0, NQ) as i:
                done[0] = base0
                step = tie(i * K3)
                dve.wait_ge(S3["op"], i + PRIME)
                v.tensor_scalar(OSq[:], OS_all[:, :, bass.ts(i, QC)], 1.0, None, ALU.mult).then_inc(S3["osq"], 1)
                dve.wait_ge(S3["op"], i + 1 + PRIME)
                dve.wait_ge(S3["xnTp"], i + PRIME)
                norm(step, S3, i, bank[5][0:TT, :].rearrange("p (t d) -> p t d", t=QT), x1_all[:, bass.ts(i, QT), :], lambda t: xn[:, t, :])
                dve.wait_ge(S3["xn"], i + 1 + PRIME)
                v.tensor_scalar(x2_all[:, bass.ts(i, QT), :], xn[:], 1.0, None, ALU.mult).then_inc(S3["x2"], 1)
                assert done[0] - base0 == K3, done[0] - base0
            done[0] = base0 + NQ * K3
            step = tie(0)

            def wide(t):
                return t[:].unsqueeze(2).to_broadcast([TT, NT, NE])
            dve.wait_ge(S4["lg"], 1 + PRIME)
            lg = bank[7][0:TT, 0:NT * NE].rearrange("p (t e) -> p t e", e=NE)
            step(v.reduce_max(m1[:], lg, AX.X))
            v.tensor_tensor(pr[:], lg, wide(m1), ALU.subtract).then_inc(S4["pr"], 1)
            dve.wait_ge(S4["e"], 1 + PRIME)
            step(v.reduce_sum(m1[:], pw[:], AX.X))
            step(v.reciprocal(m2[:], m1[:]))
            step(v.tensor_tensor(pr[:], pw[:], wide(m2), ALU.mult))
            step(v.tensor_copy(pw[:], pr[:]))
            for k in range(TOPK):
                step(v.reduce_max(m1[:], pw[:], AX.X))
                step(v.tensor_tensor(eq[:], pw[:], wide(m1), ALU.is_equal))
                step(v.tensor_tensor(eq[:], eq[:], index_prio[:].unsqueeze(1).to_broadcast([TT, NT, NE]), ALU.mult))
                step(v.reduce_max(m2[:], eq[:], AX.X))
                step(v.tensor_tensor(hot[:], eq[:], wide(m2), ALU.is_equal))
                if k == 0:
                    step(v.tensor_copy(mask[:], hot[:]))
                    step(v.scalar_tensor_tensor(flat(pw), flat(hot), -2.0, flat(pw), ALU.mult, ALU.add))
                else:
                    step(v.tensor_tensor(mask[:], mask[:], hot[:], ALU.add))
            step(v.tensor_scalar(pw[:], pr[:], 1.0, None, ALU.add))
            step(v.tensor_tensor(pw[:], pw[:], mask[:], ALU.mult))
            step(v.tensor_tensor(pr[:], pr[:], mask[:], ALU.mult))
            step(v.scalar_tensor_tensor(flat(pr), flat(mask), 1.0, flat(pr), ALU.subtract, ALU.add))
            v.tensor_copy(gsel[:], pr[:].rearrange("p t e -> p e t")).then_inc(S4["g"], 1)
            dve.wait_ge(S4["gTp"], 1 + PRIME)
            step(v.tensor_copy(G[:], bank[0][:, 0:TT]))

            rounds = [0]

            def count(op, where, column):
                v.tensor_scalar(gscr[:], G[:], where, 0.0, op, ALU.add, accum_out=cnt[:, column:column + 1]).then_inc(S4["cnt"], 1)
                rounds[0] += 1
                dve.wait_ge(S4["tot"], rounds[0] + PRIME)
                return bank[1][:, 0:1]

            for s in (64, 32, 16, 8, 4, 2, 1):
                step(v.tensor_scalar(cand[:], thr[:], 2.0 ** -(s - 1), None, ALU.mult))
                tot = count(ALU.is_ge, cand[:], 0)
                step(v.tensor_scalar(fac[:], tot, float(CAP), 2.0 ** -s, ALU.is_ge, ALU.max))
                step(v.tensor_tensor(thr[:], thr[:], fac[:], ALU.mult))
            step(v.tensor_scalar(stepv[:], thr[:], 0.5, None, ALU.mult))
            for s in range(23):
                step(v.tensor_tensor(cand[:], thr[:], stepv[:], ALU.add))
                tot = count(ALU.is_ge, cand[:], 0)
                step(v.tensor_scalar(fac[:], tot, float(CAP), None, ALU.is_ge))
                step(v.scalar_tensor_tensor(thr[:], fac[:], stepv[:], thr[:], ALU.mult, ALU.add))
                step(v.tensor_scalar(stepv[:], stepv[:], 0.5, None, ALU.mult))
            tot = count(ALU.is_ge, 0.0, 0)
            step(v.tensor_scalar(fac[:], tot, float(CAP), None, ALU.is_ge))
            step(v.tensor_tensor(thr[:], thr[:], fac[:], ALU.mult))
            tot = count(ALU.is_gt, thr[:], 0)
            step(v.tensor_scalar(room[:], tot, -1.0, float(CAP), ALU.mult, ALU.add))
            step(v.tensor_scalar(gtm[:], G[:], thr[:], None, ALU.is_gt))
            step(v.tensor_scalar(eqm[:], G[:], thr[:], None, ALU.is_equal))
            step(v.tensor_tensor_scan(pref[:], eqm[:], zrow[:], 0.0, ALU.add, ALU.add))
            v.tensor_copy(cnt[:, 1:2], pref[:, TT - 1:TT]).then_inc(S4["eqc"], 1)
            dve.wait_ge(S4["eqp"], 1 + PRIME)
            step(v.tensor_tensor(room[:], room[:], bank[1][:, 0:1], ALU.subtract))
            step(v.tensor_scalar(pref[:], pref[:], room[:], None, ALU.is_le))
            step(v.tensor_tensor(eqm[:], eqm[:], pref[:], ALU.mult))
            step(v.tensor_tensor(gtm[:], gtm[:], eqm[:], ALU.add))
            v.tensor_tensor(Gs[:], G[:], gtm[:], ALU.mult).then_inc(S4["gs"], 1)
            dve.wait_ge(S4["gsTp"], 1 + PRIME)
            v.tensor_copy(gate[:], bank[0][0:TT, 0:128].rearrange("p (e t) -> p e t", e=NE)).then_inc(S4["gate"], 1)
            dve.wait_ge(S4["gate"], 1 + PRIME)

            with dve.Fori(0, NE // 2) as i:
                dve.wait_ge(S4["acc"], i * (2 * NT + 1) + PRIME)
                v.tensor_scalar(gate_e[:], gate[:, bass.ts(i, 2), :], 1.0, None, ALU.mult).then_inc(S4["acc"], 1)
                dve.wait_ge(S4["acc"], i * (2 * NT + 1) + 1 + PRIME)
                for e in range(2):
                    for t in range(NT):
                        k = e * NT + t
                        dve.wait_ge(S4["dn"], i * (2 * NT) + k + 1 + PRIME)
                        v.scalar_tensor_tensor(x2_all[:, t, :], bank[4 + k % 4][0:TT, 0:D], gate_e[:, e, t:t + 1], x2_all[:, t, :],
                                               ALU.mult, ALU.add).then_inc(S4["acc"], 1)
                        if e == 0 and t == NT - 1:
                            dve.wait_ge(S4["acc"], i * (2 * NT + 1) + 1 + NT + PRIME)
            dve.wait_ge(S4["acc"], (NE // 2) * (2 * NT + 1) + PRIME)
            for i in range(NQ):
                q = slice(QT * i, QT * i + QT)
                for t in range(QT):
                    step(v.bn_stats(stats[:, t, :], x2_all[:, QT * i + t, :]))
                for t in range(QT):
                    step(v.bn_aggr(mv[:, t, :], stats[:, t, :]))
                v.tensor_scalar(ve[:], mv[:, :, 1], EPS, None, ALU.add).then_inc(S4["ve"], 1)
                dve.wait_ge(S4["rstd"], i + 1 + PRIME)
                for t in range(QT):
                    xt = x2_all[:, QT * i + t, :]
                    ins = v.tensor_scalar(xt, xt, mv[:, t, 0:1], rstd[:, t:t + 1], ALU.subtract, ALU.mult)
                    if t < QT - 1:
                        step(ins)
                ins.then_inc(S4["xn"], 1)

        @block.tensor
        def _(pe):
            t_ = nc.tensor
            mm = t_.matmul
            pe.wait_ge(weights, 16 * 12)
            pe.wait_ge(consts, 1)
            mm(bank[0][:, 0:128], w_sb["wq"][:], w_sb["wk"][:], start=True, stop=True)
            t_.transpose(bank[1][:, 0:128], w_sb["wv"][:], ident[:])
            for s in range(SLOTS):
                last = mm(bank[2][:, 128 * s:128 * s + 128], perm[:, s, :], w_sb["xWo"][:], start=True, stop=True)
            last.then_inc(w_ps, 1)
            pe.wait_ge(w_ev, 3)
            with pe.Fori(0, NQ) as i:
                pe.wait_ge(S1["x"], (i + 1) * 16)
                for t in range(QT):
                    last = t_.transpose(bank[0][:, TT * t:TT * t + TT], xq[:, t, :], ident[0:TT, 0:TT])
                last.then_inc(S1["xTp"], 1)
                pe.wait_ge(S1["xT"], i + 1 + PRIME)
                mm(bank[1][:, 0:QC], qk[:], xT[:], start=True, stop=True).then_inc(S1["up"], 1)
                for t in range(QT):
                    last = mm(bank[2][0:TT, D * t:D * t + D], xT[:, TT * t:TT * t + TT], wvT[:], start=True, stop=True)
                last.then_inc(S1["vp"], 1)
                pe.wait_ge(S1["u"], i + 1 + PRIME)
                for t in range(QT):
                    last = mm(bank[3][0:TT, TT * t:TT * t + TT], xT[:, TT * t:TT * t + TT], u_sb[:, TT * t:TT * t + TT], start=True, stop=True)
                last.then_inc(S1["sp"], 1)
                pe.wait_ge(S1["a"], i + 1 + PRIME)
                for t in range(QT):
                    last = t_.transpose(bank[4][0:TT, TT * t:TT * t + TT], s_sb[:, t, :], ident[0:TT, 0:TT])
                last.then_inc(S1["aTp"], 1)
                pe.wait_ge(S1["v"], i + 1 + PRIME)
                pe.wait_ge(S1["aT"], i + 1 + PRIME)
                for t in range(QT):
                    last = mm(bank[5][0:TT, D * t:D * t + D], aT[:, t, :], v_sb[:, t, :], start=True, stop=True)
                last.then_inc(S1["op"], 1)
                pe.wait_ge(S1["xn"], i + 1 + PRIME)
                for t in range(QT):
                    last = t_.transpose(bank[6][:, TT * t:TT * t + TT], xn[:, t, :], ident[0:TT, 0:TT])
                last.then_inc(S1["xnTp"], 1)
                pe.wait_ge(S1["xnT"], i + 1 + PRIME)
                pe.wait_ge(S1["x1"], i + 1 + PRIME)
                mm(bank[7][:, 0:QC], w_sb["xWq"][:], xT[:], start=True, stop=True).then_inc(S1["qp"], 1)
            pe.wait_ge(S1["q"], NQ + PRIME)


            def period(b, par, half):
                for c in range(NC):
                    if has(b, 0):
                        if c == 0:
                            pe.wait_ge(D_[f"khi{par}"], (half + 1) * (16 * 2 * HG))
                            pe.wait_ge(D_[f"klo{par}"], (half + 1) * (16 * HG))
                            pe.wait_ge(D_["mrow"], (b + 1) * (16 * RG))
                            pe.wait_ge(F["qs"], b + 1 + PRIME)
                        if not (isinstance(b, int) and b == 0 and c < 2):
                            pe.wait_ge(F["e"], b * NC + (c - 1) + PRIME)
                        for g in range(HG):
                            last = mm(bank[2 + 2 * (c % 2) + g // 2][0:CK, 4 * S * (g % 2):4 * S * (g % 2) + 4 * S],
                                      K_st[:, par, g, c * CK:c * CK + CK], Q_st[:, par, g].rearrange("p h q -> p (h q)"), start=True, stop=True)
                        last.then_inc(F["bp"], 1)
                    if c < 3 and has(b, 2):
                        if c == 0:
                            pe.wait_ge(D_["c"], (b + 3) * 16)
                            if not isinstance(b, int) or b >= 0:
                                pe.wait_ge(F["v"], (b + 1) * NB + PRIME)
                            elif b == -1:
                                pe.wait_ge(F["k"], NB + PRIME)
                            else:
                                pe.wait_ge(F["ready"], 4 + PRIME)
                        else:
                            pe.wait_ge(F["cT"], b * NB + (2 * NB + c) + PRIME)
                        for k in range(4):
                            last = t_.transpose(bank[7][0:DC, CK * k:CK * k + CK], C2[:, 4 * c + k, :], ident[0:CK, 0:CK])
                        last.then_inc(F["cTp"], 1)
                    if 3 <= c < 6 and has(b, 2):
                        n = c - 3
                        if n == 0:
                            pe.wait_ge(F["cT"], b * NB + 3 * NB + PRIME)
                        else:
                            pe.wait_ge(F["k"], b * NB + (2 * NB + n) + PRIME)
                        mm(bank[7][:, 0:KB], WkA[:], ctxT2[:, par, n * KB:n * KB + KB], start=True, stop=True).then_inc(F["kp"], 1)
                    if c == 6 and has(b, -1):
                        pe.wait_ge(F["o"], b + PRIME)
                        if has(b, 2):
                            pe.wait_ge(F["k"], b * NB + 3 * NB + PRIME)
                        elif has(b, 0):
                            pe.wait_ge(F["v"], (b + 1) * NB + PRIME)
                        else:
                            pe.wait_ge(F["r"], 2 * (b - 1) + PRIME)
                        mm(bank[7][:, 0:SLOTS * S], sum_rows[:], O_sb, start=True, stop=True).then_inc(F["rp"], 1)
                    if c in V_SLOTS and has(b, 1):
                        n = V_SLOTS.index(c)
                        if n > 0:
                            pe.wait_ge(F["v"], b * NB + (NB + n) + PRIME)
                        elif has(b, -1):
                            pe.wait_ge(F["r"], 2 * b + PRIME)
                        elif has(b, 2):
                            pe.wait_ge(F["k"], b * NB + 3 * NB + PRIME)
                        for k in range(4):
                            q = 4 * n + k
                            last = mm(bank[7][0:CK, 128 * k:128 * k + 128], ctxT2[:, 1 - par, CK * q:CK * q + CK], WvA[:], start=True, stop=True)
                        last.then_inc(F["vp"], 1)
                    for ahead, n in pieces(c):
                        if not has(b, ahead):
                            if n == 1 and has(b, 1):
                                pe.wait_ge(F["mx"], b + 2 + PRIME)
                                mm(bank[1][0:RG, 0:128], m2x, ident[:], start=True, stop=True).then_inc(F["mTp"], 1)
                            continue
                        if n == 0:
                            pe.wait_ge(F["qa"], b + (ahead + 1) + PRIME)
                        if n < NB:
                            pe.wait_ge(F["khi"], b * NB + (ahead * NB + n + 1) + PRIME)
                        if n == 1:
                            if has(b, 1):
                                pe.wait_ge(F["mx"], b + 2 + PRIME)
                                mm(bank[1][0:RG, 0:128], m2x, ident[:], start=True, stop=True).then_inc(F["mTp"], 1)
                            pe.wait_ge(F["am"], b * AP_ + (ahead * AP_ + 1) + PRIME)
                        elif n == 2:
                            if has(b, 1):
                                pe.wait_ge(F["mr"], b + 2 + PRIME)
                        elif not (isinstance(b, int) and b + ahead == 0 and n == 0):
                            pe.wait_ge(F["am"], b * AP_ + (ahead * AP_ + n - 1) + PRIME)
                        p = (par + ahead) % 2
                        mm(bank_of(n)[:, 0:KB], Q_bd[:, p].rearrange("p h q -> p (h q)")[:, 128 * (n // NB):128 * (n // NB) + 128],
                           K_hi[:, p, (n % NB) * KB:(n % NB) * KB + KB], start=True, stop=True).then_inc(F["ap"], 1)
                    ago = -1 if c == 0 else 0
                    if has(b, ago):
                        k = (c - 1) % NC
                        if k == 0:
                            pe.wait_ge(F["v"], (b + 1) * NB + PRIME)
                            if not isinstance(b, int) or b >= 1:
                                pe.wait_ge(F["o"], b + PRIME)
                        pe.wait_ge(F["e"], b * NC + c + PRIME)
                        weights_, values = P2[k % 2], V2[(par + ago) % 2]
                        for m in range(4):
                            mm(bank[6][32 * m:32 * m + V3, 0:3 * S], values[:, k, V3 * m:V3 * m + V3], weights_[:, 3 * S * m:3 * S * m + 3 * S],
                               start=(k == 0), stop=(k == NC - 1), skip_group_check=True)
                        for m in range(4):
                            last = mm(bank[6][32 * m:32 * m + V1, 3 * S:4 * S], values[:, k, 4 * V3 + V1 * m:4 * V3 + V1 * m + V1],
                                      weights_[:, (12 + m) * S:(13 + m) * S], start=False, stop=(k == NC - 1), skip_group_check=True)
                        last.then_inc(F["pv"], 1)
            periods(pe, period)
            pe.wait_ge(F["bad"], 1 + PRIME)
            mm(bank[0][:, 0:1], ones[:], bad[:, 0:1], start=True, stop=True).then_inc(F["sum"], 1)
            pe.wait_ge(F["flag"], 1 + PRIME)
            clamped = pe.value_load(flag_int[0:1, 0:1], min_val=0, max_val=1)
            with pe.If(clamped > 0):
                with pe.Fori(0, B) as i:
                    pe.wait_ge(S2["c"], (i + 1) * 16)
                    pe.wait_ge(S2["qbd"], i + 1 + PRIME)
                    pe.wait_ge(S2["m"], i * G2 + PRIME)
                    for c in range(NC):
                        last = t_.transpose(bank[c // 4][0:DC, CK * (c % 4):CK * (c % 4) + CK], C[:, c, :], ident[0:CK, 0:CK])
                    last.then_inc(S2["cTp"], 1)
                    pe.wait_ge(S2["cT"], i * NB + NB + PRIME)
                    for n in range(NB):
                        last = mm(bank[n][:, 0:KB], WkA[:], ctxT[:, KB * n:KB * n + KB], start=True, stop=True)
                    last.then_inc(S2["kp"], 1)
                    pe.wait_ge(S2["pT"], i * (G2 * NB) + PRIME)
                    for c in range(NC):
                        last = mm(bank[3 + c // 4][0:CK, 128 * (c % 4):128 * (c % 4) + 128], ctxT[:, CK * c:CK * c + CK], WvA[:], start=True, stop=True)
                    last.then_inc(S2["vp"], 1)
                    pe.wait_ge(S2["k"], i * NB + NB + PRIME)
                    pe.wait_ge(S2["v"], i * NB + NB + PRIME)
                    pe.wait_ge(S2["qbd"], i + 1 + PRIME)
                    for j in range(G2):
                        n = i * G2 + j
                        pe.wait_ge(S2["m"], n + PRIME)
                        for c in range(NB):
                            last = mm(bank[c][0:TT, 0:KB], Qbd[:, 2 * j:2 * j + 2, :].rearrange("p h q -> p (h q)"), KT[:, KB * c:KB * c + KB],
                                      start=True, stop=True)
                        last.then_inc(S2["sp"], 1)
                        pe.wait_ge(S2["e"], n + 1 + PRIME)
                        pe.wait_ge(S2["pT"], n * NB + PRIME)
                        for c in range(NC):
                            last = t_.transpose(bank[3 + c // 4][0:CK, TT * (c % 4):TT * (c % 4) + TT], P[:, CK * c:CK * c + CK], ident[0:TT, 0:TT])
                        last.then_inc(S2["pTp"], 1)
                        pe.wait_ge(S2["pT"], n * NB + NB + PRIME)
                        pe.wait_ge(S2["om"], n + PRIME)
                        if j == 0:
                            pe.wait_ge(S2["os"], i * 2 + PRIME)
                        for c in range(NC):
                            last = mm(bank[6][0:TT, 0:16], PT[:, c, :], V[:, c, 16 * j:16 * j + 16], start=(c == 0), stop=(c == NC - 1))
                        last.then_inc(S2["op"], 1)
                    pe.wait_ge(S2["om"], i * G2 + G2 + PRIME)
                    mm(bank[7][:, 0:S], Om[:], fold_q[:], start=True, stop=True)
                    for c in range(NC):
                        last = mm(bank[7][:, S:2 * S], V[:, c, :], ones[0:CK, 0:S], start=(c == 0), stop=(c == NC - 1))
                    last.then_inc(S2["otp"], 1)
                    pe.wait_ge(S2["ot"], i + 1 + PRIME)
                    for a in range(2):
                        for s in range(SLOTS):
                            o = (a * SLOTS + s) * S
                            last = mm(bank[6][:, o:o + S], perm[:, s, :], OT[:, a, :], start=True, stop=True)
                    last.then_inc(S2["osp"], 1)
                pe.wait_ge(S2["nanrow"], 1 + PRIME)
                mm(bank[0][:, 0:1], ones[0:TT, :], nan_mask[:], start=True, stop=True).then_inc(S2["nanall"], 1)

            with pe.Fori(0, NQ) as i:
                pe.wait_ge(S3["osq"], i + 1 + PRIME)
                pe.wait_ge(S3["y"], i + PRIME)
                for t in range(QT):
                    for s in range(SLOTS):
                        mm(bank[5][0:TT, D * t:D * t + D], OSq[:, s, TT * t:TT * t + TT], WoP[:, s, :], start=(s == 0), stop=False)
                    last = mm(bank[5][0:TT, D * t:D * t + D], ones[0:1, 0:TT], bo_row[:], start=False, stop=True)
                last.then_inc(S3["op"], 1)
                pe.wait_ge(S3["xn"], i + 1 + PRIME)
                pe.wait_ge(S3["xnT"], i + PRIME)
                for t in range(QT):
                    last = t_.transpose(bank[6][:, TT * t:TT * t + TT], xn[:, t, :], ident[0:TT, 0:TT])
                last.then_inc(S3["xnTp"], 1)
            pe.wait_ge(S3["xnT"], NQ + PRIME)
            for t in range(NT):
                last = mm(bank[7][0:TT, NE * t:NE * t + NE], x2T[:, TT * t:TT * t + TT], Wr_sb[:], start=True, stop=True)
            last.then_inc(S4["lg"], 1)
            pe.wait_ge(S4["g"], 1 + PRIME)
            t_.transpose(bank[0][:, 0:TT], gsel[:].rearrange("p e t -> p (e t)"), ident[0:TT, 0:TT]).then_inc(S4["gTp"], 1)
            for r in range(7 + 23 + 2):
                pe.wait_ge(S4["cnt"], r + 1 + PRIME)
                mm(bank[1][:, 0:1], expert_rows[:], cnt[:, 0:1], start=True, stop=True).then_inc(S4["tot"], 1)
            pe.wait_ge(S4["eqc"], 1 + PRIME)
            mm(bank[1][:, 0:1], before_rows[:], cnt[:, 1:2], start=True, stop=True).then_inc(S4["eqp"], 1)
            pe.wait_ge(S4["gs"], 1 + PRIME)
            t_.transpose(bank[0][0:TT, 0:128], Gs[:], ident[:]).then_inc(S4["gsTp"], 1)
            pe.wait_ge(S4["gate"], 1 + PRIME)

            with pe.Fori(0, NE // 2) as i:
                pe.wait_ge(S4["w"], (i + 1) * 48)
                for e in range(2):
                    for f in range(FC):
                        for q in range(NQ):
                            k = (e * FC + f) * NQ + q
                            if k >= NQ:
                                pe.wait_ge(S4["h"], i * (2 * FC * NQ) + k - NQ + 1 + PRIME)
                            mm(bank[q][:, 0:QC], w1[:, e, 128 * f:128 * f + 128], x2T[:, QC * q:QC * q + QC], start=True, stop=True).then_inc(S4["up"], 1)
                    pe.wait_ge(S4["h"], i * (2 * FC * NQ) + (e + 1) * FC * NQ + PRIME)
                    for t in range(NT):
                        k = e * NT + t
                        if k >= 4:
                            pe.wait_ge(S4["acc"], i * (2 * NT + 1) + 1 + k - 3 + PRIME)
                        else:
                            pe.wait_ge(S4["acc"], i * (2 * NT + 1) + PRIME)
                        for f in range(FC):
                            last = mm(bank[4 + k % 4][0:TT, 0:D], hT[:, f, TT * t:TT * t + TT], w2[:, e, f, :], start=(f == 0), stop=(f == FC - 1))
                        last.then_inc(S4["dn"], 1)


def flat(t):
    return t[:].rearrange("p t e -> p (t e)")


def view3(t, cols):
    return t[:].rearrange("p (n k) -> p n k", k=cols)



_INS = ["x", "ctx_768", "L0_attn_wq", "L0_attn_wk", "L0_attn_wv", "L0_xattn_Wq", "L0_xattn_bq", "L0_xattn_Wk",
        "L0_xattn_bk", "L0_xattn_Wv", "L0_xattn_bv", "L0_xattn_Wo", "L0_xattn_bo", "L0_ffn_Wr", "L0_ffn_W1", "L0_ffn_W2"]


def kernel(**inputs):
    import numpy as np
    import concourse.bacc as bacc
    from concourse.bass_utils import run_bass_kernel_spmd

    nc = bacc.Bacc("TRN2", target_bir_lowering=False, num_devices=1)
    arrays, args = {}, []
    for name in _INS:
        a = np.ascontiguousarray(inputs[name])
        arrays[f"in_{name}"] = a
        args.append(nc.dram_tensor(f"in_{name}", a.shape, mybir.dt.from_np(a.dtype), kind="ExternalInput").ap())
    out = nc.dram_tensor("out", (B, S, D), F32, kind="ExternalOutput").ap()
    decoder_kernel(nc, *args, out)
    r = run_bass_kernel_spmd(nc, [arrays], core_ids=[0])
    return r.results[0]["out"]
```

```python
import math
from collections import namedtuple
from contextlib import ExitStack

import concourse.bass as bass
from concourse import mybir

F32 = mybir.dt.float32
F32R = mybir.dt.float32r
I32 = mybir.dt.int32
ALU = mybir.AluOpType
ACT = mybir.ActivationFunctionType
AX = mybir.AxisListType

B, S, D = 32, 56, 128
NK, DC = 1500, 96
H, DH = 16, 8
NE, FF, TOPK = 8, 512, 2
CAP = max(math.ceil(B * S * TOPK * 1.25 / NE), 1)
EPS, CLAMP = 1e-5, 10000.0
TT = 2 * S
NT = B // 2
QT = 4
NQ = NT // QT
QC = QT * TT
CK = 125
NC = NK // CK
KB = 500
NB = NK // KB
G2 = H // 2
X_OF = ("x0", "x1q")
UNITS = NE * NQ
ROUNDS = 7 + 23 + 2
V_SLOTS = (9, 10, 11)
SLOTS = 4
FC = FF // 128
NEG = -3.0e38
HQ = H * S
RG = HQ // 128
HG = H // 4
AP_ = RG * NB
SUM = 0
V3, V1 = 3 * DH + 1, DH + 1
VC = 4 * (V3 + V1)
PLAIN = 9000.0
ARENA = 19700
PRIME = 4


Quad = namedtuple("Quad", "xq xT u v s e aT nm rs ri y xn stats mv ve rstd pad")


def decoder_kernel(nc, gate_rows, x, ctx_in, wq, wk, wv, xWq, xbq, xWk, xbk, xWv, xbv, xWo, xbo, Wr, W1, W2, out):
    stack = ExitStack()

    def sb(name, shape, dt=F32):
        return stack.enter_context(nc.sbuf_tensor(name, shape, dt))

    def sem(name):
        return stack.enter_context(nc.semaphore(name))

    with stack:
        psum = stack.enter_context(nc.psum_tensor("psum", [128, 8, 512], F32))
        bank = [psum[:, i, :] for i in range(8)]
        ident = sb("ident", [128, 128])
        other_batch = sb("other_batch", [TT, TT])
        causal = sb("causal", [TT, TT])
        head_rows = sb("head_rows", [128, H])
        pair_rows = sb("pair_rows", [TT, 2])
        fold_q = sb("fold_q", [TT, S])
        expert_rows = sb("expert_rows", [128, 128])
        before_rows = sb("before_rows", [128, 128])
        ones = sb("ones", [128, 128])
        minus_half = sb("minus_half", [128, QT])
        index_prio = sb("index_prio", [TT, NE])
        perm = sb("perm", [128, SLOTS, 128])
        w_sb = {n: sb(n + "_sb", [128, 128]) for n in ("wq", "wk", "wv", "xWq", "xWo")}
        qk = sb("qk", [128, 128])
        wvT = sb("wvT", [128, 128])
        bq_col = sb("bq_col", [128, 1])
        WkA = sb("WkA", [DC + 1, 128])
        WvA = sb("WvA", [DC + 1, 128])
        WoP = sb("WoP", [128, SLOTS, 128])
        bo_row = sb("bo_row", [1, 128])
        Wr_sb = sb("Wr_sb", [128, NE])
        x1_all = sb("x1_all", [TT, NT, D])
        x2_all = x1_all
        Qt_all = sb("Qt_all", [128, B * S])
        OS_all = sb("OS_all", [128, SLOTS, B * S])
        K_hi = sb("K_hi", [128, 2, NK], F32R)
        K_st = sb("K_st", [128, 2, HG, NK], F32R)
        Q_st = sb("Q_st", [DC + 1, 2, HG, 4, S], F32R)
        Q_bd = sb("Q_bd", [128, 2, H, S], F32R)
        max_row = sb("max_row", [RG, 128], F32R)
        four_heads = sb("four_heads", [DC, 4])
        sum_rows = sb("sum_rows", [128, 128])
        sum_row = sb("sum_row", [128, 1])
        arena = sb("arena", [128, ARENA])
        used = [0]
        whole = arena[:]

        def at(parts, *shape, place=None):
            n = math.prod(shape)
            o = used[0]
            used[0] += n
            place = whole if place is None else place
            assert used[0] <= place.shape[-1], used[0]
            v = place[0:parts, o:o + n]
            if len(shape) == 2:
                v = v.rearrange("p (a b) -> p a b", b=shape[1])
            elif len(shape) == 3:
                v = v.rearrange("p (a b c) -> p a b c", b=shape[1], c=shape[2])
            return v

        Qs_all = at(DC, HG, B * S)
        start = used[0]

        def quad_buffers(place):
            new = lambda *shape: at(*shape, place=place)
            return Quad(xq=new(TT, QT, D), xT=new(128, QC), u=new(128, QC), v=new(TT, QT, D), s=new(TT, QT, TT), e=new(TT, QT, TT),
                        aT=new(TT, QT, TT), nm=new(TT, QT), rs=new(TT, QT), ri=new(TT, QT), y=new(TT, QT, D), xn=new(TT, QT, D),
                        stats=new(TT, QT, 6), mv=new(TT, QT, 2), ve=new(TT, QT), rstd=new(TT, QT), pad=new(1, 1))
        first = quad_buffers(whole)
        after1 = used[0]
        used[0] = 0
        quads1 = [first, quad_buffers(OS_all[:].rearrange("p s n -> p (s n)"))]
        used[0] = after1
        quads3 = [first, quad_buffers(whole)]
        in_place = used[0]
        OSq = [at(128, SLOTS, QC) for _ in range(2)]
        used[0] = in_place
        gates = [at(128, NQ, QC) for _ in range(2)]
        used[0] = 0
        results = at(128, UNITS // 2, QC, place=OS_all[:].rearrange("p s n -> p (s n)"))
        y_sum = Qt_all[:].rearrange("p (q n) -> p q n", q=NQ)
        x_hi = K_hi[:].rearrange("p a k -> p (a k)")[:, 0:B * S]
        x_lo = Q_bd[:].rearrange("p a h q -> p (a h q)")
        used[0] = 0
        expert_place = K_st[:].rearrange("p a g k -> p (a g k)")
        h_hi, h_lo = [[at(128, FC, QC, place=expert_place) for _ in range(2)] for _ in range(2)]
        w1_hi, w1_lo = [[at(128, FF, place=expert_place) for _ in range(2)] for _ in range(2)]
        w2_hi, w2_lo = [[at(128, FC, 128, place=expert_place) for _ in range(2)] for _ in range(2)]
        Q_hi = K_hi[:].rearrange("p a k -> p (a k)")[:, 0:B * S]
        Q_lo = Q_bd[:].rearrange("p a h q -> p (a h q)")
        used[0] = start
        P2 = [at(CK, HQ) for _ in range(2)]
        K_lo = at(128, NK)
        O_sb = at(128, SLOTS * S)
        R_sb = at(128, SLOTS * S)
        mx = at(128, RG, NB)
        used[0] = max(used[0], after1)
        C2 = at(CK, NC, DC)
        ctxT2 = at(DC + 1, 2, NK)
        V2 = [at(CK, NC, VC) for _ in range(2)]
        m2x = at(128, RG)
        m_high = at(128, RG)
        m_low = at(128, RG)
        chk = at(128, 1)
        chk_sum = at(128, 1)
        bad = at(128, 2)
        used[0] = start
        C = at(CK, NC, DC)
        ctxT = at(DC + 1, NK)
        KT = at(128, NK)
        V = at(CK, NC, 128)
        Qbd = at(128, H, S)
        Sc = at(TT, NK)
        P = at(TT, NK)
        PT = at(CK, NC, TT)
        Om = at(TT, 128)
        OT = at(128, 2, S)
        c1 = at(TT, 1)
        c2 = at(TT, 1)
        rowmax = at(TT, 1)
        negmax = at(TT, 1)
        rowsum = at(TT, 1)
        rinv = at(TT, 1)
        numbers = at(TT, 1)
        nan_mask = at(TT, 1)
        nan_col = at(128, 1)
        nan_int = at(128, 1).bitcast(I32)
        OM_all = at(128, SLOTS, B)
        used[0] = 0
        x2T = at(128, NT * TT)
        pr = at(TT, NT, NE)
        pw = at(TT, NT, NE)
        eq = at(TT, NT, NE)
        hot = at(TT, NT, NE)
        mask = at(TT, NT, NE)
        m1 = at(TT, NT)
        m2 = at(TT, NT)
        gsel = at(TT, NE, NT)
        G = at(128, TT)
        gscr = at(128, TT)
        gtm = at(128, TT)
        eqm = at(128, TT)
        pref = at(128, TT)
        cand = at(128, 1)
        fac = at(128, 1)
        cnt = at(128, 2)
        room = at(128, 1)
        Gs = at(128, TT)
        w1 = at(128, 2, FF)
        w2 = at(128, 2, FC, 128)
        assert used[0] <= start, used[0]
        flag_int = sb("flag_int", [1, 1], I32)
        zrow = sb("zrow", [128, TT])
        thr = sb("thr", [128, 1])
        stepv = sb("stepv", [128, 1])

        dve_step = sem("dve_step")
        clamp_step = sem("clamp_step")
        pool_step = sem("pool_step")
        consts = sem("consts")
        weights = sem("weights")
        w_ps = sem("w_ps"); w_ev = sem("w_ev")

        S1 = {n: sem("s1_" + n) for n in ("x0", "x1q", "s", "split", "xTp", "xT", "up", "u", "vp", "v", "sp", "max", "e", "a", "aTp", "aT", "op",
                                          "y", "ve", "rstd", "xn", "x1", "xnTp", "xnT", "qp", "q")}
        S2 = {n: sem("s2_" + n) for n in ("c", "cTp", "cT", "kp", "k", "vp", "v", "qbd", "sp", "s", "m", "e", "pTp", "pT", "op", "om",
                                          "otp", "ot", "osp", "os", "nan", "nanrow", "nanall", "fix")}
        S3 = {n: sem("s3_" + n) for n in ("osq", "op", "y", "ve", "rstd", "xn", "xnTp", "xnT", "x2")}
        S4 = {n: sem("s4_" + n) for n in ("x_lo", "lg", "pr", "e", "g", "gTp", "cnt", "tot", "eqc", "eqp", "gs", "w_hi", "w_split", "up", "hi", "lo", "dn",
                                          "y", "gated", "acc", "op", "y2", "ve", "rstd", "xn")}
        W_ = [sem(f"w_{p}") for p in range(2)]
        G_ = [sem(f"g_{p}") for p in range(2)]
        g_out, out_done = sem("g_out"), sem("out_done")

        F = {n: sem("f_" + n) for n in ("cTp", "cT", "kp", "k", "khi", "klo", "vp", "v", "qa", "qs", "ap", "am", "mx", "ab", "m", "mTp", "mr",
                                        "bp", "e", "pv", "o", "rp", "r", "os", "chk", "ready", "bad", "sum", "flag")}
        D_ = {n: sem("d_" + n) for n in ("c", "khi0", "khi1", "klo0", "klo1", "mrow", "q")}
        primed = [s_ for d in (S1, S2, S3, S4) for n, s_ in d.items() if n not in ("x0", "x1q", "c")] + list(F.values())

        def periods(eng, period):
            for b in range(-2, 2):
                period(b, b % 2, b // 2)
            with eng.Fori(1, B // 2 - 2) as i:
                for par in range(2):
                    period(i * 2 + par, par, i)
            for b in range(B - 4, B + 1):
                period(b, b % 2, b // 2)

        def pieces(c):
            if c < 6:
                return [(1, 9 + 2 * c), (1, 10 + 2 * c)]
            return [(2, n) for n in {6: (0,), 7: (1,), 8: (2, 3), 9: (4,), 10: (5, 6), 11: (7, 8)}[c]]

        def bank_of(n):
            return bank[(n + 1 if 1 <= n < 9 else n + 1 if n >= 9 else 0) % 2]

        def experts_after(eng, unit):
            with eng.Fori(0, NE // 4) as i:
                for k in range(2 * NQ):
                    unit(i * (2 * NQ) + (UNITS // 2 + k), k)

        def has(b, ahead):
            return not isinstance(b, int) or 0 <= b + ahead < B

        block = stack.enter_context(nc.Block())

        @block.sync
        def _(sp):
            for t, src in ((w_sb["wq"], wq), (w_sb["wk"], wk), (w_sb["wv"], wv), (w_sb["xWq"], xWq), (w_sb["xWo"], xWo)):
                sp.dma_start(t[:], src).then_inc(weights, 16)
            sp.dma_start(bq_col[:], xbq.rearrange("(p a) -> p a", a=1)).then_inc(weights, 16)
            sp.dma_start(WkA[0:DC, :], xWk).then_inc(weights, 16)
            sp.dma_start(WkA[DC:DC + 1, :], xbk.rearrange("(a p) -> a p", a=1)).then_inc(weights, 16)
            sp.dma_start(WvA[0:DC, :], xWv).then_inc(weights, 16)
            sp.dma_start(WvA[DC:DC + 1, :], xbv.rearrange("(a p) -> a p", a=1)).then_inc(weights, 16)
            sp.dma_start(bo_row[:], xbo.rearrange("(a p) -> a p", a=1)).then_inc(weights, 16)
            sp.dma_start(Wr_sb[:], Wr).then_inc(weights, 16)
            for s_ in primed:
                sp.sem_inc(s_, PRIME)
            xv = x.rearrange("(n t b) s d -> n (b s) t d", t=QT, b=2)

            def load_tokens(n, h):
                sp.wait_ge(S1["y"], n - 1 + PRIME)
                sp.dma_start(quads1[h].xq, xv[bass.ds(n, 1), :, :, :].rearrange("a p t d -> (a p) t d")).then_inc(S1[X_OF[h]], 16)

            def stack_queries(n):
                sp.wait_ge(S1["split"], 2 * (n + 1) + PRIME)
                for q, part in enumerate((Q_hi, Q_lo, Q_hi)):
                    for g in range(HG):
                        sp.dma_start(Qs_all[32 * q:32 * q + 32, g, bass.ts(n, 2 * QC)], part[32 * g:32 * g + 32, bass.ts(n, 2 * QC)].bitcast(F32))\
                          .then_inc(D_["q"], 16)
            for h in range(2):
                load_tokens(h, h)
            with sp.Fori(0, NQ // 2 - 1) as i:
                for h in range(2):
                    load_tokens(i * 2 + (2 + h), h)
                stack_queries(i)
            cv = ctx_in.rearrange("b (p c) d -> b p c d", c=NC)

            def load_context(b):
                sp.dma_start(C2, cv[bass.ds(b, 1), :, :, :].rearrange("a p c d -> (a p) c d")).then_inc(D_["c"], 16)
            load_context(0)
            stack_queries(NQ // 2 - 1)

            def period(b, par, half):
                if has(b, 1):
                    sp.wait_ge(F["klo"], (b + 2) * NB + PRIME)
                    if not isinstance(b, int) or b >= 1:
                        sp.wait_ge(F["bp"], b * NC + PRIME)
                    for q, part in ((2, K_lo), (0, K_hi[:, 1 - par]), (1, K_hi[:, 1 - par])):
                        for g in range(HG):
                            sp.dma_start(K_st[32 * q:32 * q + 32, 1 - par, g, :].bitcast(F32), part[32 * g:32 * g + 32, :].bitcast(F32))\
                              .then_inc(D_[f"{'klo' if q == 2 else 'khi'}{1 - par}"], 16)
                if has(b, 3):
                    sp.wait_ge(F["cTp"], (b + 3) * NB + PRIME)
                    load_context(b + 3)
                if has(b, 1):
                    sp.wait_ge(F["mr"], b + 2 + PRIME)
                    last_row = Q_st[DC:DC + 1, 1 - par].rearrange("a g h q -> a (g h q)")
                    for j in range(RG):
                        sp.dma_start(last_row[:, 128 * j:128 * j + 128].bitcast(F32), max_row[j:j + 1, :].bitcast(F32)).then_inc(D_["mrow"], 16)
            periods(sp, period)
            sp.wait_ge(F["flag"], 1 + PRIME)
            clamped = sp.value_load(flag_int[0:1, 0:1], min_val=0, max_val=1)
            with sp.If(clamped > 0), sp.Fori(0, B) as i:
                sp.wait_ge(S2["cTp"], i + PRIME)
                sp.dma_start(C[:], cv[bass.ds(i, 1), :, :, :].rearrange("a p c d -> (a p) c d")).then_inc(S2["c"], 16)
            def load_weights(e, p):
                sp.wait_ge(S4["w_split"], e - 1 + PRIME)
                sp.dma_start(w1[:, p], W1[bass.ds(e, 1)].rearrange("a p f -> (a p) f")).then_inc(W_[p], 16)
                sp.dma_start(w2[:, p], W2[bass.ds(e, 1)].rearrange("a (c p) d -> (a p) c d", p=128)).then_inc(W_[p], 16)

            def load_gates(e, p):
                if e >= 2:
                    sp.wait_ge(S4["gated"], e * NQ - NQ + PRIME)
                sp.dma_start(gates[p].rearrange("p q n -> p (q n)"), gate_rows[bass.ds(e, 1), :].to_broadcast([128, B * S])).then_inc(G_[p], 16)
            for e in range(NE - 2):
                load_weights(e, e % 2)
            sp.wait_ge(S4["gs"], 1 + PRIME)
            sp.dma_start(gate_rows.rearrange("e (t n) -> (e t) n", n=TT), Gs).then_inc(g_out, 16)
            sp.wait_ge(g_out, 16)
            for e in range(NE):
                load_gates(e, e % 2)
                if e in (1, 2):
                    load_weights(NE - 3 + e, (NE - 3 + e) % 2)
            ov = out.rearrange("(n t b) s d -> n (b s) t d", t=QT, b=2)
            for n in range(NQ):
                sp.wait_ge(S4["xn"], n + 1 + PRIME)
                sp.dma_start(ov[n], x2_all[:, QT * n:QT * n + QT, :]).then_inc(out_done, 16)
            sp.wait_ge(out_done, 16 * NQ)

        @block.gpsimd
        def _(pool):
            g = nc.gpsimd
            n = [0]

            def step(ins):
                n[0] += 1
                ins.then_inc(pool_step, 1)
                pool.wait_ge(pool_step, n[0])

            def keep(t, pattern, base, mult, op=ALU.is_ge, fill=0.0):
                step(g.affine_select(out=t, in_=t, pattern=pattern, compare_op=op, fill=fill, base=base,
                                     channel_multiplier=mult))

            for t, v in ((ident, 0.0), (perm, 0.0)):
                step(g.memset(t[:], v))
            keep(ident[:], [[-1, 128]], 0, 1, ALU.not_equal, 1.0)
            for s in range(SLOTS - 1):
                step(g.tensor_copy(perm[:, s, :].rearrange("p (g c) -> p g c", c=32)[:, :, 1 + DH * s:1 + DH * s + DH],
                                   ident[:, 0:96].rearrange("p (g c) -> p g c", c=24)[:, :, DH * s:DH * s + DH]))
            g.tensor_copy(perm[:, 3, :].rearrange("p (g c) -> p g c", c=32)[:, :, 1:V1],
                          ident[:, 96:128].rearrange("p (g c) -> p g c", c=DH)).then_inc(consts, 1)
            for t, v in ((other_batch, 0.0), (causal, 1.0), (head_rows, 1.0), (pair_rows, 1.0), (fold_q, 0.0),
                         (expert_rows, 1.0), (before_rows, 1.0), (ones, 1.0), (minus_half, -0.5), (zrow, 0.0),
                         (sum_rows, 0.0), (sum_row, 0.0), (thr, 1.0), (stepv, 0.5)):
                step(g.memset(t[:], v))
            keep(other_batch[:, 0:S], [[0, S]], S - 1, -1, fill=NEG)
            keep(other_batch[:, S:TT], [[0, S]], -S, 1, fill=NEG)
            keep(causal[:], [[-1, TT]], 0, 1)
            keep(causal[:, 0:S], [[0, S]], S - 1, -1)
            keep(head_rows[:], [[-DH, H]], 0, 1)
            keep(head_rows[:], [[DH, H]], DH - 1, -1)
            keep(pair_rows[:, 0:1], [[0, 1]], S - 1, -1)
            keep(pair_rows[:, 1:2], [[0, 1]], -S, 1)
            keep(fold_q[:], [[-1, S]], 0, 1, ALU.not_equal, 1.0)
            keep(fold_q[:], [[-1, S]], -S, 1, ALU.not_equal, 1.0)
            ev = expert_rows[:].rearrange("p (e s) -> p e s", s=NT)
            keep(ev, [[-NT, NE], [0, NT]], 0, 1)
            keep(ev, [[NT, NE], [0, NT]], NT - 1, -1)
            bv = before_rows[:].rearrange("p (e s) -> p e s", s=NT)
            keep(bv, [[-NT, NE], [0, NT]], 0, 1)
            keep(bv, [[NT, NE], [1, NT]], -1, -1)
            for e in range(NE):
                step(g.memset(index_prio[:, e:e + 1], float(NE - e)))
            keep(sum_rows[:].rearrange("p (g c) -> p g c", c=32), [[-32, 4], [0, 32]], -SUM, 1, ALU.not_equal, 1.0)
            for g4 in range(4):
                keep(sum_row[:], [[0, 1]], -SUM - 32 * g4, 1, ALU.not_equal, 1.0)
            for a3 in range(3):
                step(g.tensor_copy(four_heads[32 * a3:32 * a3 + 32, :], head_rows[32 * a3:32 * a3 + 32, 4 * a3:4 * a3 + 4]))
            pool.sem_inc(consts, 1)
            for par in range(2):
                step(g.memset(V2[par][:, :, 0:4 * V3].rearrange("p c (m r) -> p c m r", r=V3)[:, :, :, SUM], 1.0))
                step(g.memset(V2[par][:, :, 4 * V3:VC].rearrange("p c (m r) -> p c m r", r=V1)[:, :, :, SUM], 1.0))
            step(g.memset(ctxT2[DC:DC + 1], 1.0))
            step(g.memset(K_st[DC:DC + 1].rearrange("p a g k -> p (a g k)").bitcast(F32), 1.0))
            pool.sem_inc(F["ready"], 1)
            with pool.Fori(0, NQ // 2) as i:
                for h in range(2):
                    q = quads1[h]
                    pool.wait_ge(S1["ve"], i * 2 + (h + 1) + PRIME)
                    pool.wait_ge(S1["xn"], i * 2 + (h - 1) + PRIME)
                    g.tensor_tensor(q.rstd, q.ve, minus_half[0:TT], ALU.pow).then_inc(S1["rstd"], 1)
            pool.wait_ge(S1["q"], NQ + PRIME)
            pool.wait_ge(D_["q"], 16 * 3 * HG * (NQ // 2))

            def period(b, par, half):
                if has(b, 2):
                    if not isinstance(b, int) or b >= 0:
                        pool.wait_ge(F["ap"], (b + 1) * AP_ + PRIME)
                    g.tensor_tensor(Q_bd[:, par], Qt_all[:, bass.ds((b + 2) * S, S)].unsqueeze(1).to_broadcast([128, H, S]),
                                    head_rows[:].unsqueeze(2).to_broadcast([128, H, S]), ALU.mult).then_inc(F["qa"], 1)
                if has(b, 1):
                    if not isinstance(b, int) or b >= 1:
                        pool.wait_ge(F["bp"], b * NC + PRIME)
                    g.tensor_tensor(Q_st[0:DC, 1 - par], Qs_all[:, :, bass.ds((b + 1) * S, S)].unsqueeze(2).to_broadcast([DC, HG, 4, S]),
                                    four_heads[:].unsqueeze(1).unsqueeze(3).to_broadcast([DC, HG, 4, S]), ALU.mult).then_inc(F["qs"], 1)
                if has(b, 2):
                    for n in range(NB):
                        pool.wait_ge(F["khi"], b * NB + (2 * NB + n + 1) + PRIME)
                        low = K_lo[:, n * KB:n * KB + KB]
                        g.tensor_tensor(low.bitcast(F32R), low, K_hi[:, par, n * KB:n * KB + KB].bitcast(F32), ALU.subtract).then_inc(F["klo"], 1)
            periods(pool, period)
            pool.wait_ge(F["flag"], 1 + PRIME)
            with pool.Fori(0, NQ // 2) as i:
                for h in range(2):
                    q = quads3[h]
                    pool.wait_ge(S3["ve"], i * 2 + (h + 1) + PRIME)
                    pool.wait_ge(S3["xn"], i * 2 + (h - 1) + PRIME)
                    g.tensor_tensor(q.rstd, q.ve, minus_half[0:TT], ALU.pow).then_inc(S3["rstd"], 1)
                for h in range(2):
                    cols = bass.ts(i * 2 + h, QC)
                    pool.wait_ge(S3["xnT"], i * 2 + (h + 1) + PRIME)
                    g.tensor_tensor(x_lo[:, cols], x2T[:, cols], x_hi[:, cols].bitcast(F32), ALU.subtract).then_inc(S4["x_lo"], 1)
            g.memset(y_sum, 0.0)

            def split_weights(e, p, loads):
                pool.wait_ge(W_[p], loads * 32)
                if not isinstance(e, int) or e >= 2:
                    pool.wait_ge(S4["dn"], e * NQ - NQ + PRIME)
                g.tensor_tensor(w1_hi[p], w1[:, p], ones[:, 0:1].to_broadcast([128, FF]), ALU.mult)
                g.tensor_tensor(w2_hi[p], w2[:, p], ones[:, 0:1].unsqueeze(2).to_broadcast([128, FC, 128]), ALU.mult).then_inc(S4["w_hi"], 1)
                pool.wait_ge(S4["w_hi"], e + 1 + PRIME)
                g.tensor_tensor(w1_lo[p], w1[:, p], w1_hi[p].bitcast(F32), ALU.subtract)
                g.tensor_tensor(w2_lo[p], w2[:, p], w2_hi[p].bitcast(F32), ALU.subtract).then_inc(S4["w_split"], 1)
            for e in range(NE // 2):
                split_weights(e, e % 2, e // 2 + 1)
            with pool.Fori(0, NE // 4) as i:
                for k in range(4 * NQ):
                    if k % (2 * NQ) == 0:
                        split_weights(i * 2 + (NE // 2 + k // (2 * NQ)), k // (2 * NQ), i + (NE // 4 + 1))
                    p = (k // NQ) % 2
                    pool.wait_ge(G_[p], (i * 2 + (k // (2 * NQ) + 1)) * 16)
                    pool.wait_ge(S4["y"], i * (4 * NQ) + (k + 1) + PRIME)
                    g.tensor_tensor(results[:, k], results[:, k], gates[p][:, k % NQ], ALU.mult).then_inc(S4["gated"], 1)
            for n in range(NQ):
                q = quads3[n % 2]
                pool.wait_ge(S4["ve"], n + 1 + PRIME)
                pool.wait_ge(S4["xn"], n - 1 + PRIME)
                g.tensor_tensor(q.rstd, q.ve, minus_half[0:TT], ALU.pow).then_inc(S4["rstd"], 1)

        @block.scalar
        def _(act):
            a = nc.scalar
            with act.Fori(0, NQ // 2) as i:
                for h in range(2):
                    act.wait_ge(S1["xTp"], i * 2 + (h + 1) + PRIME)
                    a.copy(quads1[h].xT, bank[0][:, 0:QC]).then_inc(S1["xT"], 1)
                for h in range(2):
                    act.wait_ge(S1["up"], i * 2 + (h + 1) + PRIME)
                    a.copy(quads1[h].u, bank[1][:, 0:QC]).then_inc(S1["u"], 1)
                    act.wait_ge(S1["vp"], i * 2 + (h + 1) + PRIME)
                    a.copy(quads1[h].v, bank[2][0:TT, :].rearrange("p (t d) -> p t d", t=QT)).then_inc(S1["v"], 1)
                for h in range(2):
                    act.wait_ge(S1["max"], i * 2 + (h + 1) + PRIME)
                    a.activation(quads1[h].e, quads1[h].s, ACT.Exp).then_inc(S1["e"], 1)
                for h in range(2):
                    act.wait_ge(S1["aTp"], i * 2 + (h + 1) + PRIME)
                    a.copy(quads1[h].aT, bank[4][0:TT, 0:QC].rearrange("p (t k) -> p t k", t=QT)).then_inc(S1["aT"], 1)
                for h in range(2):
                    act.wait_ge(S1["xnTp"], i * 2 + (h + 1) + PRIME)
                    a.copy(quads1[h].xT, bank[6][:, 0:QC]).then_inc(S1["xnT"], 1)
                    act.wait_ge(S1["xn"], i * 2 + (h + 1) + PRIME)
                    a.copy(x1_all[:, bass.ts(i * 2 + h, QT), :], quads1[h].xn).then_inc(S1["x1"], 1)
            act.wait_ge(F["ready"], 2 + PRIME)

            def period(b, par, half):
                for c in range(NC):
                    if c == 1 and has(b, -1):
                        act.wait_ge(F["pv"], b * NC + PRIME)
                        if not isinstance(b, int) or b >= 2:
                            act.wait_ge(F["os"], b - 1 + PRIME)
                        a.copy(O_sb, bank[6][:, 0:SLOTS * S]).then_inc(F["o"], 1)
                    if has(b, 0):
                        act.wait_ge(F["bp"], b * NC + (c + 1) + PRIME)
                        if not (isinstance(b, int) and b == 0 and c < 2):
                            act.wait_ge(F["pv"], b * NC + (c - 1) + PRIME)
                        a.activation(P2[c % 2].rearrange("p (n k) -> p n k", n=2), psum[0:CK, 2 + 2 * (c % 2):4 + 2 * (c % 2), 0:HQ // 2], ACT.Exp)\
                         .then_inc(F["e"], 1)
                    if c < 3 and has(b, 2):
                        act.wait_ge(F["cTp"], b * NB + (2 * NB + c + 1) + PRIME)
                        if not isinstance(b, int) or b >= 0:
                            act.wait_ge(F["vp"], (b + 1) * NB + PRIME)
                        a.copy(ctxT2[0:DC, par, c * KB:c * KB + KB], bank[7][0:DC, 0:KB]).then_inc(F["cT"], 1)
                    if 3 <= c < 6 and has(b, 2):
                        n = c - 3
                        act.wait_ge(F["kp"], b * NB + (2 * NB + n + 1) + PRIME)
                        if not isinstance(b, int) or b >= 0:
                            act.wait_ge(F["ap"], (b + 1) * AP_ + PRIME)
                            act.wait_ge(D_[f"khi{par}"], (half + 1) * (16 * 2 * HG))
                        if not isinstance(b, int) or b >= -1:
                            act.wait_ge(D_[f"klo{1 - par}"], (half + (par + 1)) * (16 * HG))
                        a.copy(K_lo[:, n * KB:n * KB + KB], bank[7][:, 0:KB]).then_inc(F["k"], 1)
                        act.wait_ge(F["k"], b * NB + (2 * NB + n + 1) + PRIME)
                        if isinstance(b, int) and b == -2 and n == 0:
                            act.wait_ge(D_["q"], 16 * 3 * HG * (NQ // 2))
                        a.copy(K_hi[:, par, n * KB:n * KB + KB], K_lo[:, n * KB:n * KB + KB]).then_inc(F["khi"], 1)
                    if c in V_SLOTS and has(b, 1):
                        n = V_SLOTS.index(c)
                        act.wait_ge(F["vp"], b * NB + (NB + n + 1) + PRIME)
                        if not isinstance(b, int) or b >= 1:
                            act.wait_ge(F["pv"], b * NC + PRIME)
                        src = bank[7][0:CK, :].rearrange("p (c k) -> p c k", c=4)
                        three = V2[1 - par][:, 4 * n:4 * n + 4, 0:4 * V3].rearrange("p c (m r) -> p c m r", r=V3)
                        one = V2[1 - par][:, 4 * n:4 * n + 4, 4 * V3:VC].rearrange("p c (m r) -> p c m r", r=V1)
                        a.copy(three[:, :, :, 1:V3], src[:, :, 0:96].rearrange("p c (m r) -> p c m r", r=24))
                        a.copy(one[:, :, :, 1:V1], src[:, :, 96:128].rearrange("p c (m r) -> p c m r", r=DH)).then_inc(F["v"], 1)
            periods(act, period)
            act.wait_ge(F["flag"], 1 + PRIME)
            clamped = act.value_load(flag_int[0:1, 0:1], min_val=0, max_val=1)
            with act.If(clamped > 0), act.Fori(0, B) as i:
                for n in range(NB):
                    act.wait_ge(S2["cTp"], i + 1 + PRIME)
                    a.copy(ctxT[0:DC, n * KB:n * KB + KB], bank[n][0:DC, 0:KB]).then_inc(S2["cT"], 1)
                for n in range(NB):
                    act.wait_ge(S2["kp"], i + 1 + PRIME)
                    a.copy(KT[:, n * KB:n * KB + KB], bank[n][:, 0:KB]).then_inc(S2["k"], 1)
                for n in range(NB):
                    act.wait_ge(S2["vp"], i + 1 + PRIME)
                    a.copy(V[:, 4 * n:4 * n + 4, :], bank[3 + n][0:CK, :].rearrange("p (c d) -> p c d", c=4)).then_inc(S2["v"], 1)
                for j in range(G2):
                    act.wait_ge(S2["m"], i * G2 + j + 1 + PRIME)
                    act.wait_ge(S2["pTp"], i * G2 + j + PRIME)
                    a.activation(P[:], Sc[:], ACT.Exp, bias=negmax[:], accum_out=rowsum[:]).then_inc(S2["e"], 1)
                    for n in range(NB):
                        act.wait_ge(S2["pTp"], i * G2 + j + 1 + PRIME)
                        a.copy(PT[:, 4 * n:4 * n + 4, :], bank[3 + n][0:CK, 0:4 * TT].rearrange("p (c q) -> p c q", c=4)).then_inc(S2["pT"], 1)
                act.wait_ge(S2["otp"], i + 1 + PRIME)
                a.copy(OT[:], bank[7][:, 0:2 * S].rearrange("p (a q) -> p a q", a=2)).then_inc(S2["ot"], 1)
            with act.Fori(0, NQ // 2) as i:
                for h in range(2):
                    act.wait_ge(S3["xnTp"], i * 2 + (h + 1) + PRIME)
                    a.copy(x2T[:, bass.ts(i * 2 + h, QC)], bank[6][:, 0:QC])
                    a.copy(x_hi[:, bass.ts(i * 2 + h, QC)], bank[6][:, 0:QC]).then_inc(S3["xnT"], 1)
            act.wait_ge(S4["pr"], 1 + PRIME)
            a.activation(pw[:], pr[:], ACT.Exp).then_inc(S4["e"], 1)

            def unit(u, k):
                for f in range(FC):
                    act.wait_ge(S4["up"], u * FC + (f + 1) + PRIME)
                    act.wait_ge(S4["dn"], u - 1 + PRIME)
                    a.activation(h_hi[k % 2][:, f], bank[f][:, 0:QC], ACT.Relu).then_inc(S4["hi"], 1)

            def result(u, p, slot):
                act.wait_ge(S4["dn"], u + 1 + PRIME)
                if not isinstance(u, int) or u >= UNITS // 2:
                    act.wait_ge(S4["acc"], u - (UNITS // 2 - 1) + PRIME)
                a.activation(results[:, bass.ds(slot, 1)], bank[4 + p][:, 0:QC].unsqueeze(1), ACT.Copy).then_inc(S4["y"], 1)
            for u in range(UNITS // 2):
                unit(u, u)
                if u:
                    result(u - 1, (u - 1) % 2, u - 1)
            with act.Fori(0, NE // 4) as i:
                for k in range(2 * NQ):
                    u = i * (2 * NQ) + (UNITS // 2 + k)
                    unit(u, k)
                    result(u - 1, (k - 1) % 2, i * (2 * NQ) + (k - 1) if k else i * (-2 * NQ) + (UNITS // 2 - 1))
            result(UNITS - 1, 1, UNITS // 2 - 1)

        @block.vector
        def _(dve):
            v = nc.vector
            done = [0]

            def tie(base, sem_=dve_step):
                def step(ins):
                    done[0] += 1
                    ins.then_inc(sem_, 1)
                    dve.wait_ge(sem_, base + done[0])
                return step

            def norm(both, S_, i, quads, src, resid, dst=None, added="y"):
                for h, q in enumerate(quads):
                    dve.wait_ge(S_["op"], i * 2 + (h + 1) + PRIME)
                    v.tensor_tensor(q.y, src(h), resid(h), ALU.add).then_inc(S_[added], 1)
                for h, q in enumerate(quads):
                    dve.wait_ge(S_[added], i * 2 + (h + 1) + PRIME)
                    for t in range(QT):
                        last = v.bn_stats(q.stats[:, t, :], q.y[:, t, :])
                    both(h, last)
                for h, q in enumerate(quads):
                    v.memset(q.pad, 0.0)
                    for t in range(QT):
                        last = v.bn_aggr(q.mv[:, t, :], q.stats[:, t, :])
                    both(h, last)
                for h, q in enumerate(quads):
                    v.tensor_scalar(q.ve, q.mv[:, :, 1], EPS, None, ALU.add).then_inc(S_["ve"], 1)
                for h, q in enumerate(quads):
                    dve.wait_ge(S_["rstd"], i * 2 + (h + 1) + PRIME)
                    for t in range(QT):
                        last = v.tensor_scalar(dst(h, t) if dst else q.xn[:, t, :], q.y[:, t, :], q.mv[:, t, 0:1], q.rstd[:, t:t + 1], ALU.subtract, ALU.mult)
                    last.then_inc(S_["xn"], 1)

            def tie_both(base):
                def both(h, ins):
                    done[0] += 1
                    ins.then_inc(dve_step, 1)
                    if h == 1:
                        dve.wait_ge(dve_step, base + done[0])
                return both

            dve.wait_ge(w_ps, 1)
            v.tensor_copy(qk[:], bank[0][:, 0:128]).then_inc(w_ev, 1)
            v.tensor_copy(wvT[:], bank[1][:, 0:128]).then_inc(w_ev, 1)
            v.tensor_copy(WoP[:], bank[2][:].rearrange("p (s c) -> p s c", s=SLOTS)).then_inc(w_ev, 1)
            dve.wait_ge(weights, 16 * 12)
            step0 = tie(0)
            step0(v.tensor_scalar(bq_col[:], bq_col[:], DH ** -0.5, None, ALU.mult))

            dve.wait_ge(consts, 2)
            K1 = 2 * (2 + 3 + 2)
            base0 = done[0]
            with dve.Fori(0, NQ // 2) as i:
                done[0] = base0
                both = tie_both(i * K1)
                for h, q in enumerate(quads1):
                    dve.wait_ge(S1["sp"], i * 2 + (h + 1) + PRIME)
                    v.scalar_tensor_tensor(q.s, bank[3][0:TT, 0:QC].rearrange("p (t q) -> p t q", t=QT), float(D) ** -0.5,
                                           other_batch[:].unsqueeze(1).to_broadcast([TT, QT, TT]), ALU.mult, ALU.add).then_inc(S1["s"], 1)
                for h, q in enumerate(quads1):
                    dve.wait_ge(S1["s"], i * 2 + (h + 1) + PRIME)
                    both(h, v.reduce_max(q.nm, q.s, AX.X))
                for h, q in enumerate(quads1):
                    v.tensor_tensor(q.s, q.s, q.nm.unsqueeze(2).to_broadcast([TT, QT, TT]), ALU.subtract).then_inc(S1["max"], 1)
                for h, q in enumerate(quads1):
                    dve.wait_ge(S1["e"], i * 2 + (h + 1) + PRIME)
                    both(h, v.reduce_sum(q.rs, q.e, AX.X))
                for h, q in enumerate(quads1):
                    both(h, v.reciprocal(q.ri, q.rs))
                for h, q in enumerate(quads1):
                    both(h, v.tensor_tensor(q.e, q.e, causal[:].unsqueeze(1).to_broadcast([TT, QT, TT]), ALU.mult))
                for h, q in enumerate(quads1):
                    v.tensor_tensor(q.s, q.e, q.ri.unsqueeze(2).to_broadcast([TT, QT, TT]), ALU.mult).then_inc(S1["a"], 1)
                norm(both, S1, i, quads1, lambda h: bank[5][0:TT, :].rearrange("p (t d) -> p t d", t=QT), lambda h: quads1[h].xq)
                for h in range(2):
                    dve.wait_ge(S1["qp"], i * 2 + (h + 1) + PRIME)
                    v.tensor_scalar(Qt_all[:, bass.ts(i * 2 + h, QC)], bank[7][:, 0:QC], DH ** -0.5, bq_col[:], ALU.mult, ALU.add).then_inc(S1["q"], 1)
                for h in range(2):
                    dve.wait_ge(S1["q"], i * 2 + (h + 1) + PRIME)
                    both(h, v.tensor_scalar(Q_hi[:, bass.ts(i * 2 + h, QC)], Qt_all[:, bass.ts(i * 2 + h, QC)], 1.0, None, ALU.mult))
                for h in range(2):
                    cols = bass.ts(i * 2 + h, QC)
                    v.tensor_tensor(Q_lo[:, cols], Qt_all[:, cols], Q_hi[:, cols].bitcast(F32), ALU.subtract).then_inc(S1["split"], 1)
                assert done[0] - base0 == K1, done[0] - base0
            done[0] = base0 + (NQ // 2) * K1

            step = tie(0)
            dve.wait_ge(S1["split"], NQ + PRIME)
            step(v.memset(m_high, 0.0))
            step(v.memset(m_low, 0.0))
            step(v.memset(bank[6], 0.0))
            step(v.memset(chk_sum, 0.0))

            dve.sem_inc(F["ready"], 1)

            def period(b, par, half):
                for c in range(NC):
                    if c == 6 and has(b, 1):
                        dve.wait_ge(F["am"], (b + 2) * AP_ + PRIME)
                        if not isinstance(b, int) or b >= 0:
                            dve.wait_ge(F["mTp"], b + 1 + PRIME)
                            dve.wait_ge(F["ab"], (b + 1) * 2 + PRIME)
                        v.reduce_max(m2x, mx, AX.X).then_inc(F["mx"], 1)
                        dve.wait_ge(F["mx"], b + 2 + PRIME)
                        v.tensor_tensor(m_high, m_high, m2x, ALU.max).then_inc(F["ab"], 1)
                        v.tensor_tensor(m_low, m_low, m2x, ALU.min).then_inc(F["ab"], 1)
                    for ahead, n in pieces(c):
                        if not has(b, ahead):
                            continue
                        dve.wait_ge(F["ap"], b * AP_ + (ahead * AP_ + n + 1) + PRIME)
                        if n == 0 and (not isinstance(b, int) or b >= -1):
                            dve.wait_ge(F["mx"], b + 2 + PRIME)
                        v.reduce_max(mx[:, n // NB, n % NB:n % NB + 1], bank_of(n)[:, 0:KB], AX.X).then_inc(F["am"], 1)
                    if c == 7 and has(b, 1):
                        dve.wait_ge(F["mTp"], b + 2 + PRIME)
                        if not isinstance(b, int) or b >= 0:
                            dve.wait_ge(D_["mrow"], (b + 1) * (16 * RG))
                        v.tensor_scalar(max_row[:], bank[1][0:RG, 0:128], -1.0, None, ALU.mult).then_inc(F["mr"], 1)
                    if c in (6, 7) and has(b, -1):
                        if c == 6:
                            dve.wait_ge(F["rp"], b + PRIME)
                            if not isinstance(b, int) or b >= 2:
                                dve.wait_ge(F["os"], b - 1 + PRIME)
                        part = slice((c - 6) * (SLOTS * S // 2), (c - 5) * (SLOTS * S // 2))
                        v.reciprocal(R_sb[:, part], bank[7][:, part]).then_inc(F["r"], 1)
                    if c == 7 and has(b, -1):
                        dve.wait_ge(F["r"], 2 * b + PRIME)
                        if not isinstance(b, int) or b >= 2:
                            dve.wait_ge(F["chk"], b - 1 + PRIME)
                        v.scalar_tensor_tensor(OS_all[:, :, bass.ds((b - 1) * S, S)], O_sb.rearrange("p (s q) -> p s q", s=SLOTS), 1.0,
                                               R_sb.rearrange("p (s q) -> p s q", s=SLOTS), ALU.mult, ALU.mult, accum_out=chk).then_inc(F["os"], 1)
                        dve.wait_ge(F["os"], b + PRIME)
                        v.tensor_tensor(chk_sum, chk_sum, chk, ALU.add).then_inc(F["chk"], 1)
            periods(dve, period)
            dve.wait_ge(F["chk"], B + PRIME)
            dve.wait_ge(F["ab"], 2 * B + PRIME)
            step(v.tensor_scalar(m_low, m_low, -1.0, None, ALU.mult))
            step(v.tensor_tensor(m_high, m_high, m_low, ALU.max))
            step(v.reduce_max(bad[:, 0:1], m_high, AX.X))
            step(v.tensor_scalar(bad[:, 0:1], bad[:, 0:1], PLAIN, None, ALU.is_ge))
            step(v.tensor_scalar(bad[:, 1:2], chk_sum, 0.0, None, ALU.is_ge))
            step(v.tensor_scalar(bad[:, 1:2], bad[:, 1:2], -1.0, -1.0, ALU.add, ALU.mult))
            step(v.tensor_tensor(bad[:, 1:2], bad[:, 1:2], sum_row[:], ALU.mult))
            v.tensor_tensor(bad[:, 0:1], bad[:, 0:1], bad[:, 1:2], ALU.add).then_inc(F["bad"], 1)
            dve.wait_ge(F["sum"], 1 + PRIME)
            v.tensor_scalar(flag_int[:], bank[0][0:1, 0:1], 0.5, None, ALU.is_ge).then_inc(F["flag"], 1)
            dve.wait_ge(F["flag"], 1 + PRIME)
            clamped = dve.value_load(flag_int[0:1, 0:1], min_val=0, max_val=1)
            with dve.If(clamped > 0):
                outer, done[0] = done[0], 0
                step = tie(0, clamp_step)
                step(v.memset(ctxT[DC:DC + 1, :], 1.0))
                step(v.memset(numbers, float(NK)))

                K2 = G2 * 7
                base0 = done[0]
                with dve.Fori(0, B) as i:
                    done[0] = base0
                    step = tie(i * K2, clamp_step)
                    dve.wait_ge(S2["sp"], i * G2 + PRIME)
                    dve.wait_ge(S1["q"], NQ + PRIME)
                    v.tensor_tensor(Qbd[:], Qt_all[:, bass.ts(i, S)].unsqueeze(1).to_broadcast([128, H, S]),
                                    head_rows[:].unsqueeze(2).to_broadcast([128, H, S]), ALU.mult).then_inc(S2["qbd"], 1)
                    for j in range(G2):
                        n = i * G2 + j
                        dve.wait_ge(S2["sp"], n + 1 + PRIME)
                        dve.wait_ge(S2["e"], n + PRIME)
                        src = psum[0:TT, 0:NB, 0:KB]
                        step(v.tensor_scalar(view3(Sc, KB), src, 0.0, 0.0, ALU.is_ge, ALU.add, accum_out=c1[:]))
                        step(v.tensor_scalar(view3(Sc, KB), src, 0.0, 0.0, ALU.is_lt, ALU.add, accum_out=c2[:]))
                        step(v.tensor_scalar(view3(Sc, KB), src, CLAMP, -CLAMP, ALU.min, ALU.max, accum_out=rowmax[:]))
                        step(v.tensor_tensor(c1[:], c1[:], c2[:], ALU.add))
                        step(v.tensor_tensor(numbers[:], numbers[:], c1[:], ALU.min))
                        step(v.tensor_scalar(Sc[:], Sc[:], -CLAMP, None, ALU.max))
                        v.tensor_scalar(negmax[:], rowmax[:], -1.0, None, ALU.mult).then_inc(S2["m"], 1)
                        dve.wait_ge(S2["e"], n + 1 + PRIME)
                        step(v.reciprocal(rinv[:], rowsum[:]))
                        dve.wait_ge(S2["op"], n + 1 + PRIME)
                        v.scalar_tensor_tensor(Om[:, 16 * j:16 * j + 16].rearrange("p (a d) -> p a d", a=2),
                                               bank[6][0:TT, 0:16].rearrange("p (a d) -> p a d", a=2), rinv[:],
                                               pair_rows[:].unsqueeze(2).to_broadcast([TT, 2, DH]), ALU.mult, ALU.mult).then_inc(S2["om"], 1)
                    dve.wait_ge(S2["osp"], i + 1 + PRIME)
                    v.tensor_scalar(OS_all[:, :, bass.ts(i, S)], bank[6][:, 0:SLOTS * S].rearrange("p (s q) -> p s q", s=SLOTS), 1.0, None, ALU.mult).then_inc(S2["os"], 1)
                    v.tensor_scalar(OM_all[:, :, bass.ds(i, 1)], bank[6][:, SLOTS * S:2 * SLOTS * S].rearrange("p (s q) -> p s q", s=SLOTS)[:, :, 0:1], 1.0 / NK,
                                    None, ALU.mult).then_inc(S2["os"], 1)
                    assert done[0] - base0 == K2, done[0] - base0
                done[0] = base0 + B * K2
                step = tie(0, clamp_step)
                v.tensor_scalar(nan_mask[:], numbers[:], float(NK), None, ALU.is_lt).then_inc(S2["nanrow"], 1)
                dve.wait_ge(S2["nanall"], 1 + PRIME)
                step(v.tensor_scalar(nan_col[:], bank[0][:, 0:1], 0.5, None, ALU.is_ge))
                step(v.tensor_copy(nan_int[:], nan_col[:]))
                dve.wait_ge(S2["os"], 2 * B + PRIME)
                v.copy_predicated(OS_all[:].rearrange("p s (b q) -> p (s b) q", q=S), nan_int.unsqueeze(2).to_broadcast([128, SLOTS * B, S]),
                                  OM_all[:].rearrange("p s b -> p (s b)").unsqueeze(2).to_broadcast([128, SLOTS * B, S])).then_inc(S2["fix"], 1)
                dve.wait_ge(S2["fix"], 1 + PRIME)
                done[0] = outer

            K3 = 2 * 2
            base0 = done[0]
            with dve.Fori(0, NQ // 2) as i:
                done[0] = base0
                both = tie_both(i * K3)
                for h in range(2):
                    dve.wait_ge(S3["op"], i * 2 + (h - 1) + PRIME)
                    v.tensor_scalar(OSq[h], OS_all[:, :, bass.ts(i * 2 + h, QC)], 1.0, None, ALU.mult).then_inc(S3["osq"], 1)
                dve.wait_ge(S3["xnTp"], i * 2 + PRIME)
                dve.wait_ge(S3["x2"], i * 2 + PRIME)
                norm(both, S3, i, quads3, lambda h: bank[5][0:TT, :].rearrange("p (t d) -> p t d", t=QT), lambda h: x1_all[:, bass.ts(i * 2 + h, QT), :])
                for h, q in enumerate(quads3):
                    dve.wait_ge(S3["xn"], i * 2 + (h + 1) + PRIME)
                    v.tensor_scalar(x2_all[:, bass.ts(i * 2 + h, QT), :], q.xn, 1.0, None, ALU.mult).then_inc(S3["x2"], 1)
                assert done[0] - base0 == K3, done[0] - base0
            done[0] = base0 + (NQ // 2) * K3
            step = tie(0)

            def wide(t):
                return t[:].unsqueeze(2).to_broadcast([TT, NT, NE])
            dve.wait_ge(S4["lg"], 1 + PRIME)
            lg = bank[7][0:TT, 0:NT * NE].rearrange("p (t e) -> p t e", e=NE)
            step(v.reduce_max(m1[:], lg, AX.X))
            v.tensor_tensor(pr[:], lg, wide(m1), ALU.subtract).then_inc(S4["pr"], 1)
            dve.wait_ge(S4["e"], 1 + PRIME)
            step(v.reduce_sum(m1[:], pw[:], AX.X))
            step(v.reciprocal(m2[:], m1[:]))
            step(v.tensor_tensor(pr[:], pw[:], wide(m2), ALU.mult))
            step(v.tensor_copy(pw[:], pr[:]))
            for k in range(TOPK):
                step(v.reduce_max(m1[:], pw[:], AX.X))
                step(v.tensor_tensor(eq[:], pw[:], wide(m1), ALU.is_equal))
                step(v.tensor_tensor(eq[:], eq[:], index_prio[:].unsqueeze(1).to_broadcast([TT, NT, NE]), ALU.mult))
                step(v.reduce_max(m2[:], eq[:], AX.X))
                step(v.tensor_tensor(hot[:], eq[:], wide(m2), ALU.is_equal))
                if k == 0:
                    step(v.tensor_copy(mask[:], hot[:]))
                    step(v.scalar_tensor_tensor(flat(pw), flat(hot), -2.0, flat(pw), ALU.mult, ALU.add))
                else:
                    step(v.tensor_tensor(mask[:], mask[:], hot[:], ALU.add))
            step(v.tensor_scalar(pw[:], pr[:], 1.0, None, ALU.add))
            step(v.tensor_tensor(pw[:], pw[:], mask[:], ALU.mult))
            step(v.tensor_tensor(pr[:], pr[:], mask[:], ALU.mult))
            step(v.scalar_tensor_tensor(flat(pr), flat(mask), 1.0, flat(pr), ALU.subtract, ALU.add))
            v.tensor_copy(gsel[:], pr[:].rearrange("p t e -> p e t")).then_inc(S4["g"], 1)
            dve.wait_ge(S4["gTp"], 1 + PRIME)
            step(v.tensor_copy(G[:], bank[7][:, 0:TT]))

            def low_part(u, k, f):
                dve.wait_ge(S4["hi"], u * FC + (f + 1) + PRIME)
                v.scalar_tensor_tensor(h_lo[k % 2][:, f], bank[f][:, 0:QC], 0.0, h_hi[k % 2][:, f].bitcast(F32), ALU.max, ALU.subtract)\
                 .then_inc(S4["lo"], 1)

            rounds = [0]

            def count(op, where):
                v.tensor_scalar(gscr[:], G[:], where, 0.0, op, ALU.add, accum_out=cnt[:, 0:1]).then_inc(S4["cnt"], 1)
                for n in low_parts(rounds[0]):
                    low_part(n // FC, n // FC, n % FC)
                rounds[0] += 1
                dve.wait_ge(S4["tot"], rounds[0] + PRIME)
                return bank[6][:, 0:1]

            for s in (64, 32, 16, 8, 4, 2, 1):
                step(v.tensor_scalar(cand[:], thr[:], 2.0 ** -(s - 1), None, ALU.mult))
                tot = count(ALU.is_ge, cand[:])
                step(v.tensor_scalar(fac[:], tot, float(CAP), 2.0 ** -s, ALU.is_ge, ALU.max))
                step(v.tensor_tensor(thr[:], thr[:], fac[:], ALU.mult))
            step(v.tensor_scalar(stepv[:], thr[:], 0.5, None, ALU.mult))
            for s in range(23):
                step(v.tensor_tensor(cand[:], thr[:], stepv[:], ALU.add))
                tot = count(ALU.is_ge, cand[:])
                step(v.tensor_scalar(fac[:], tot, float(CAP), None, ALU.is_ge))
                step(v.scalar_tensor_tensor(thr[:], fac[:], stepv[:], thr[:], ALU.mult, ALU.add))
                step(v.tensor_scalar(stepv[:], stepv[:], 0.5, None, ALU.mult))
            tot = count(ALU.is_ge, 0.0)
            step(v.tensor_scalar(fac[:], tot, float(CAP), None, ALU.is_ge))
            step(v.tensor_tensor(thr[:], thr[:], fac[:], ALU.mult))
            tot = count(ALU.is_gt, thr[:])
            assert rounds[0] == ROUNDS
            step(v.tensor_scalar(room[:], tot, -1.0, float(CAP), ALU.mult, ALU.add))
            step(v.tensor_scalar(gtm[:], G[:], thr[:], None, ALU.is_gt))
            step(v.tensor_scalar(eqm[:], G[:], thr[:], None, ALU.is_equal))
            step(v.tensor_tensor_scan(pref[:], eqm[:], zrow[:], 0.0, ALU.add, ALU.add))
            v.tensor_copy(cnt[:, 1:2], pref[:, TT - 1:TT]).then_inc(S4["eqc"], 1)
            dve.wait_ge(S4["eqp"], 1 + PRIME)
            step(v.tensor_tensor(room[:], room[:], bank[6][:, 0:1], ALU.subtract))
            step(v.tensor_scalar(pref[:], pref[:], room[:], None, ALU.is_le))
            step(v.tensor_tensor(eqm[:], eqm[:], pref[:], ALU.mult))
            step(v.tensor_tensor(gtm[:], gtm[:], eqm[:], ALU.add))
            v.tensor_tensor(Gs[:], G[:], gtm[:], ALU.mult).then_inc(S4["gs"], 1)
            for n in range(low_parts(ROUNDS - 1).stop, FC * UNITS // 2):
                low_part(n // FC, n // FC, n % FC)

            def unit(u, k):
                for f in range(FC):
                    low_part(u, k, f)
                for a2 in range(2):
                    n = u * 2 + (a2 - UNITS)
                    dve.wait_ge(S4["gated"], n + 1 + PRIME)
                    dve.wait_ge(S4["acc"], n - (NQ - 1) + PRIME)
                    q = (2 * k + a2) % NQ
                    v.tensor_tensor(y_sum[:, q], y_sum[:, q], results[:, 2 * k + a2], ALU.add).then_inc(S4["acc"], 1)
            experts_after(dve, unit)
            for i in range(NQ // 2):
                dve.wait_ge(S4["xn"], 2 * i + PRIME)
                norm(tie_both(0), S4, i, quads3, lambda h: bank[2 * i + h][0:TT, :].rearrange("p (t d) -> p t d", t=QT),
                     lambda h: x2_all[:, QT * (2 * i + h):QT * (2 * i + h) + QT, :], lambda h, t: x2_all[:, QT * (2 * i + h) + t, :], "y2")

        @block.tensor
        def _(pe):
            t_ = nc.tensor
            mm = t_.matmul
            pe.wait_ge(weights, 16 * 12)
            pe.wait_ge(consts, 1)
            mm(bank[0][:, 0:128], w_sb["wq"][:], w_sb["wk"][:], start=True, stop=True)
            t_.transpose(bank[1][:, 0:128], w_sb["wv"][:], ident[:])
            for s in range(SLOTS):
                last = mm(bank[2][:, 128 * s:128 * s + 128], perm[:, s, :], w_sb["xWo"][:], start=True, stop=True)
            last.then_inc(w_ps, 1)
            pe.wait_ge(w_ev, 3)
            with pe.Fori(0, NQ // 2) as i:
                for h, q in enumerate(quads1):
                    n = i * 2 + h
                    pe.wait_ge(S1[X_OF[h]], (i + 1) * 16)
                    pe.wait_ge(S1["xT"], n + PRIME)
                    for t in range(QT):
                        last = t_.transpose(bank[0][:, TT * t:TT * t + TT], q.xq[:, t, :], ident[0:TT, 0:TT])
                    last.then_inc(S1["xTp"], 1)
                for h, q in enumerate(quads1):
                    n = i * 2 + h
                    pe.wait_ge(S1["xT"], n + 1 + PRIME)
                    pe.wait_ge(S1["u"], n + PRIME)
                    mm(bank[1][:, 0:QC], qk[:], q.xT, start=True, stop=True).then_inc(S1["up"], 1)
                    pe.wait_ge(S1["v"], n + PRIME)
                    for t in range(QT):
                        last = mm(bank[2][0:TT, D * t:D * t + D], q.xT[:, TT * t:TT * t + TT], wvT[:], start=True, stop=True)
                    last.then_inc(S1["vp"], 1)
                for h, q in enumerate(quads1):
                    n = i * 2 + h
                    pe.wait_ge(S1["u"], n + 1 + PRIME)
                    pe.wait_ge(S1["s"], n + PRIME)
                    for t in range(QT):
                        last = mm(bank[3][0:TT, TT * t:TT * t + TT], q.xT[:, TT * t:TT * t + TT], q.u[:, TT * t:TT * t + TT], start=True, stop=True)
                    last.then_inc(S1["sp"], 1)
                for h, q in enumerate(quads1):
                    n = i * 2 + h
                    pe.wait_ge(S1["a"], n + 1 + PRIME)
                    pe.wait_ge(S1["aT"], n + PRIME)
                    for t in range(QT):
                        last = t_.transpose(bank[4][0:TT, TT * t:TT * t + TT], q.s[:, t, :], ident[0:TT, 0:TT])
                    last.then_inc(S1["aTp"], 1)
                for h, q in enumerate(quads1):
                    n = i * 2 + h
                    pe.wait_ge(S1["v"], n + 1 + PRIME)
                    pe.wait_ge(S1["aT"], n + 1 + PRIME)
                    pe.wait_ge(S1["y"], n + PRIME)
                    for t in range(QT):
                        last = mm(bank[5][0:TT, D * t:D * t + D], q.aT[:, t, :], q.v[:, t, :], start=True, stop=True)
                    last.then_inc(S1["op"], 1)
                for h, q in enumerate(quads1):
                    n = i * 2 + h
                    pe.wait_ge(S1["xn"], n + 1 + PRIME)
                    pe.wait_ge(S1["xnT"], n + PRIME)
                    for t in range(QT):
                        last = t_.transpose(bank[6][:, TT * t:TT * t + TT], q.xn[:, t, :], ident[0:TT, 0:TT])
                    last.then_inc(S1["xnTp"], 1)
                for h, q in enumerate(quads1):
                    n = i * 2 + h
                    pe.wait_ge(S1["xnT"], n + 1 + PRIME)
                    pe.wait_ge(S1["x1"], n + 1 + PRIME)
                    pe.wait_ge(S1["q"], n + PRIME)
                    mm(bank[7][:, 0:QC], w_sb["xWq"][:], q.xT, start=True, stop=True).then_inc(S1["qp"], 1)
            pe.wait_ge(consts, 2)
            pe.wait_ge(S1["q"], NQ + PRIME)


            def period(b, par, half):
                for c in range(NC):
                    if has(b, 0):
                        if c == 0:
                            pe.wait_ge(D_[f"khi{par}"], (half + 1) * (16 * 2 * HG))
                            pe.wait_ge(D_[f"klo{par}"], (half + 1) * (16 * HG))
                            pe.wait_ge(D_["mrow"], (b + 1) * (16 * RG))
                            pe.wait_ge(F["qs"], b + 1 + PRIME)
                        if not (isinstance(b, int) and b == 0 and c < 2):
                            pe.wait_ge(F["e"], b * NC + (c - 1) + PRIME)
                        for g in range(HG):
                            last = mm(bank[2 + 2 * (c % 2) + g // 2][0:CK, 4 * S * (g % 2):4 * S * (g % 2) + 4 * S],
                                      K_st[0:DC + 1, par, g, c * CK:c * CK + CK], Q_st[:, par, g].rearrange("p h q -> p (h q)"), start=True, stop=True)
                        last.then_inc(F["bp"], 1)
                    if c < 3 and has(b, 2):
                        if c == 0:
                            pe.wait_ge(D_["c"], (b + 3) * 16)
                            if not isinstance(b, int) or b >= 0:
                                pe.wait_ge(F["v"], (b + 1) * NB + PRIME)
                            elif b == -1:
                                pe.wait_ge(F["k"], NB + PRIME)
                            else:
                                pe.wait_ge(F["ready"], 2 + PRIME)
                        else:
                            pe.wait_ge(F["cT"], b * NB + (2 * NB + c) + PRIME)
                        for k in range(4):
                            last = t_.transpose(bank[7][0:DC, CK * k:CK * k + CK], C2[:, 4 * c + k, :], ident[0:CK, 0:CK])
                        last.then_inc(F["cTp"], 1)
                    if 3 <= c < 6 and has(b, 2):
                        n = c - 3
                        if n == 0:
                            pe.wait_ge(F["cT"], b * NB + 3 * NB + PRIME)
                        else:
                            pe.wait_ge(F["k"], b * NB + (2 * NB + n) + PRIME)
                        mm(bank[7][:, 0:KB], WkA[:], ctxT2[:, par, n * KB:n * KB + KB], start=True, stop=True).then_inc(F["kp"], 1)
                    if c == 6 and has(b, -1):
                        pe.wait_ge(F["o"], b + PRIME)
                        if has(b, 2):
                            pe.wait_ge(F["k"], b * NB + 3 * NB + PRIME)
                        elif has(b, 0):
                            pe.wait_ge(F["v"], (b + 1) * NB + PRIME)
                        else:
                            pe.wait_ge(F["r"], 2 * (b - 1) + PRIME)
                        mm(bank[7][:, 0:SLOTS * S], sum_rows[:], O_sb, start=True, stop=True).then_inc(F["rp"], 1)
                    if c in V_SLOTS and has(b, 1):
                        n = V_SLOTS.index(c)
                        if n > 0:
                            pe.wait_ge(F["v"], b * NB + (NB + n) + PRIME)
                        elif has(b, -1):
                            pe.wait_ge(F["r"], 2 * b + PRIME)
                        elif has(b, 2):
                            pe.wait_ge(F["k"], b * NB + 3 * NB + PRIME)
                        for k in range(4):
                            q = 4 * n + k
                            last = mm(bank[7][0:CK, 128 * k:128 * k + 128], ctxT2[:, 1 - par, CK * q:CK * q + CK], WvA[:], start=True, stop=True)
                        last.then_inc(F["vp"], 1)
                    for ahead, n in pieces(c):
                        if not has(b, ahead):
                            if n == 1 and has(b, 1):
                                pe.wait_ge(F["mx"], b + 2 + PRIME)
                                mm(bank[1][0:RG, 0:128], m2x, ident[:], start=True, stop=True).then_inc(F["mTp"], 1)
                            continue
                        if n == 0:
                            pe.wait_ge(F["qa"], b + (ahead + 1) + PRIME)
                        if n < NB:
                            pe.wait_ge(F["khi"], b * NB + (ahead * NB + n + 1) + PRIME)
                        if n == 1:
                            if has(b, 1):
                                pe.wait_ge(F["mx"], b + 2 + PRIME)
                                mm(bank[1][0:RG, 0:128], m2x, ident[:], start=True, stop=True).then_inc(F["mTp"], 1)
                            pe.wait_ge(F["am"], b * AP_ + (ahead * AP_ + 1) + PRIME)
                        elif n == 2:
                            if has(b, 1):
                                pe.wait_ge(F["mr"], b + 2 + PRIME)
                        elif not (isinstance(b, int) and b + ahead == 0 and n == 0):
                            pe.wait_ge(F["am"], b * AP_ + (ahead * AP_ + n - 1) + PRIME)
                        p = (par + ahead) % 2
                        mm(bank_of(n)[:, 0:KB], Q_bd[:, p].rearrange("p h q -> p (h q)")[:, 128 * (n // NB):128 * (n // NB) + 128],
                           K_hi[:, p, (n % NB) * KB:(n % NB) * KB + KB], start=True, stop=True).then_inc(F["ap"], 1)
                    ago = -1 if c == 0 else 0
                    if has(b, ago):
                        k = (c - 1) % NC
                        if k == 0:
                            pe.wait_ge(F["v"], (b + 1) * NB + PRIME)
                            if not isinstance(b, int) or b >= 1:
                                pe.wait_ge(F["o"], b + PRIME)
                        pe.wait_ge(F["e"], b * NC + c + PRIME)
                        weights_, values = P2[k % 2], V2[(par + ago) % 2]
                        for m in range(4):
                            mm(bank[6][32 * m:32 * m + V3, 0:3 * S], values[:, k, V3 * m:V3 * m + V3], weights_[:, 3 * S * m:3 * S * m + 3 * S],
                               start=(k == 0), stop=(k == NC - 1), skip_group_check=True)
                        for m in range(4):
                            last = mm(bank[6][32 * m:32 * m + V1, 3 * S:4 * S], values[:, k, 4 * V3 + V1 * m:4 * V3 + V1 * m + V1],
                                      weights_[:, (12 + m) * S:(13 + m) * S], start=False, stop=(k == NC - 1), skip_group_check=True)
                        last.then_inc(F["pv"], 1)
            periods(pe, period)
            pe.wait_ge(F["bad"], 1 + PRIME)
            mm(bank[0][:, 0:1], ones[:], bad[:, 0:1], start=True, stop=True).then_inc(F["sum"], 1)
            pe.wait_ge(F["flag"], 1 + PRIME)
            clamped = pe.value_load(flag_int[0:1, 0:1], min_val=0, max_val=1)
            with pe.If(clamped > 0):
                with pe.Fori(0, B) as i:
                    pe.wait_ge(S2["c"], (i + 1) * 16)
                    pe.wait_ge(S2["qbd"], i + 1 + PRIME)
                    pe.wait_ge(S2["m"], i * G2 + PRIME)
                    for c in range(NC):
                        last = t_.transpose(bank[c // 4][0:DC, CK * (c % 4):CK * (c % 4) + CK], C[:, c, :], ident[0:CK, 0:CK])
                    last.then_inc(S2["cTp"], 1)
                    pe.wait_ge(S2["cT"], i * NB + NB + PRIME)
                    for n in range(NB):
                        last = mm(bank[n][:, 0:KB], WkA[:], ctxT[:, KB * n:KB * n + KB], start=True, stop=True)
                    last.then_inc(S2["kp"], 1)
                    pe.wait_ge(S2["pT"], i * (G2 * NB) + PRIME)
                    for c in range(NC):
                        last = mm(bank[3 + c // 4][0:CK, 128 * (c % 4):128 * (c % 4) + 128], ctxT[:, CK * c:CK * c + CK], WvA[:], start=True, stop=True)
                    last.then_inc(S2["vp"], 1)
                    pe.wait_ge(S2["k"], i * NB + NB + PRIME)
                    pe.wait_ge(S2["v"], i * NB + NB + PRIME)
                    pe.wait_ge(S2["qbd"], i + 1 + PRIME)
                    for j in range(G2):
                        n = i * G2 + j
                        pe.wait_ge(S2["m"], n + PRIME)
                        for c in range(NB):
                            last = mm(bank[c][0:TT, 0:KB], Qbd[:, 2 * j:2 * j + 2, :].rearrange("p h q -> p (h q)"), KT[:, KB * c:KB * c + KB],
                                      start=True, stop=True)
                        last.then_inc(S2["sp"], 1)
                        pe.wait_ge(S2["e"], n + 1 + PRIME)
                        pe.wait_ge(S2["pT"], n * NB + PRIME)
                        for c in range(NC):
                            last = t_.transpose(bank[3 + c // 4][0:CK, TT * (c % 4):TT * (c % 4) + TT], P[:, CK * c:CK * c + CK], ident[0:TT, 0:TT])
                        last.then_inc(S2["pTp"], 1)
                        pe.wait_ge(S2["pT"], n * NB + NB + PRIME)
                        pe.wait_ge(S2["om"], n + PRIME)
                        if j == 0:
                            pe.wait_ge(S2["os"], i * 2 + PRIME)
                        for c in range(NC):
                            last = mm(bank[6][0:TT, 0:16], PT[:, c, :], V[:, c, 16 * j:16 * j + 16], start=(c == 0), stop=(c == NC - 1))
                        last.then_inc(S2["op"], 1)
                    pe.wait_ge(S2["om"], i * G2 + G2 + PRIME)
                    mm(bank[7][:, 0:S], Om[:], fold_q[:], start=True, stop=True)
                    for c in range(NC):
                        last = mm(bank[7][:, S:2 * S], V[:, c, :], ones[0:CK, 0:S], start=(c == 0), stop=(c == NC - 1))
                    last.then_inc(S2["otp"], 1)
                    pe.wait_ge(S2["ot"], i + 1 + PRIME)
                    for a in range(2):
                        for s in range(SLOTS):
                            o = (a * SLOTS + s) * S
                            last = mm(bank[6][:, o:o + S], perm[:, s, :], OT[:, a, :], start=True, stop=True)
                    last.then_inc(S2["osp"], 1)
                pe.wait_ge(S2["nanrow"], 1 + PRIME)
                mm(bank[0][:, 0:1], ones[0:TT, :], nan_mask[:], start=True, stop=True).then_inc(S2["nanall"], 1)

            with pe.Fori(0, NQ // 2) as i:
                for h in range(2):
                    n = i * 2 + h
                    pe.wait_ge(S3["osq"], n + 1 + PRIME)
                    pe.wait_ge(S3["y"], n + PRIME)
                    for t in range(QT):
                        for s in range(SLOTS):
                            mm(bank[5][0:TT, D * t:D * t + D], OSq[h][:, s, TT * t:TT * t + TT], WoP[:, s, :], start=(s == 0), stop=False)
                        last = mm(bank[5][0:TT, D * t:D * t + D], ones[0:1, 0:TT], bo_row[:], start=False, stop=True)
                    last.then_inc(S3["op"], 1)
                for h, q in enumerate(quads3):
                    n = i * 2 + h
                    pe.wait_ge(S3["xn"], n + 1 + PRIME)
                    pe.wait_ge(S3["xnT"], n + PRIME)
                    for t in range(QT):
                        last = t_.transpose(bank[6][:, TT * t:TT * t + TT], q.xn[:, t, :], ident[0:TT, 0:TT])
                    last.then_inc(S3["xnTp"], 1)
            pe.wait_ge(S3["xnT"], NQ + PRIME)
            for t in range(NT):
                last = mm(bank[7][0:TT, NE * t:NE * t + NE], x2T[:, TT * t:TT * t + TT], Wr_sb[:], start=True, stop=True)
            last.then_inc(S4["lg"], 1)
            pe.wait_ge(S4["g"], 1 + PRIME)
            t_.transpose(bank[7][:, 0:TT], gsel[:].rearrange("p e t -> p (e t)"), ident[0:TT, 0:TT]).then_inc(S4["gTp"], 1)

            def up(u, k, f, p):
                if k % NQ == 0 and f == 0:
                    pe.wait_ge(S4["w_split"], p[1] + 1 + PRIME)
                pe.wait_ge(S4["lo"], u * FC + (f - 3) + PRIME)
                cols = slice(QC * (k % NQ), QC * (k % NQ) + QC)
                w_cols = slice(128 * f, 128 * f + 128)
                mm(bank[f][:, 0:QC], w1_hi[p[0]][:, w_cols], x_hi[:, cols], start=True, stop=False)
                mm(bank[f][:, 0:QC], w1_hi[p[0]][:, w_cols], x_lo[:, cols], start=False, stop=False)
                mm(bank[f][:, 0:QC], w1_lo[p[0]][:, w_cols], x_hi[:, cols], start=False, stop=True).then_inc(S4["up"], 1)

            def down(u, k, f, p):
                if f == 0:
                    pe.wait_ge(S4["y"], u - 1 + PRIME)
                pe.wait_ge(S4["lo"], u * FC + (f + 1) + PRIME)
                dst = bank[4 + k % 2][:, 0:QC]
                mm(dst, w2_hi[p][:, f], h_hi[k % 2][:, f], start=(f == 0), stop=False)
                mm(dst, w2_hi[p][:, f], h_lo[k % 2][:, f], start=False, stop=False)
                last = mm(dst, w2_lo[p][:, f], h_hi[k % 2][:, f], start=False, stop=(f == FC - 1))
                if f == FC - 1:
                    last.then_inc(S4["dn"], 1)
            pe.wait_ge(S4["x_lo"], NQ + PRIME)
            rounds = 0
            for u in range(UNITS // 2):
                for f in range(FC):
                    while rounds < ROUNDS and low_parts(rounds).stop <= u * FC + f:
                        pe.wait_ge(S4["cnt"], rounds + 1 + PRIME)
                        mm(bank[6][:, 0:1], expert_rows[:], cnt[:, 0:1], start=True, stop=True).then_inc(S4["tot"], 1)
                        rounds += 1
                    up(u, u, f, ((u // NQ) % 2, u // NQ))
                    if u:
                        down(u - 1, u - 1, f, ((u - 1) // NQ) % 2)
                    if rounds == ROUNDS and u * FC + f == low_parts(ROUNDS - 1).stop + 3:
                        pe.wait_ge(S4["eqc"], 1 + PRIME)
                        mm(bank[6][:, 0:1], before_rows[:], cnt[:, 1:2], start=True, stop=True).then_inc(S4["eqp"], 1)
            with pe.Fori(0, NE // 4) as i:
                for k in range(2 * NQ):
                    u = i * (2 * NQ) + (UNITS // 2 + k)
                    for f in range(FC):
                        up(u, k, f, (k // NQ, i * 2 + (NE // 2 + k // NQ)))
                        down(u - 1, k - 1, f, ((k - 1) // NQ) % 2)
            for f in range(FC):
                down(UNITS - 1, UNITS - 1, f, 1)
            for n in range(NQ):
                pe.wait_ge(S4["acc"], UNITS - NQ + n + 1 + PRIME)
                for t in range(QT):
                    last = t_.transpose(bank[n][0:TT, D * t:D * t + D], y_sum[:, n, TT * t:TT * t + TT], ident[:])
                last.then_inc(S4["op"], 1)


def low_parts(r):
    per = (52, ROUNDS)
    return range(r * per[0] // per[1], (r + 1) * per[0] // per[1])


def flat(t):
    return t[:].rearrange("p t e -> p (t e)")


def view3(t, cols):
    return t[:].rearrange("p (n k) -> p n k", k=cols)



_INS = ["x", "ctx_768", "L0_attn_wq", "L0_attn_wk", "L0_attn_wv", "L0_xattn_Wq", "L0_xattn_bq", "L0_xattn_Wk",
        "L0_xattn_bk", "L0_xattn_Wv", "L0_xattn_bv", "L0_xattn_Wo", "L0_xattn_bo", "L0_ffn_Wr", "L0_ffn_W1", "L0_ffn_W2"]


def kernel(**inputs):
    import numpy as np
    import concourse.bacc as bacc
    from concourse.bass_utils import run_bass_kernel_spmd

    nc = bacc.Bacc("TRN2", target_bir_lowering=False, num_devices=1)
    arrays, args = {}, []
    for name in _INS:
        a = np.ascontiguousarray(inputs[name])
        arrays[f"in_{name}"] = a
        args.append(nc.dram_tensor(f"in_{name}", a.shape, mybir.dt.from_np(a.dtype), kind="ExternalInput").ap())
    out = nc.dram_tensor("out", (B, S, D), F32, kind="ExternalOutput").ap()
    gate_rows = nc.dram_tensor("gate_rows", (NE, B * S), F32, kind="Internal").ap()
    decoder_kernel(nc, gate_rows, *args, out)
    r = run_bass_kernel_spmd(nc, [arrays], core_ids=[0])
    return r.results[0]["out"]
```

```python
import math
from collections import namedtuple
from itertools import islice
from contextlib import ExitStack

import concourse.bass as bass
from concourse import mybir

F32 = mybir.dt.float32
F32R = mybir.dt.float32r
I32 = mybir.dt.int32
ALU = mybir.AluOpType
ACT = mybir.ActivationFunctionType
AX = mybir.AxisListType

B, S, D = 32, 56, 128
NK, DC = 1500, 96
H, DH = 16, 8
NE, FF, TOPK = 8, 512, 2
CAP = max(math.ceil(B * S * TOPK * 1.25 / NE), 1)
EPS, CLAMP = 1e-5, 10000.0
TT = 2 * S
NT = B // 2
QT = 4
NQ = NT // QT
QC = QT * TT
CK = 125
NC = NK // CK
KB = 500
NB = NK // KB
G2 = H // 2
UNITS = NE * NQ
ROUNDS = 7 + 23 + 2
EARLY, BETWEEN = 10, 46
FIRST_CONTEXT, FIRST_KEYS = (2, 3, 0), (2, 3, 5)
V_SLOTS = (9, 10, 11)
SLOTS = 4
FC = FF // 128
NEG = -3.0e38
HQ = H * S
RG = HQ // 128
HG = H // 4
PIECES = RG * NB
SUM = 0
V3, V1 = 3 * DH + 1, DH + 1
VC = 4 * (V3 + V1)
PLAIN = 9000.0
ARENA = 19700
PRIME = 4


Quad = namedtuple("Quad", "xq xT u v s e aT nm rs ri y stats mv ve rstd pad")


def decoder_kernel(nc, gate_rows, x, ctx_in, wq, wk, wv, xWq, xbq, xWk, xbk, xWv, xbv, xWo, xbo, Wr, W1, W2, out):
    stack = ExitStack()

    def sb(name, shape, dt=F32):
        return stack.enter_context(nc.sbuf_tensor(name, shape, dt))

    def sem(name):
        return stack.enter_context(nc.semaphore(name))

    with stack:
        psum = stack.enter_context(nc.psum_tensor("psum", [128, 8, 512], F32))
        bank = [psum[:, i, :] for i in range(8)]
        ident = sb("ident", [128, 128])
        other_batch = sb("other_batch", [TT, TT])
        causal = sb("causal", [TT, TT])
        head_rows = sb("head_rows", [128, H])
        pair_rows = sb("pair_rows", [TT, 2])
        fold_q = sb("fold_q", [TT, S])
        expert_rows = sb("expert_rows", [128, 128])
        before_rows = sb("before_rows", [128, 128])
        ones = sb("ones", [128, 128])
        minus_half = sb("minus_half", [128, QT])
        index_prio = sb("index_prio", [TT, NE])
        perm = sb("perm", [128, SLOTS, 128])
        w_sb = {n: sb(n + "_sb", [128, 128]) for n in ("wq", "wk", "wv", "xWq", "xWo")}
        qk = sb("qk", [128, 128])
        wvT = sb("wvT", [128, 128])
        bq_col = sb("bq_col", [128, 1])
        WkA = sb("WkA", [DC + 1, 128])
        WvA = sb("WvA", [DC + 1, 128])
        WoP = sb("WoP", [128, SLOTS, 128])
        bo_row = sb("bo_row", [1, 128])
        Wr_sb = sb("Wr_sb", [128, NE])
        x1_all = sb("x1_all", [TT, NT, D])
        x2_all = x1_all
        Qt_all = sb("Qt_all", [128, B * S])
        OS_all = sb("OS_all", [128, SLOTS, B * S])
        K_hi = sb("K_hi", [128, 2, NK], F32R)
        K_st = sb("K_st", [128, 2, HG, NK], F32R)
        Q_st = sb("Q_st", [DC + 1, 2, HG, 4, S], F32R)
        Q_bd = sb("Q_bd", [128, 2, H, S], F32R)
        max_row = sb("max_row", [RG, 128], F32R)
        four_heads = sb("four_heads", [DC, 4])
        sum_rows = sb("sum_rows", [128, 128])
        sum_row = sb("sum_row", [128, 1])
        arena = sb("arena", [128, ARENA])
        used = [0]
        whole = arena[:]

        def at(parts, *shape, place=None):
            n = math.prod(shape)
            o = used[0]
            used[0] += n
            place = whole if place is None else place
            assert used[0] <= place.shape[-1], used[0]
            v = place[0:parts, o:o + n]
            if len(shape) == 2:
                v = v.rearrange("p (a b) -> p a b", b=shape[1])
            elif len(shape) == 3:
                v = v.rearrange("p (a b c) -> p a b c", b=shape[1], c=shape[2])
            return v

        Qs_all = at(DC, HG, B * S)
        start = used[0]

        def quad_buffers(first, second):
            a, b = lambda *shape: at(*shape, place=first), lambda *shape: at(*shape, place=second)
            used[0] = len_of[id(first)]
            big = dict(xq=a(TT, QT, D), xT=a(128, QC), u=a(128, QC), v=a(TT, QT, D), s=a(TT, QT, TT), e=a(TT, QT, TT))
            len_of[id(first)], used[0] = used[0], len_of[id(second)] if second is not first else used[0]
            small = dict(aT=b(TT, QT, TT), nm=b(TT, QT), rs=b(TT, QT), ri=b(TT, QT), y=b(TT, QT, D),
                         stats=b(TT, QT, 6), mv=b(TT, QT, 2), ve=b(TT, QT), rstd=b(TT, QT), pad=b(1, 1))
            len_of[id(second)] = used[0]
            return Quad(**big, **small)
        outputs_place = OS_all[:].rearrange("p s n -> p (s n)")
        queries_place = arena[:, 0:start]
        rest_place = arena[:, start:ARENA]
        len_of = {id(outputs_place): 0, id(queries_place): 0, id(rest_place): 0}
        quads1 = [quad_buffers(p, r) for p, r in ((rest_place, queries_place), (outputs_place, outputs_place),
                                                  (queries_place, queries_place), (outputs_place, queries_place))]
        after1 = start + len_of[id(rest_place)]
        used[0] = start
        quads3 = [Quad(*[None] * 10, y=at(TT, QT, D), stats=at(TT, QT, 6), mv=at(TT, QT, 2),
                       ve=at(TT, QT), rstd=at(TT, QT), pad=at(1, 1)) for _ in range(NQ)]
        gates = [at(128, NQ, QC) for _ in range(2)]
        used[0] = 0
        results = at(128, UNITS // 2, QC, place=outputs_place)
        y_sum = Qt_all[:].rearrange("p (q n) -> p q n", q=NQ)
        x_hi = K_hi[:].rearrange("p a k -> p (a k)")[:, 0:B * S]
        x_lo = Q_bd[:].rearrange("p a h q -> p (a h q)")
        used[0] = 0
        expert_place = K_st[:].rearrange("p a g k -> p (a g k)")
        h_hi, h_lo = [[at(128, FC, QC, place=expert_place) for _ in range(2)] for _ in range(2)]
        w1_hi, w1_lo = [[at(128, FF, place=expert_place) for _ in range(2)] for _ in range(2)]
        w2_hi, w2_lo = [[at(128, FC, 128, place=expert_place) for _ in range(2)] for _ in range(2)]
        Q_hi, Q_lo = [K_st[:, 1].rearrange("p g k -> p (g k)")[:, a:a + B * S] for a in (0, B * S)]
        used[0] = start
        P2 = [at(CK, HQ) for _ in range(2)]
        O_sb = at(128, SLOTS * S)
        R_sb = at(128, SLOTS * S)
        mx = at(128, RG, NB)
        used[0] = max(used[0], after1)
        K_lo = at(128, NK)
        C2 = at(CK, NC, DC)
        ctxT2 = at(DC + 1, 2, NK)
        V2 = [at(CK, NC, VC) for _ in range(2)]
        m2x = at(128, RG)
        m_high = at(128, RG)
        m_low = at(128, RG)
        chk = at(128, 1)
        chk_sum = at(128, 1)
        bad = at(128, 2)
        used[0] = start
        C = at(CK, NC, DC)
        ctxT = at(DC + 1, NK)
        KT = at(128, NK)
        V = at(CK, NC, 128)
        Qbd = at(128, H, S)
        Sc = at(TT, NK)
        P = at(TT, NK)
        PT = at(CK, NC, TT)
        Om = at(TT, 128)
        OT = at(128, 2, S)
        c1 = at(TT, 1)
        c2 = at(TT, 1)
        rowmax = at(TT, 1)
        negmax = at(TT, 1)
        rowsum = at(TT, 1)
        rinv = at(TT, 1)
        numbers = at(TT, 1)
        nan_mask = at(TT, 1)
        nan_col = at(128, 1)
        nan_int = at(128, 1).bitcast(I32)
        OM_all = at(128, SLOTS, B)
        used[0] = 0
        x2T = at(128, NT * TT)
        pr = at(TT, NT, NE)
        pw = at(TT, NT, NE)
        eq = at(TT, NT, NE)
        hot = at(TT, NT, NE)
        mask = at(TT, NT, NE)
        m1 = at(TT, NT)
        m2 = at(TT, NT)
        gsel = at(TT, NE, NT)
        G = at(128, TT)
        gscr = at(128, TT)
        gtm = at(128, TT)
        eqm = at(128, TT)
        pref = at(128, TT)
        cand = at(128, 1)
        fac = at(128, 1)
        cnt = at(128, 2)
        room = at(128, 1)
        Gs = at(128, TT)
        w1 = at(128, 2, FF)
        w2 = at(128, 2, FC, 128)
        assert used[0] <= start, used[0]
        flag_int = sb("flag_int", [1, 1], I32)
        zeros = sb("zeros", [128, TT])
        thr = sb("thr", [128, 1])
        halves = sb("halves", [128, 23])
        bits = sb("bits", [128, 23])

        dve_step = sem("dve_step")
        clamp_step = sem("clamp_step")
        pool_step = sem("pool_step")
        consts = sem("consts")
        weights = sem("weights")
        more_weights = sem("more_weights")
        w_ps = sem("w_ps")
        w_ev = sem("w_ev")

        S1 = {n: sem("s1_" + n) for n in (
            "scores_scaled", "queries_split", "x_transposed", "x_copied", "u_made", "u_copied",
            "values_made", "values_copied", "scores_made", "max_subtracted", "exp_done", "weights_done",
            "weights_transposed", "weights_copied", "outputs_made", "residual_added", "variance_ready",
            "rstd_ready", "normed", "normed_transposed", "normed_copied", "queries_made", "queries_copied")}
        S2 = {n: sem("s2_" + n) for n in (
            "context_loaded", "context_transposed", "context_copied", "keys_made", "keys_copied",
            "values_made", "values_copied", "queries_spread", "scores_made", "max_ready", "weights_ready",
            "weights_transposed", "weights_copied", "outputs_made", "outputs_masked", "outputs_transposed",
            "transposed_copied", "outputs_placed", "outputs_stored", "nan_rows", "nan_summed", "nan_fixed")}
        S3 = {n: sem("s3_" + n) for n in (
            "attended", "outputs_made", "residual_added", "variance_ready", "rstd_ready", "normed",
            "normed_transposed", "normed_copied")}
        S4 = {n: sem("s4_" + n) for n in (
            "x_split", "logits_made", "logits_shifted", "exp_done", "gates_ready", "gates_transposed",
            "counted", "total_made", "equal_counted", "equal_before_made", "gates_final", "weights_high",
            "weights_split", "hidden_made", "hidden_high", "hidden_low", "result_made", "result_copied",
            "result_gated", "result_added", "outputs_made", "residual_added", "variance_ready", "rstd_ready",
            "normed")}
        W_ = [sem(f"w_{p}") for p in range(2)]
        G_ = [sem(f"g_{p}") for p in range(2)]
        g_out, out_done = sem("g_out"), sem("out_done")

        F = {n: sem("f_" + n) for n in (
            "context_transposed", "context_copied", "keys_made", "keys_copied", "keys_high", "keys_low",
            "values_made", "values_copied", "queries_spread", "stacked_spread", "max_scores_made",
            "piece_max_taken", "row_max_taken", "extremes_kept", "max_transposed", "max_row_ready",
            "scores_made", "weights_ready", "outputs_made", "outputs_copied", "sums_spread", "sums_inverted",
            "outputs_scaled", "check_added", "ones_ready", "bank_cleared", "bad_ready", "bad_summed",
            "flag_ready")}
        X_ = [sem(f"x_{n}") for n in range(NQ)]
        D_ = {n: sem("d_" + n) for n in ("c", "khi0", "khi1", "klo0", "klo1", "mrow", "q")}
        primed = [s_ for d in (S1, S2, S3, S4) for n, s_ in d.items() if n != "context_loaded"] + list(F.values())

        def periods(eng, period):
            for b in range(-2, 2):
                period(b, b % 2, b // 2)
            with eng.Fori(1, B // 2 - 2) as i:
                for par in range(2):
                    period(i * 2 + par, par, i)
            for b in range(B - 4, B + 1):
                period(b, b % 2, b // 2)

        def pieces(c):
            if c < 6:
                return [(1, 9 + 2 * c), (1, 10 + 2 * c)]
            return [(2, n) for n in {6: (0,), 7: (1,), 8: (2, 3), 9: (4,), 10: (5, 6), 11: (7, 8)}[c]]

        def bank_of(n):
            return bank[(n + 1 if 1 <= n < 9 else n + 1 if n >= 9 else 0) % 2]

        def experts_after(eng, unit):
            with eng.Fori(0, NE // 4) as i:
                for k in range(2 * NQ):
                    unit(i * (2 * NQ) + (UNITS // 2 + k), k)

        def has(b, ahead):
            return not isinstance(b, int) or 0 <= b + ahead < B

        block = stack.enter_context(nc.Block())

        @block.sync
        def _(sp):
            for t, src in ((w_sb["wq"], wq), (w_sb["wk"], wk), (w_sb["wv"], wv), (w_sb["xWo"], xWo)):
                sp.dma_start(t[:], src).then_inc(weights, 16)
            xv = x.rearrange("(n t b) s d -> n (b s) t d", t=QT, b=2)
            for n in range(NQ):
                sp.dma_start(quads1[n].xq, xv[n]).then_inc(X_[n], 16)
            cv = ctx_in.rearrange("b (p c) d -> b p c d", c=NC)

            def load_context(b):
                sp.dma_start(C2, cv[bass.ds(b, 1), :, :, :].rearrange("a p c d -> (a p) c d")).then_inc(D_["c"], 16)
            load_context(0)
            for t, src in ((bq_col[:], xbq.rearrange("(p a) -> p a", a=1)), (w_sb["xWq"][:], xWq),
                           (WkA[0:DC, :], xWk), (WkA[DC:DC + 1, :], xbk.rearrange("(a p) -> a p", a=1)),
                           (WvA[0:DC, :], xWv), (WvA[DC:DC + 1, :], xbv.rearrange("(a p) -> a p", a=1)),
                           (bo_row[:], xbo.rearrange("(a p) -> a p", a=1)), (Wr_sb[:], Wr)):
                sp.dma_start(t, src).then_inc(more_weights, 16)
            for s_ in primed:
                sp.sem_inc(s_, PRIME)

            sp.wait_ge(F["context_transposed"], NB + PRIME)
            load_context(1)
            sp.wait_ge(S1["queries_split"], NQ + PRIME)
            for q, part in enumerate((Q_hi, Q_lo, Q_hi)):
                for g in range(HG):
                    sp.dma_start(Qs_all[32 * q:32 * q + 32, g, :], part[32 * g:32 * g + 32, :].bitcast(F32)).then_inc(D_["q"], 16)

            def period(b, par, half):
                if has(b, 1):
                    sp.wait_ge(F["keys_low"], (b + 2) * NB + PRIME)
                    if not isinstance(b, int) or b >= 1:
                        sp.wait_ge(F["scores_made"], b * NC + PRIME)
                    for q, part in ((2, K_lo), (0, K_hi[:, 1 - par]), (1, K_hi[:, 1 - par])):
                        for g in range(HG):
                            sp.dma_start(K_st[32 * q:32 * q + 32, 1 - par, g, :].bitcast(F32), part[32 * g:32 * g + 32, :].bitcast(F32))\
                              .then_inc(D_[f"{'klo' if q == 2 else 'khi'}{1 - par}"], 16)
                if has(b, 3) and not (isinstance(b, int) and b == -2):
                    sp.wait_ge(F["context_transposed"], (b + 3) * NB + PRIME)
                    load_context(b + 3)
                if has(b, 1):
                    sp.wait_ge(F["max_row_ready"], b + 2 + PRIME)
                    last_row = Q_st[DC:DC + 1, 1 - par].rearrange("a g h q -> a (g h q)")
                    for j in range(RG):
                        sp.dma_start(last_row[:, 128 * j:128 * j + 128].bitcast(F32), max_row[j:j + 1, :].bitcast(F32)).then_inc(D_["mrow"], 16)
            periods(sp, period)
            sp.wait_ge(F["flag_ready"], 1 + PRIME)
            clamped = sp.value_load(flag_int[0:1, 0:1], min_val=0, max_val=1)
            with sp.If(clamped > 0), sp.Fori(0, B) as i:
                sp.wait_ge(S2["context_transposed"], i + PRIME)
                sp.dma_start(C[:], cv[bass.ds(i, 1), :, :, :].rearrange("a p c d -> (a p) c d")).then_inc(S2["context_loaded"], 16)
            def load_weights(e, p):
                sp.wait_ge(S4["weights_split"], e - 1 + PRIME)
                sp.dma_start(w1[:, p], W1[bass.ds(e, 1)].rearrange("a p f -> (a p) f")).then_inc(W_[p], 16)
                sp.dma_start(w2[:, p], W2[bass.ds(e, 1)].rearrange("a (c p) d -> (a p) c d", p=128)).then_inc(W_[p], 16)

            def load_gates(e, p):
                if e >= 2:
                    sp.wait_ge(S4["result_gated"], e * NQ - NQ + PRIME)
                sp.dma_start(gates[p].rearrange("p q n -> p (q n)"), gate_rows[bass.ds(e, 1), :].to_broadcast([128, B * S])).then_inc(G_[p], 16)
            for e in range(NE - 2):
                load_weights(e, e % 2)
            sp.wait_ge(S4["gates_final"], 1 + PRIME)
            sp.dma_start(gate_rows.rearrange("e (t n) -> (e t) n", n=TT), Gs).then_inc(g_out, 16)
            sp.wait_ge(g_out, 16)
            for e in range(NE):
                load_gates(e, e % 2)
                if e in (1, 2):
                    load_weights(NE - 3 + e, (NE - 3 + e) % 2)
            ov = out.rearrange("(n t b) s d -> n (b s) t d", t=QT, b=2)
            for n in range(NQ):
                sp.wait_ge(S4["normed"], n + 1 + PRIME)
                sp.dma_start(ov[n], x2_all[:, QT * n:QT * n + QT, :]).then_inc(out_done, 16)
            sp.wait_ge(out_done, 16 * NQ)

        @block.gpsimd
        def _(pool):
            g = nc.gpsimd
            ended = [0]

            def step(ins):
                ended[0] += 1
                ins.then_inc(pool_step, 1)
                pool.wait_ge(pool_step, ended[0])

            def keep(t, pattern, base, mult, op=ALU.is_ge, fill=0.0):
                step(g.affine_select(out=t, in_=t, pattern=pattern, compare_op=op, fill=fill, base=base,
                                     channel_multiplier=mult))

            for t, v in ((ident, 0.0), (perm, 0.0)):
                step(g.memset(t[:], v))
            keep(ident[:], [[-1, 128]], 0, 1, ALU.not_equal, 1.0)
            for s in range(SLOTS - 1):
                step(g.tensor_copy(perm[:, s, :].rearrange("p (g c) -> p g c", c=32)[:, :, 1 + DH * s:1 + DH * s + DH],
                                   ident[:, 0:96].rearrange("p (g c) -> p g c", c=24)[:, :, DH * s:DH * s + DH]))
            g.tensor_copy(perm[:, 3, :].rearrange("p (g c) -> p g c", c=32)[:, :, 1:V1],
                          ident[:, 96:128].rearrange("p (g c) -> p g c", c=DH)).then_inc(consts, 1)
            for t, v in ((other_batch, 0.0), (causal, 1.0), (head_rows, 1.0), (pair_rows, 1.0), (fold_q, 0.0),
                         (expert_rows, 1.0), (before_rows, 1.0), (ones, 1.0), (minus_half, -0.5), (zeros, 0.0),
                         (sum_rows, 0.0), (sum_row, 0.0), (thr, 1.0)):
                step(g.memset(t[:], v))
            keep(other_batch[:, 0:S], [[0, S]], S - 1, -1, fill=NEG)
            keep(other_batch[:, S:TT], [[0, S]], -S, 1, fill=NEG)
            keep(causal[:], [[-1, TT]], 0, 1)
            keep(causal[:, 0:S], [[0, S]], S - 1, -1)
            keep(head_rows[:], [[-DH, H]], 0, 1)
            keep(head_rows[:], [[DH, H]], DH - 1, -1)
            keep(pair_rows[:, 0:1], [[0, 1]], S - 1, -1)
            keep(pair_rows[:, 1:2], [[0, 1]], -S, 1)
            keep(fold_q[:], [[-1, S]], 0, 1, ALU.not_equal, 1.0)
            keep(fold_q[:], [[-1, S]], -S, 1, ALU.not_equal, 1.0)
            ev = expert_rows[:].rearrange("p (e s) -> p e s", s=NT)
            keep(ev, [[-NT, NE], [0, NT]], 0, 1)
            keep(ev, [[NT, NE], [0, NT]], NT - 1, -1)
            bv = before_rows[:].rearrange("p (e s) -> p e s", s=NT)
            keep(bv, [[-NT, NE], [0, NT]], 0, 1)
            keep(bv, [[NT, NE], [1, NT]], -1, -1)
            for s in range(23):
                step(g.memset(halves[:, s:s + 1], 0.5 ** (s + 1)))
            for e in range(NE):
                step(g.memset(index_prio[:, e:e + 1], float(NE - e)))
            keep(sum_rows[:].rearrange("p (g c) -> p g c", c=32), [[-32, 4], [0, 32]], -SUM, 1, ALU.not_equal, 1.0)
            for g4 in range(4):
                keep(sum_row[:], [[0, 1]], -SUM - 32 * g4, 1, ALU.not_equal, 1.0)
            for a3 in range(3):
                step(g.tensor_copy(four_heads[32 * a3:32 * a3 + 32, :], head_rows[32 * a3:32 * a3 + 32, 4 * a3:4 * a3 + 4]))
            pool.sem_inc(consts, 1)
            for par in range(2):
                step(g.memset(V2[par][:, :, 0:4 * V3].rearrange("p c (m r) -> p c m r", r=V3)[:, :, :, SUM], 1.0))
                step(g.memset(V2[par][:, :, 4 * V3:VC].rearrange("p c (m r) -> p c m r", r=V1)[:, :, :, SUM], 1.0))
            step(g.memset(ctxT2[DC:DC + 1], 1.0))
            pool.sem_inc(F["ones_ready"], 1)
            step(g.memset(K_st[DC:DC + 1, 0].rearrange("p g k -> p (g k)").bitcast(F32), 1.0))

            def low_keys(b, par):
                for n in range(NB):
                    pool.wait_ge(F["keys_high"], b * NB + (2 * NB + n + 1) + PRIME)
                    low = K_lo[:, n * KB:n * KB + KB]
                    g.tensor_tensor(low.bitcast(F32R), low, K_hi[:, par, n * KB:n * KB + KB].bitcast(F32), ALU.subtract).then_inc(F["keys_low"], 1)
            low_keys(-2, 0)
            for n, q in enumerate(quads1):
                pool.wait_ge(S1["variance_ready"], n + 1 + PRIME)
                g.tensor_tensor(q.rstd, q.ve, minus_half[0:TT], ALU.pow).then_inc(S1["rstd_ready"], 1)
            pool.wait_ge(S1["queries_copied"], 1 + PRIME)

            def period(b, par, half):
                if has(b, 2):
                    if not isinstance(b, int) or b >= 0:
                        pool.wait_ge(F["max_scores_made"], (b + 1) * PIECES + PRIME)
                    g.tensor_tensor(Q_bd[:, par], Qt_all[:, bass.ds((b + 2) * S, S)].unsqueeze(1).to_broadcast([128, H, S]),
                                    head_rows[:].unsqueeze(2).to_broadcast([128, H, S]), ALU.mult).then_inc(F["queries_spread"], 1)
                if has(b, 1):
                    if not isinstance(b, int) or b >= 1:
                        pool.wait_ge(F["scores_made"], b * NC + PRIME)
                    elif b == -1:
                        pool.wait_ge(D_["q"], 16 * 3 * HG)
                    g.tensor_tensor(Q_st[0:DC, 1 - par], Qs_all[:, :, bass.ds((b + 1) * S, S)].unsqueeze(2).to_broadcast([DC, HG, 4, S]),
                                    four_heads[:].unsqueeze(1).unsqueeze(3).to_broadcast([DC, HG, 4, S]), ALU.mult).then_inc(F["stacked_spread"], 1)
                if has(b, 2) and not (isinstance(b, int) and b == -2):
                    low_keys(b, par)
                if isinstance(b, int) and b == -1:
                    pool.wait_ge(F["keys_low"], 2 * NB + PRIME)
                    step(g.memset(K_st[DC:DC + 1, 1].rearrange("p g k -> p (g k)").bitcast(F32), 1.0))
            periods(pool, period)
            pool.wait_ge(F["flag_ready"], 1 + PRIME)
            for n, q in enumerate(quads3):
                pool.wait_ge(S3["variance_ready"], n + 1 + PRIME)
                g.tensor_tensor(q.rstd, q.ve, minus_half[0:TT], ALU.pow).then_inc(S3["rstd_ready"], 1)
            for n in range(NQ):
                pool.wait_ge(S3["normed_copied"], n + 1 + PRIME)
                g.tensor_tensor(x_lo[:, tokens(n)], x2T[:, tokens(n)], x_hi[:, tokens(n)].bitcast(F32), ALU.subtract).then_inc(S4["x_split"], 1)
            g.memset(y_sum, 0.0)

            def split_weights(e, p, loads):
                pool.wait_ge(W_[p], loads * 32)
                if not isinstance(e, int) or e >= 2:
                    pool.wait_ge(S4["result_made"], e * NQ - NQ + PRIME)
                g.tensor_tensor(w1_hi[p], w1[:, p], ones[:, 0:1].to_broadcast([128, FF]), ALU.mult)
                g.tensor_tensor(w2_hi[p], w2[:, p], ones[:, 0:1].unsqueeze(2).to_broadcast([128, FC, 128]), ALU.mult).then_inc(S4["weights_high"], 1)
                pool.wait_ge(S4["weights_high"], e + 1 + PRIME)
                g.tensor_tensor(w1_lo[p], w1[:, p], w1_hi[p].bitcast(F32), ALU.subtract)
                g.tensor_tensor(w2_lo[p], w2[:, p], w2_hi[p].bitcast(F32), ALU.subtract).then_inc(S4["weights_split"], 1)
            for e in range(NE // 2):
                split_weights(e, e % 2, e // 2 + 1)
            with pool.Fori(0, NE // 4) as i:
                for k in range(4 * NQ):
                    if k % (2 * NQ) == 0:
                        split_weights(i * 2 + (NE // 2 + k // (2 * NQ)), k // (2 * NQ), i + (NE // 4 + 1))
                    p = (k // NQ) % 2
                    pool.wait_ge(G_[p], (i * 2 + (k // (2 * NQ) + 1)) * 16)
                    pool.wait_ge(S4["result_copied"], i * (4 * NQ) + (k + 1) + PRIME)
                    g.tensor_tensor(results[:, k], results[:, k], gates[p][:, k % NQ], ALU.mult).then_inc(S4["result_gated"], 1)
            for n in range(NQ):
                q = quads3[n]
                pool.wait_ge(S4["variance_ready"], n + 1 + PRIME)
                g.tensor_tensor(q.rstd, q.ve, minus_half[0:TT], ALU.pow).then_inc(S4["rstd_ready"], 1)

        @block.scalar
        def _(act):
            a = nc.scalar
            for n in range(NQ):
                act.wait_ge(S1["x_transposed"], n + 1 + PRIME)
                a.copy(quads1[n].xT, bank[n % 2][:, 0:QC]).then_inc(S1["x_copied"], 1)
            for n in range(NQ):
                act.wait_ge(S1["u_made"], n + 1 + PRIME)
                a.copy(quads1[n].u, bank[2 + n % 2][:, 0:QC]).then_inc(S1["u_copied"], 1)
            for n in range(NQ):
                act.wait_ge(S1["values_made"], n + 1 + PRIME)
                a.copy(quads1[n].v, bank[4 + n % 2][0:TT, :].rearrange("p (t d) -> p t d", t=QT)).then_inc(S1["values_copied"], 1)
            for c in range(NB):
                act.wait_ge(F["context_transposed"], c + 1 + PRIME)
                a.copy(ctxT2[0:DC, 0, c * KB:c * KB + KB], bank[FIRST_CONTEXT[c]][0:DC, 0:KB]).then_inc(F["context_copied"], 1)
            for n in range(NQ):
                act.wait_ge(S1["max_subtracted"], n + 1 + PRIME)
                a.activation(quads1[n].e, quads1[n].s, ACT.Exp).then_inc(S1["exp_done"], 1)
            for n in range(NB):
                act.wait_ge(F["keys_made"], n + 1 + PRIME)
                a.copy(K_lo[:, n * KB:n * KB + KB], bank[FIRST_KEYS[n]][:, 0:KB]).then_inc(F["keys_copied"], 1)
                act.wait_ge(F["keys_copied"], n + 1 + PRIME)
                a.copy(K_hi[:, 0, n * KB:n * KB + KB], K_lo[:, n * KB:n * KB + KB]).then_inc(F["keys_high"], 1)
            for n in range(NQ):
                act.wait_ge(S1["weights_transposed"], n + 1 + PRIME)
                a.copy(quads1[n].aT, bank[n % 2][0:TT, 0:QC].rearrange("p (t k) -> p t k", t=QT)).then_inc(S1["weights_copied"], 1)
            for n in range(NQ):
                act.wait_ge(S1["normed_transposed"], n + 1 + PRIME)
                a.copy(quads1[n].xT, bank[4 + n % 2][:, 0:QC]).then_inc(S1["normed_copied"], 1)
            act.wait_ge(F["ones_ready"], 1 + PRIME)

            def period(b, par, half):
                for c in range(NC):
                    if c == 1 and has(b, -1):
                        act.wait_ge(F["outputs_made"], b * NC + PRIME)
                        if not isinstance(b, int) or b >= 2:
                            act.wait_ge(F["outputs_scaled"], b - 1 + PRIME)
                        a.copy(O_sb, bank[6][:, 0:SLOTS * S]).then_inc(F["outputs_copied"], 1)
                    if has(b, 0):
                        act.wait_ge(F["scores_made"], b * NC + (c + 1) + PRIME)
                        if not (isinstance(b, int) and b == 0 and c < 2):
                            act.wait_ge(F["outputs_made"], b * NC + (c - 1) + PRIME)
                        a.activation(P2[c % 2].rearrange("p (n k) -> p n k", n=2), psum[0:CK, 2 + 2 * (c % 2):4 + 2 * (c % 2), 0:HQ // 2], ACT.Exp)\
                         .then_inc(F["weights_ready"], 1)
                    if c < 3 and has(b, 2) and not (isinstance(b, int) and b == -2):
                        act.wait_ge(F["context_transposed"], b * NB + (2 * NB + c + 1) + PRIME)
                        if not isinstance(b, int) or b >= 0:
                            act.wait_ge(F["values_made"], (b + 1) * NB + PRIME)
                        a.copy(ctxT2[0:DC, par, c * KB:c * KB + KB], bank[7][0:DC, 0:KB]).then_inc(F["context_copied"], 1)
                    if 3 <= c < 6 and has(b, 2) and not (isinstance(b, int) and b == -2):
                        n = c - 3
                        act.wait_ge(F["keys_made"], b * NB + (2 * NB + n + 1) + PRIME)
                        if not isinstance(b, int) or b >= 0:
                            act.wait_ge(F["max_scores_made"], (b + 1) * PIECES + PRIME)
                            act.wait_ge(D_[f"khi{par}"], (half + 1) * (16 * 2 * HG))
                        if not isinstance(b, int) or b >= -1:
                            act.wait_ge(D_[f"klo{1 - par}"], (half + (par + 1)) * (16 * HG))
                        a.copy(K_lo[:, n * KB:n * KB + KB], bank[7][:, 0:KB]).then_inc(F["keys_copied"], 1)
                        act.wait_ge(F["keys_copied"], b * NB + (2 * NB + n + 1) + PRIME)
                        a.copy(K_hi[:, par, n * KB:n * KB + KB], K_lo[:, n * KB:n * KB + KB]).then_inc(F["keys_high"], 1)
                    if c in V_SLOTS and has(b, 1):
                        n = V_SLOTS.index(c)
                        act.wait_ge(F["values_made"], b * NB + (NB + n + 1) + PRIME)
                        if not isinstance(b, int) or b >= 1:
                            act.wait_ge(F["outputs_made"], b * NC + PRIME)
                        src = bank[7][0:CK, :].rearrange("p (c k) -> p c k", c=4)
                        three = V2[1 - par][:, 4 * n:4 * n + 4, 0:4 * V3].rearrange("p c (m r) -> p c m r", r=V3)
                        one = V2[1 - par][:, 4 * n:4 * n + 4, 4 * V3:VC].rearrange("p c (m r) -> p c m r", r=V1)
                        a.copy(three[:, :, :, 1:V3], src[:, :, 0:96].rearrange("p c (m r) -> p c m r", r=24))
                        a.copy(one[:, :, :, 1:V1], src[:, :, 96:128].rearrange("p c (m r) -> p c m r", r=DH)).then_inc(F["values_copied"], 1)
            periods(act, period)
            act.wait_ge(F["flag_ready"], 1 + PRIME)
            clamped = act.value_load(flag_int[0:1, 0:1], min_val=0, max_val=1)
            with act.If(clamped > 0), act.Fori(0, B) as i:
                for n in range(NB):
                    act.wait_ge(S2["context_transposed"], i + 1 + PRIME)
                    a.copy(ctxT[0:DC, n * KB:n * KB + KB], bank[n][0:DC, 0:KB]).then_inc(S2["context_copied"], 1)
                for n in range(NB):
                    act.wait_ge(S2["keys_made"], i + 1 + PRIME)
                    a.copy(KT[:, n * KB:n * KB + KB], bank[n][:, 0:KB]).then_inc(S2["keys_copied"], 1)
                for n in range(NB):
                    act.wait_ge(S2["values_made"], i + 1 + PRIME)
                    a.copy(V[:, 4 * n:4 * n + 4, :], bank[3 + n][0:CK, :].rearrange("p (c d) -> p c d", c=4)).then_inc(S2["values_copied"], 1)
                for j in range(G2):
                    act.wait_ge(S2["max_ready"], i * G2 + j + 1 + PRIME)
                    act.wait_ge(S2["weights_transposed"], i * G2 + j + PRIME)
                    a.activation(P[:], Sc[:], ACT.Exp, bias=negmax[:], accum_out=rowsum[:]).then_inc(S2["weights_ready"], 1)
                    for n in range(NB):
                        act.wait_ge(S2["weights_transposed"], i * G2 + j + 1 + PRIME)
                        a.copy(PT[:, 4 * n:4 * n + 4, :], bank[3 + n][0:CK, 0:4 * TT].rearrange("p (c q) -> p c q", c=4)).then_inc(S2["weights_copied"], 1)
                act.wait_ge(S2["outputs_transposed"], i + 1 + PRIME)
                a.copy(OT[:], bank[7][:, 0:2 * S].rearrange("p (a q) -> p a q", a=2)).then_inc(S2["transposed_copied"], 1)
            for n in range(NQ):
                act.wait_ge(S3["normed_transposed"], n + 1 + PRIME)
                a.copy(x2T[:, tokens(n)], bank[6 + n % 2][:, 0:QC])
                a.copy(x_hi[:, tokens(n)], bank[6 + n % 2][:, 0:QC]).then_inc(S3["normed_copied"], 1)
            act.wait_ge(S4["logits_shifted"], 1 + PRIME)
            a.activation(pw[:], pr[:], ACT.Exp).then_inc(S4["exp_done"], 1)

            def unit(u, k):
                for f in range(FC):
                    act.wait_ge(S4["hidden_made"], u * FC + (f + 1) + PRIME)
                    act.wait_ge(S4["result_made"], u - 1 + PRIME)
                    a.activation(h_hi[k % 2][:, f], bank[f][:, 0:QC], ACT.Relu).then_inc(S4["hidden_high"], 1)

            def result(u, p, slot):
                act.wait_ge(S4["result_made"], u + 1 + PRIME)
                if not isinstance(u, int) or u >= UNITS // 2:
                    act.wait_ge(S4["result_added"], u - (UNITS // 2 - 1) + PRIME)
                a.activation(results[:, bass.ds(slot, 1)], bank[4 + p][:, 0:QC].unsqueeze(1), ACT.Copy).then_inc(S4["result_copied"], 1)
            for u in range(UNITS // 2):
                unit(u, u)
                if u:
                    result(u - 1, (u - 1) % 2, u - 1)
            with act.Fori(0, NE // 4) as i:
                for k in range(2 * NQ):
                    u = i * (2 * NQ) + (UNITS // 2 + k)
                    unit(u, k)
                    result(u - 1, (k - 1) % 2, i * (2 * NQ) + (k - 1) if k else i * (-2 * NQ) + (UNITS // 2 - 1))
            result(UNITS - 1, 1, UNITS // 2 - 1)

        @block.vector
        def _(dve):
            v = nc.vector
            done = [0]

            def tie(base, sem_=dve_step):
                def step(ins):
                    done[0] += 1
                    ins.then_inc(sem_, 1)
                    dve.wait_ge(sem_, base + done[0])
                return step

            def norm(S_, quads, src, resid, dst):
                def statistics(n, q):
                    dve.wait_ge(S_["outputs_made"], n + 1 + PRIME)
                    v.tensor_tensor(q.y, src(n), resid(n), ALU.add).then_inc(S_["residual_added"], 1)
                    dve.wait_ge(S_["residual_added"], n + 1 + PRIME)
                    for t in range(QT):
                        last = v.bn_stats(q.stats[:, t, :], q.y[:, t, :])
                    step(last)
                    v.memset(q.pad, 0.0)
                    for t in range(QT):
                        last = v.bn_aggr(q.mv[:, t, :], q.stats[:, t, :])
                    step(last)
                    v.tensor_scalar(q.ve, q.mv[:, :, 1], EPS, None, ALU.add).then_inc(S_["variance_ready"], 1)

                def scale(n, q):
                    dve.wait_ge(S_["rstd_ready"], n + 1 + PRIME)
                    for t in range(QT):
                        last = v.tensor_scalar(dst[:, QT * n + t, :], q.y[:, t, :], q.mv[:, t, 0:1], q.rstd[:, t:t + 1], ALU.subtract, ALU.mult)
                    last.then_inc(S_["normed"], 1)
                step = tie(0)
                for n, q in enumerate(quads):
                    statistics(n, q)
                    if n:
                        scale(n - 1, quads[n - 1])
                scale(NQ - 1, quads[NQ - 1])

            def all_quads(n, ins):
                done[0] += 1
                ins.then_inc(dve_step, 1)
                if n == NQ - 1:
                    dve.wait_ge(dve_step, done[0])

            dve.wait_ge(w_ps, 1)
            v.tensor_copy(qk[:], bank[0][:, 0:128]).then_inc(w_ev, 1)
            v.tensor_copy(wvT[:], bank[1][:, 0:128]).then_inc(w_ev, 1)
            v.tensor_copy(WoP[:], bank[2][:].rearrange("p (s c) -> p s c", s=SLOTS)).then_inc(w_ev, 1)
            dve.wait_ge(more_weights, 16 * 8)
            step0 = tie(0)
            step0(v.tensor_scalar(bq_col[:], bq_col[:], DH ** -0.5, None, ALU.mult))

            dve.wait_ge(consts, 2)
            for n, q in enumerate(quads1):
                dve.wait_ge(S1["scores_made"], n + 1 + PRIME)
                v.scalar_tensor_tensor(q.s, bank[6 + n % 2][0:TT, 0:QC].rearrange("p (t q) -> p t q", t=QT), float(D) ** -0.5,
                                       other_batch[:].unsqueeze(1).to_broadcast([TT, QT, TT]), ALU.mult, ALU.add).then_inc(S1["scores_scaled"], 1)
            for n, q in enumerate(quads1):
                dve.wait_ge(S1["scores_scaled"], n + 1 + PRIME)
                all_quads(n, v.reduce_max(q.nm, q.s, AX.X))
            for n, q in enumerate(quads1):
                v.tensor_tensor(q.s, q.s, q.nm.unsqueeze(2).to_broadcast([TT, QT, TT]), ALU.subtract).then_inc(S1["max_subtracted"], 1)
            for n, q in enumerate(quads1):
                dve.wait_ge(S1["exp_done"], n + 1 + PRIME)
                all_quads(n, v.reduce_sum(q.rs, q.e, AX.X))
            for n, q in enumerate(quads1):
                all_quads(n, v.reciprocal(q.ri, q.rs))
            for n, q in enumerate(quads1):
                all_quads(n, v.tensor_tensor(q.e, q.e, causal[:].unsqueeze(1).to_broadcast([TT, QT, TT]), ALU.mult))
            for n, q in enumerate(quads1):
                v.tensor_tensor(q.s, q.e, q.ri.unsqueeze(2).to_broadcast([TT, QT, TT]), ALU.mult).then_inc(S1["weights_done"], 1)
            norm(S1, quads1, lambda n: bank[2 + n % 2][0:TT, :].rearrange("p (t d) -> p t d", t=QT), lambda n: quads1[n].xq, x1_all)
            step = tie(0)
            for n in range(NQ):
                dve.wait_ge(S1["queries_made"], n + 1 + PRIME)
                v.tensor_scalar(Qt_all[:, tokens(n)], bank[6 + n % 2][:, 0:QC], DH ** -0.5, bq_col[:], ALU.mult, ALU.add).then_inc(S1["queries_copied"], 1)
                dve.wait_ge(S1["queries_copied"], n + 1 + PRIME)
                step(v.tensor_copy(Q_hi[:, tokens(n)], Qt_all[:, tokens(n)]))
                v.tensor_tensor(Q_lo[:, tokens(n)], Qt_all[:, tokens(n)], Q_hi[:, tokens(n)].bitcast(F32), ALU.subtract).then_inc(S1["queries_split"], 1)

            step = tie(0)
            dve.wait_ge(S1["queries_split"], NQ + PRIME)
            step(v.memset(m_high, 0.0))
            step(v.memset(m_low, 0.0))
            step(v.memset(bank[6], 0.0))
            step(v.memset(chk_sum, 0.0))

            dve.sem_inc(F["bank_cleared"], 1)

            def period(b, par, half):
                for c in range(NC):
                    if c == 6 and has(b, 1):
                        dve.wait_ge(F["piece_max_taken"], (b + 2) * PIECES + PRIME)
                        if not isinstance(b, int) or b >= 0:
                            dve.wait_ge(F["max_transposed"], b + 1 + PRIME)
                            dve.wait_ge(F["extremes_kept"], (b + 1) * 2 + PRIME)
                        v.reduce_max(m2x, mx, AX.X).then_inc(F["row_max_taken"], 1)
                        dve.wait_ge(F["row_max_taken"], b + 2 + PRIME)
                        v.tensor_tensor(m_high, m_high, m2x, ALU.max).then_inc(F["extremes_kept"], 1)
                        v.tensor_tensor(m_low, m_low, m2x, ALU.min).then_inc(F["extremes_kept"], 1)
                    for ahead, n in pieces(c):
                        if not has(b, ahead):
                            continue
                        dve.wait_ge(F["max_scores_made"], b * PIECES + (ahead * PIECES + n + 1) + PRIME)
                        if n == 0 and (not isinstance(b, int) or b >= -1):
                            dve.wait_ge(F["row_max_taken"], b + 2 + PRIME)
                        v.reduce_max(mx[:, n // NB, n % NB:n % NB + 1], bank_of(n)[:, 0:KB], AX.X).then_inc(F["piece_max_taken"], 1)
                    if c == 7 and has(b, 1):
                        dve.wait_ge(F["max_transposed"], b + 2 + PRIME)
                        if not isinstance(b, int) or b >= 0:
                            dve.wait_ge(D_["mrow"], (b + 1) * (16 * RG))
                        v.tensor_scalar(max_row[:], bank[1][0:RG, 0:128], -1.0, None, ALU.mult).then_inc(F["max_row_ready"], 1)
                    if c in (6, 7) and has(b, -1):
                        if c == 6:
                            dve.wait_ge(F["sums_spread"], b + PRIME)
                            if not isinstance(b, int) or b >= 2:
                                dve.wait_ge(F["outputs_scaled"], b - 1 + PRIME)
                        part = slice((c - 6) * (SLOTS * S // 2), (c - 5) * (SLOTS * S // 2))
                        v.reciprocal(R_sb[:, part], bank[7][:, part]).then_inc(F["sums_inverted"], 1)
                    if c == 7 and has(b, -1):
                        dve.wait_ge(F["sums_inverted"], 2 * b + PRIME)
                        if not isinstance(b, int) or b >= 2:
                            dve.wait_ge(F["check_added"], b - 1 + PRIME)
                        v.scalar_tensor_tensor(OS_all[:, :, bass.ds((b - 1) * S, S)], O_sb.rearrange("p (s q) -> p s q", s=SLOTS), 1.0,
                                               R_sb.rearrange("p (s q) -> p s q", s=SLOTS), ALU.mult, ALU.mult, accum_out=chk).then_inc(F["outputs_scaled"], 1)
                        dve.wait_ge(F["outputs_scaled"], b + PRIME)
                        v.tensor_tensor(chk_sum, chk_sum, chk, ALU.add).then_inc(F["check_added"], 1)
            periods(dve, period)
            dve.wait_ge(F["check_added"], B + PRIME)
            dve.wait_ge(F["extremes_kept"], 2 * B + PRIME)
            step(v.tensor_scalar(m_low, m_low, -1.0, None, ALU.mult))
            step(v.tensor_tensor(m_high, m_high, m_low, ALU.max))
            step(v.reduce_max(bad[:, 0:1], m_high, AX.X))
            step(v.tensor_scalar(bad[:, 0:1], bad[:, 0:1], PLAIN, None, ALU.is_ge))
            step(v.tensor_scalar(bad[:, 1:2], chk_sum, 0.0, None, ALU.is_ge))
            step(v.tensor_scalar(bad[:, 1:2], bad[:, 1:2], -1.0, -1.0, ALU.add, ALU.mult))
            step(v.tensor_tensor(bad[:, 1:2], bad[:, 1:2], sum_row[:], ALU.mult))
            v.tensor_tensor(bad[:, 0:1], bad[:, 0:1], bad[:, 1:2], ALU.add).then_inc(F["bad_ready"], 1)
            dve.wait_ge(F["bad_summed"], 1 + PRIME)
            v.tensor_scalar(flag_int[:], bank[0][0:1, 0:1], 0.5, None, ALU.is_ge).then_inc(F["flag_ready"], 1)
            dve.wait_ge(F["flag_ready"], 1 + PRIME)
            clamped = dve.value_load(flag_int[0:1, 0:1], min_val=0, max_val=1)
            with dve.If(clamped > 0):
                outer, done[0] = done[0], 0
                step = tie(0, clamp_step)
                step(v.memset(ctxT[DC:DC + 1, :], 1.0))
                step(v.memset(numbers, float(NK)))

                K2 = G2 * 7
                base0 = done[0]
                with dve.Fori(0, B) as i:
                    done[0] = base0
                    step = tie(i * K2, clamp_step)
                    dve.wait_ge(S2["scores_made"], i * G2 + PRIME)
                    dve.wait_ge(S1["queries_copied"], NQ + PRIME)
                    v.tensor_tensor(Qbd[:], Qt_all[:, bass.ts(i, S)].unsqueeze(1).to_broadcast([128, H, S]),
                                    head_rows[:].unsqueeze(2).to_broadcast([128, H, S]), ALU.mult).then_inc(S2["queries_spread"], 1)
                    for j in range(G2):
                        n = i * G2 + j
                        dve.wait_ge(S2["scores_made"], n + 1 + PRIME)
                        dve.wait_ge(S2["weights_ready"], n + PRIME)
                        src = psum[0:TT, 0:NB, 0:KB]
                        step(v.tensor_scalar(view3(Sc, KB), src, 0.0, 0.0, ALU.is_ge, ALU.add, accum_out=c1[:]))
                        step(v.tensor_scalar(view3(Sc, KB), src, 0.0, 0.0, ALU.is_lt, ALU.add, accum_out=c2[:]))
                        step(v.tensor_scalar(view3(Sc, KB), src, CLAMP, -CLAMP, ALU.min, ALU.max, accum_out=rowmax[:]))
                        step(v.tensor_tensor(c1[:], c1[:], c2[:], ALU.add))
                        step(v.tensor_tensor(numbers[:], numbers[:], c1[:], ALU.min))
                        step(v.tensor_scalar(Sc[:], Sc[:], -CLAMP, None, ALU.max))
                        v.tensor_scalar(negmax[:], rowmax[:], -1.0, None, ALU.mult).then_inc(S2["max_ready"], 1)
                        dve.wait_ge(S2["weights_ready"], n + 1 + PRIME)
                        step(v.reciprocal(rinv[:], rowsum[:]))
                        dve.wait_ge(S2["outputs_made"], n + 1 + PRIME)
                        v.scalar_tensor_tensor(Om[:, 16 * j:16 * j + 16].rearrange("p (a d) -> p a d", a=2),
                                               bank[6][0:TT, 0:16].rearrange("p (a d) -> p a d", a=2), rinv[:],
                                               pair_rows[:].unsqueeze(2).to_broadcast([TT, 2, DH]), ALU.mult, ALU.mult).then_inc(S2["outputs_masked"], 1)
                    dve.wait_ge(S2["outputs_placed"], i + 1 + PRIME)
                    v.tensor_scalar(OS_all[:, :, bass.ts(i, S)], bank[6][:, 0:SLOTS * S].rearrange("p (s q) -> p s q", s=SLOTS), 1.0, None, ALU.mult).then_inc(S2["outputs_stored"], 1)
                    v.tensor_scalar(OM_all[:, :, bass.ds(i, 1)], bank[6][:, SLOTS * S:2 * SLOTS * S].rearrange("p (s q) -> p s q", s=SLOTS)[:, :, 0:1], 1.0 / NK,
                                    None, ALU.mult).then_inc(S2["outputs_stored"], 1)
                    assert done[0] - base0 == K2, done[0] - base0
                done[0] = base0 + B * K2
                step = tie(0, clamp_step)
                v.tensor_scalar(nan_mask[:], numbers[:], float(NK), None, ALU.is_lt).then_inc(S2["nan_rows"], 1)
                dve.wait_ge(S2["nan_summed"], 1 + PRIME)
                step(v.tensor_scalar(nan_col[:], bank[0][:, 0:1], 0.5, None, ALU.is_ge))
                step(v.tensor_copy(nan_int[:], nan_col[:]))
                dve.wait_ge(S2["outputs_stored"], 2 * B + PRIME)
                v.copy_predicated(OS_all[:].rearrange("p s (b q) -> p (s b) q", q=S), nan_int.unsqueeze(2).to_broadcast([128, SLOTS * B, S]),
                                  OM_all[:].rearrange("p s b -> p (s b)").unsqueeze(2).to_broadcast([128, SLOTS * B, S])).then_inc(S2["nan_fixed"], 1)
                dve.wait_ge(S2["nan_fixed"], 1 + PRIME)
                done[0] = outer

            dve.sem_inc(S3["attended"], 1)
            norm(S3, quads3, lambda n: bank[4 + n % 2][0:TT, :].rearrange("p (t d) -> p t d", t=QT), lambda n: x1_all[:, tiles(n), :], x2_all)
            step = tie(0)

            def low_part(u, k, f):
                dve.wait_ge(S4["hidden_high"], u * FC + (f + 1) + PRIME)
                v.scalar_tensor_tensor(h_lo[k % 2][:, f], bank[f][:, 0:QC], 0.0, h_hi[k % 2][:, f].bitcast(F32), ALU.max, ALU.subtract)\
                 .then_inc(S4["hidden_low"], 1)

            def wide(t):
                return t[:].unsqueeze(2).to_broadcast([TT, NT, NE])
            dve.wait_ge(S4["logits_made"], 1 + PRIME)
            lg = bank[7][0:TT, 0:NT * NE].rearrange("p (t e) -> p t e", e=NE)
            step(v.reduce_max(m1[:], lg, AX.X))
            v.tensor_tensor(pr[:], lg, wide(m1), ALU.subtract).then_inc(S4["logits_shifted"], 1)
            dve.wait_ge(S4["exp_done"], 1 + PRIME)
            early = iter(range(EARLY))

            def step_and_low(ins):
                done[0] += 1
                ins.then_inc(dve_step, 1)
                for n in islice(early, 1):
                    low_part(n // FC, n // FC, n % FC)
                dve.wait_ge(dve_step, done[0])
            step(v.reduce_sum(m1[:], pw[:], AX.X))
            step(v.reciprocal(m2[:], m1[:]))
            step(v.tensor_tensor(pr[:], pw[:], wide(m2), ALU.mult))
            step(v.tensor_copy(pw[:], pr[:]))
            for k in range(TOPK):
                step_and_low(v.reduce_max(m1[:], pw[:], AX.X))
                step_and_low(v.tensor_tensor(eq[:], pw[:], wide(m1), ALU.is_equal))
                step_and_low(v.tensor_tensor(eq[:], eq[:], index_prio[:].unsqueeze(1).to_broadcast([TT, NT, NE]), ALU.mult))
                step_and_low(v.reduce_max(m2[:], eq[:], AX.X))
                step_and_low(v.tensor_tensor(hot[:], eq[:], wide(m2), ALU.is_equal))
                if k == 0:
                    step_and_low(v.tensor_copy(mask[:], hot[:]))
                    step_and_low(v.scalar_tensor_tensor(flat(pw), flat(hot), -2.0, flat(pw), ALU.mult, ALU.add))
                else:
                    step_and_low(v.tensor_tensor(mask[:], mask[:], hot[:], ALU.add))
            step(v.tensor_tensor(pr[:], pr[:], mask[:], ALU.mult))
            step(v.scalar_tensor_tensor(flat(pr), flat(mask), 1.0, flat(pr), ALU.subtract, ALU.add))
            assert not list(early)
            v.tensor_copy(gsel[:], pr[:].rearrange("p t e -> p e t")).then_inc(S4["gates_ready"], 1)
            dve.wait_ge(S4["gates_transposed"], 1 + PRIME)
            step(v.tensor_copy(G[:], bank[7][:, 0:TT]))

            rounds = [0]

            def count(op, where):
                v.tensor_scalar(gscr[:], G[:], where, 0.0, op, ALU.add, accum_out=cnt[:, 0:1]).then_inc(S4["counted"], 1)
                for n in low_parts(rounds[0]):
                    low_part(n // FC, n // FC, n % FC)
                rounds[0] += 1
                dve.wait_ge(S4["total_made"], rounds[0] + PRIME)
                return bank[6][:, 0:1]

            for s in (64, 32, 16, 8, 4, 2, 1):
                step(v.tensor_scalar(cand[:], thr[:], 2.0 ** -(s - 1), None, ALU.mult))
                tot = count(ALU.is_ge, cand[:])
                step(v.tensor_scalar(fac[:], tot, float(CAP), 2.0 ** -s, ALU.is_ge, ALU.max))
                step(v.tensor_tensor(thr[:], thr[:], fac[:], ALU.mult))
            step(v.tensor_scalar(bits[:], halves[:], thr[:], None, ALU.mult))
            step(v.tensor_scalar(cand[:], thr[:], 1.5, None, ALU.mult))
            for s in range(23):
                bit, less = bits[:, s:s + 1], bits[:, min(s + 1, 22):min(s + 1, 22) + 1]
                tot = count(ALU.is_ge, cand[:])
                step(v.tensor_scalar(fac[:], tot, float(CAP), bit, ALU.is_ge, ALU.mult))
                step(v.scalar_tensor_tensor((cand if s < 22 else thr)[:], fac[:], less, cand[:], ALU.subtract, ALU.add))
            tot = count(ALU.is_ge, 0.0)
            step(v.tensor_scalar(fac[:], tot, float(CAP), None, ALU.is_ge))
            step(v.tensor_tensor(thr[:], thr[:], fac[:], ALU.mult))
            tot = count(ALU.is_gt, thr[:])
            assert rounds[0] == ROUNDS
            step(v.tensor_scalar(room[:], tot, -1.0, float(CAP), ALU.mult, ALU.add))
            step(v.tensor_scalar(gtm[:], G[:], thr[:], None, ALU.is_gt))
            step(v.tensor_scalar(eqm[:], G[:], thr[:], None, ALU.is_equal))
            step(v.tensor_tensor_scan(pref[:], eqm[:], zeros[:], 0.0, ALU.add, ALU.add))
            v.tensor_copy(cnt[:, 1:2], pref[:, TT - 1:TT]).then_inc(S4["equal_counted"], 1)
            dve.wait_ge(S4["equal_before_made"], 1 + PRIME)
            step(v.tensor_tensor(room[:], room[:], bank[6][:, 0:1], ALU.subtract))
            step(v.tensor_scalar(pref[:], pref[:], room[:], None, ALU.is_le))
            step(v.tensor_tensor(eqm[:], eqm[:], pref[:], ALU.mult))
            step(v.tensor_tensor(gtm[:], gtm[:], eqm[:], ALU.add))
            v.tensor_tensor(Gs[:], G[:], gtm[:], ALU.mult).then_inc(S4["gates_final"], 1)
            for n in range(low_parts(ROUNDS - 1).stop, FC * UNITS // 2):
                low_part(n // FC, n // FC, n % FC)

            def unit(u, k):
                for f in range(FC):
                    low_part(u, k, f)
                for a2 in range(2):
                    n = u * 2 + (a2 - UNITS)
                    dve.wait_ge(S4["result_gated"], n + 1 + PRIME)
                    dve.wait_ge(S4["result_added"], n - (NQ - 1) + PRIME)
                    q = (2 * k + a2) % NQ
                    v.tensor_tensor(y_sum[:, q], y_sum[:, q], results[:, 2 * k + a2], ALU.add).then_inc(S4["result_added"], 1)
            experts_after(dve, unit)
            norm(S4, quads3, lambda n: bank[n][0:TT, :].rearrange("p (t d) -> p t d", t=QT), lambda n: x2_all[:, tiles(n), :], x2_all)

        @block.tensor
        def _(pe):
            t_ = nc.tensor
            mm = t_.matmul
            pe.wait_ge(weights, 16 * 4)
            pe.wait_ge(consts, 1)
            mm(bank[0][:, 0:128], w_sb["wq"][:], w_sb["wk"][:], start=True, stop=True)
            t_.transpose(bank[1][:, 0:128], w_sb["wv"][:], ident[:])
            for s in range(SLOTS):
                last = mm(bank[2][:, 128 * s:128 * s + 128], perm[:, s, :], w_sb["xWo"][:], start=True, stop=True)
            last.then_inc(w_ps, 1)
            pe.wait_ge(w_ev, 3)
            for n, q in enumerate(quads1):
                pe.wait_ge(X_[n], 16)
                pe.wait_ge(S1["x_copied"], n - 1 + PRIME)
                for t in range(QT):
                    last = t_.transpose(bank[n % 2][:, TT * t:TT * t + TT], q.xq[:, t, :], ident[0:TT, 0:TT])
                last.then_inc(S1["x_transposed"], 1)
            for n, q in enumerate(quads1):
                pe.wait_ge(S1["x_copied"], n + 1 + PRIME)
                pe.wait_ge(S1["u_copied"], n - 1 + PRIME)
                mm(bank[2 + n % 2][:, 0:QC], qk[:], q.xT, start=True, stop=True).then_inc(S1["u_made"], 1)
            for n, q in enumerate(quads1):
                pe.wait_ge(S1["u_copied"], n + 1 + PRIME)
                pe.wait_ge(S1["scores_scaled"], n - 1 + PRIME)
                for t in range(QT):
                    last = mm(bank[6 + n % 2][0:TT, TT * t:TT * t + TT], q.xT[:, TT * t:TT * t + TT], q.u[:, TT * t:TT * t + TT], start=True, stop=True)
                last.then_inc(S1["scores_made"], 1)
            for n, q in enumerate(quads1):
                pe.wait_ge(S1["values_copied"], n - 1 + PRIME)
                for t in range(QT):
                    last = mm(bank[4 + n % 2][0:TT, D * t:D * t + D], q.xT[:, TT * t:TT * t + TT], wvT[:], start=True, stop=True)
                last.then_inc(S1["values_made"], 1)
            pe.wait_ge(D_["c"], 16)
            for c in range(NB):
                for k in range(4):
                    last = t_.transpose(bank[FIRST_CONTEXT[c]][0:DC, CK * k:CK * k + CK], C2[:, 4 * c + k, :], ident[0:CK, 0:CK])
                last.then_inc(F["context_transposed"], 1)
            pe.wait_ge(F["ones_ready"], 1 + PRIME)
            pe.wait_ge(S1["values_copied"], NQ + PRIME)
            pe.wait_ge(more_weights, 16 * 8)
            for n in range(NB):
                pe.wait_ge(F["context_copied"], NB + PRIME)
                mm(bank[FIRST_KEYS[n]][:, 0:KB], WkA[:], ctxT2[:, 0, n * KB:n * KB + KB], start=True, stop=True).then_inc(F["keys_made"], 1)
            for n, q in enumerate(quads1):
                pe.wait_ge(S1["weights_done"], n + 1 + PRIME)
                pe.wait_ge(S1["weights_copied"], n - 1 + PRIME)
                for t in range(QT):
                    last = t_.transpose(bank[n % 2][0:TT, TT * t:TT * t + TT], q.s[:, t, :], ident[0:TT, 0:TT])
                last.then_inc(S1["weights_transposed"], 1)

            def attend(n, q):
                pe.wait_ge(S1["values_copied"], n + 1 + PRIME)
                pe.wait_ge(S1["weights_copied"], n + 1 + PRIME)
                pe.wait_ge(S1["residual_added"], n - 1 + PRIME)
                for t in range(QT):
                    last = mm(bank[2 + n % 2][0:TT, D * t:D * t + D], q.aT[:, t, :], q.v[:, t, :], start=True, stop=True)
                last.then_inc(S1["outputs_made"], 1)

            def query(n, q):
                pe.wait_ge(S1["normed"], n + 1 + PRIME)
                for t in range(QT):
                    last = t_.transpose(bank[4 + n % 2][:, TT * t:TT * t + TT], x1_all[:, QT * n + t, :], ident[0:TT, 0:TT])
                last.then_inc(S1["normed_transposed"], 1)
                pe.wait_ge(S1["normed_copied"], n + 1 + PRIME)
                pe.wait_ge(S1["queries_copied"], n - 1 + PRIME)
                mm(bank[6 + n % 2][:, 0:QC], w_sb["xWq"][:], q.xT, start=True, stop=True).then_inc(S1["queries_made"], 1)
            pe.wait_ge(F["keys_copied"], NB + PRIME)
            for n, q in enumerate(quads1):
                attend(n, q)
                if n >= 2:
                    query(n - 2, quads1[n - 2])
            for n in range(NQ - 2, NQ):
                query(n, quads1[n])
            pe.wait_ge(consts, 2)
            pe.wait_ge(S1["queries_copied"], NQ + PRIME)


            def period(b, par, half):
                for c in range(NC):
                    if has(b, 0):
                        if c == 0:
                            pe.wait_ge(D_[f"khi{par}"], (half + 1) * (16 * 2 * HG))
                            pe.wait_ge(D_[f"klo{par}"], (half + 1) * (16 * HG))
                            pe.wait_ge(D_["mrow"], (b + 1) * (16 * RG))
                            pe.wait_ge(F["stacked_spread"], b + 1 + PRIME)
                        for g in range(HG):
                            last = mm(bank[2 + 2 * (c % 2) + g // 2][0:CK, 4 * S * (g % 2):4 * S * (g % 2) + 4 * S],
                                      K_st[0:DC + 1, par, g, c * CK:c * CK + CK], Q_st[:, par, g].rearrange("p h q -> p (h q)"), start=True, stop=True)
                        last.then_inc(F["scores_made"], 1)
                    if c < 3 and has(b, 2) and not (isinstance(b, int) and b == -2):
                        if c == 0:
                            pe.wait_ge(D_["c"], (b + 3) * 16)
                            if not isinstance(b, int) or b >= 0:
                                pe.wait_ge(F["values_copied"], (b + 1) * NB + PRIME)
                            else:
                                pe.wait_ge(F["keys_copied"], NB + PRIME)
                        else:
                            pe.wait_ge(F["context_copied"], b * NB + (2 * NB + c) + PRIME)
                        for k in range(4):
                            last = t_.transpose(bank[7][0:DC, CK * k:CK * k + CK], C2[:, 4 * c + k, :], ident[0:CK, 0:CK])
                        last.then_inc(F["context_transposed"], 1)
                    if 3 <= c < 6 and has(b, 2) and not (isinstance(b, int) and b == -2):
                        n = c - 3
                        if n == 0:
                            pe.wait_ge(F["context_copied"], b * NB + 3 * NB + PRIME)
                        else:
                            pe.wait_ge(F["keys_copied"], b * NB + (2 * NB + n) + PRIME)
                        mm(bank[7][:, 0:KB], WkA[:], ctxT2[:, par, n * KB:n * KB + KB], start=True, stop=True).then_inc(F["keys_made"], 1)
                    if c == 6 and has(b, -1):
                        pe.wait_ge(F["outputs_copied"], b + PRIME)
                        if has(b, 2):
                            pe.wait_ge(F["keys_copied"], b * NB + 3 * NB + PRIME)
                        elif has(b, 0):
                            pe.wait_ge(F["values_copied"], (b + 1) * NB + PRIME)
                        else:
                            pe.wait_ge(F["sums_inverted"], 2 * (b - 1) + PRIME)
                        mm(bank[7][:, 0:SLOTS * S], sum_rows[:], O_sb, start=True, stop=True).then_inc(F["sums_spread"], 1)
                    if c in V_SLOTS and has(b, 1):
                        n = V_SLOTS.index(c)
                        if n > 0:
                            pe.wait_ge(F["values_copied"], b * NB + (NB + n) + PRIME)
                        elif has(b, -1):
                            pe.wait_ge(F["sums_inverted"], 2 * b + PRIME)
                        elif has(b, 2):
                            pe.wait_ge(F["keys_copied"], b * NB + 3 * NB + PRIME)
                        for k in range(4):
                            q = 4 * n + k
                            last = mm(bank[7][0:CK, 128 * k:128 * k + 128], ctxT2[:, 1 - par, CK * q:CK * q + CK], WvA[:], start=True, stop=True)
                        last.then_inc(F["values_made"], 1)
                    for ahead, n in pieces(c):
                        if not has(b, ahead):
                            if n == 1 and has(b, 1):
                                pe.wait_ge(F["row_max_taken"], b + 2 + PRIME)
                                mm(bank[1][0:RG, 0:128], m2x, ident[:], start=True, stop=True).then_inc(F["max_transposed"], 1)
                            continue
                        if n == 0:
                            pe.wait_ge(F["queries_spread"], b + (ahead + 1) + PRIME)
                        if n < NB:
                            pe.wait_ge(F["keys_high"], b * NB + (ahead * NB + n + 1) + PRIME)
                        if n == 1:
                            if has(b, 1):
                                pe.wait_ge(F["row_max_taken"], b + 2 + PRIME)
                                mm(bank[1][0:RG, 0:128], m2x, ident[:], start=True, stop=True).then_inc(F["max_transposed"], 1)
                            pe.wait_ge(F["piece_max_taken"], b * PIECES + (ahead * PIECES + 1) + PRIME)
                        elif n == 2:
                            if has(b, 1):
                                pe.wait_ge(F["max_row_ready"], b + 2 + PRIME)
                        elif not (isinstance(b, int) and b + ahead == 0 and n == 0):
                            pe.wait_ge(F["piece_max_taken"], b * PIECES + (ahead * PIECES + n - 1) + PRIME)
                        p = (par + ahead) % 2
                        mm(bank_of(n)[:, 0:KB], Q_bd[:, p].rearrange("p h q -> p (h q)")[:, 128 * (n // NB):128 * (n // NB) + 128],
                           K_hi[:, p, (n % NB) * KB:(n % NB) * KB + KB], start=True, stop=True).then_inc(F["max_scores_made"], 1)
                    ago = -1 if c == 0 else 0
                    if has(b, ago):
                        k = (c - 1) % NC
                        if k == 0:
                            if isinstance(b, int) and b == 0:
                                pe.wait_ge(F["bank_cleared"], 1 + PRIME)
                            pe.wait_ge(F["values_copied"], (b + 1) * NB + PRIME)
                            if not isinstance(b, int) or b >= 1:
                                pe.wait_ge(F["outputs_copied"], b + PRIME)
                        pe.wait_ge(F["weights_ready"], b * NC + c + PRIME)
                        weights_, values = P2[k % 2], V2[(par + ago) % 2]
                        for m in range(4):
                            mm(bank[6][32 * m:32 * m + V3, 0:3 * S], values[:, k, V3 * m:V3 * m + V3], weights_[:, 3 * S * m:3 * S * m + 3 * S],
                               start=(k == 0), stop=(k == NC - 1), skip_group_check=True)
                        for m in range(4):
                            last = mm(bank[6][32 * m:32 * m + V1, 3 * S:4 * S], values[:, k, 4 * V3 + V1 * m:4 * V3 + V1 * m + V1],
                                      weights_[:, (12 + m) * S:(13 + m) * S], start=False, stop=(k == NC - 1), skip_group_check=True)
                        last.then_inc(F["outputs_made"], 1)
            periods(pe, period)
            pe.wait_ge(F["bad_ready"], 1 + PRIME)
            mm(bank[0][:, 0:1], ones[:], bad[:, 0:1], start=True, stop=True).then_inc(F["bad_summed"], 1)
            pe.wait_ge(F["flag_ready"], 1 + PRIME)
            clamped = pe.value_load(flag_int[0:1, 0:1], min_val=0, max_val=1)
            with pe.If(clamped > 0):
                with pe.Fori(0, B) as i:
                    pe.wait_ge(S2["context_loaded"], (i + 1) * 16)
                    pe.wait_ge(S2["queries_spread"], i + 1 + PRIME)
                    pe.wait_ge(S2["max_ready"], i * G2 + PRIME)
                    for c in range(NC):
                        last = t_.transpose(bank[c // 4][0:DC, CK * (c % 4):CK * (c % 4) + CK], C[:, c, :], ident[0:CK, 0:CK])
                    last.then_inc(S2["context_transposed"], 1)
                    pe.wait_ge(S2["context_copied"], i * NB + NB + PRIME)
                    for n in range(NB):
                        last = mm(bank[n][:, 0:KB], WkA[:], ctxT[:, KB * n:KB * n + KB], start=True, stop=True)
                    last.then_inc(S2["keys_made"], 1)
                    pe.wait_ge(S2["weights_copied"], i * (G2 * NB) + PRIME)
                    for c in range(NC):
                        last = mm(bank[3 + c // 4][0:CK, 128 * (c % 4):128 * (c % 4) + 128], ctxT[:, CK * c:CK * c + CK], WvA[:], start=True, stop=True)
                    last.then_inc(S2["values_made"], 1)
                    pe.wait_ge(S2["keys_copied"], i * NB + NB + PRIME)
                    pe.wait_ge(S2["values_copied"], i * NB + NB + PRIME)
                    pe.wait_ge(S2["queries_spread"], i + 1 + PRIME)
                    for j in range(G2):
                        n = i * G2 + j
                        pe.wait_ge(S2["max_ready"], n + PRIME)
                        for c in range(NB):
                            last = mm(bank[c][0:TT, 0:KB], Qbd[:, 2 * j:2 * j + 2, :].rearrange("p h q -> p (h q)"), KT[:, KB * c:KB * c + KB],
                                      start=True, stop=True)
                        last.then_inc(S2["scores_made"], 1)
                        pe.wait_ge(S2["weights_ready"], n + 1 + PRIME)
                        pe.wait_ge(S2["weights_copied"], n * NB + PRIME)
                        for c in range(NC):
                            last = t_.transpose(bank[3 + c // 4][0:CK, TT * (c % 4):TT * (c % 4) + TT], P[:, CK * c:CK * c + CK], ident[0:TT, 0:TT])
                        last.then_inc(S2["weights_transposed"], 1)
                        pe.wait_ge(S2["weights_copied"], n * NB + NB + PRIME)
                        pe.wait_ge(S2["outputs_masked"], n + PRIME)
                        if j == 0:
                            pe.wait_ge(S2["outputs_stored"], i * 2 + PRIME)
                        for c in range(NC):
                            last = mm(bank[6][0:TT, 0:16], PT[:, c, :], V[:, c, 16 * j:16 * j + 16], start=(c == 0), stop=(c == NC - 1))
                        last.then_inc(S2["outputs_made"], 1)
                    pe.wait_ge(S2["outputs_masked"], i * G2 + G2 + PRIME)
                    mm(bank[7][:, 0:S], Om[:], fold_q[:], start=True, stop=True)
                    for c in range(NC):
                        last = mm(bank[7][:, S:2 * S], V[:, c, :], ones[0:CK, 0:S], start=(c == 0), stop=(c == NC - 1))
                    last.then_inc(S2["outputs_transposed"], 1)
                    pe.wait_ge(S2["transposed_copied"], i + 1 + PRIME)
                    for a in range(2):
                        for s in range(SLOTS):
                            o = (a * SLOTS + s) * S
                            last = mm(bank[6][:, o:o + S], perm[:, s, :], OT[:, a, :], start=True, stop=True)
                    last.then_inc(S2["outputs_placed"], 1)
                pe.wait_ge(S2["nan_rows"], 1 + PRIME)
                mm(bank[0][:, 0:1], ones[0:TT, :], nan_mask[:], start=True, stop=True).then_inc(S2["nan_summed"], 1)

            pe.wait_ge(S3["attended"], 1 + PRIME)

            def project(n):
                pe.wait_ge(S3["residual_added"], n - 1 + PRIME)
                for t in range(QT):
                    for s in range(SLOTS):
                        mm(bank[4 + n % 2][0:TT, D * t:D * t + D], OS_all[:, s, QC * n + TT * t:QC * n + TT * t + TT], WoP[:, s, :], start=(s == 0), stop=False)
                    last = mm(bank[4 + n % 2][0:TT, D * t:D * t + D], ones[0:1, 0:TT], bo_row[:], start=False, stop=True)
                last.then_inc(S3["outputs_made"], 1)

            def transposed(n):
                pe.wait_ge(S3["normed"], n + 1 + PRIME)
                pe.wait_ge(S3["normed_copied"], n - 1 + PRIME)
                for t in range(QT):
                    last = t_.transpose(bank[6 + n % 2][:, TT * t:TT * t + TT], x2_all[:, QT * n + t, :], ident[0:TT, 0:TT])
                last.then_inc(S3["normed_transposed"], 1)
            for n in range(NQ):
                project(n)
                if n >= 2:
                    transposed(n - 2)
            for n in range(NQ - 2, NQ):
                transposed(n)
            pe.wait_ge(S3["normed_copied"], NQ + PRIME)
            for t in range(NT):
                last = mm(bank[7][0:TT, NE * t:NE * t + NE], x2T[:, TT * t:TT * t + TT], Wr_sb[:], start=True, stop=True)
            last.then_inc(S4["logits_made"], 1)

            def up(u, k, f, p):
                if k % NQ == 0 and f == 0:
                    pe.wait_ge(S4["weights_split"], p[1] + 1 + PRIME)
                pe.wait_ge(S4["hidden_low"], u * FC + (f - 3) + PRIME)
                cols = slice(QC * (k % NQ), QC * (k % NQ) + QC)
                w_cols = slice(128 * f, 128 * f + 128)
                mm(bank[f][:, 0:QC], w1_hi[p[0]][:, w_cols], x_hi[:, cols], start=True, stop=False)
                mm(bank[f][:, 0:QC], w1_hi[p[0]][:, w_cols], x_lo[:, cols], start=False, stop=False)
                mm(bank[f][:, 0:QC], w1_lo[p[0]][:, w_cols], x_hi[:, cols], start=False, stop=True).then_inc(S4["hidden_made"], 1)

            def down(u, k, f, p):
                if f == 0:
                    pe.wait_ge(S4["result_copied"], u - 1 + PRIME)
                pe.wait_ge(S4["hidden_low"], u * FC + (f + 1) + PRIME)
                dst = bank[4 + k % 2][:, 0:QC]
                mm(dst, w2_hi[p][:, f], h_hi[k % 2][:, f], start=(f == 0), stop=False)
                mm(dst, w2_hi[p][:, f], h_lo[k % 2][:, f], start=False, stop=False)
                last = mm(dst, w2_lo[p][:, f], h_hi[k % 2][:, f], start=False, stop=(f == FC - 1))
                if f == FC - 1:
                    last.then_inc(S4["result_made"], 1)
            pe.wait_ge(S4["x_split"], NQ + PRIME)
            rounds = 0
            for u in range(UNITS // 2):
                for f in range(FC):
                    if u * FC + f == EARLY:
                        pe.wait_ge(S4["gates_ready"], 1 + PRIME)
                        t_.transpose(bank[7][:, 0:TT], gsel[:].rearrange("p e t -> p (e t)"), ident[0:TT, 0:TT]).then_inc(S4["gates_transposed"], 1)
                    while rounds < ROUNDS and low_parts(rounds).stop <= u * FC + f:
                        pe.wait_ge(S4["counted"], rounds + 1 + PRIME)
                        mm(bank[6][:, 0:1], expert_rows[:], cnt[:, 0:1], start=True, stop=True).then_inc(S4["total_made"], 1)
                        rounds += 1
                    up(u, u, f, ((u // NQ) % 2, u // NQ))
                    if u:
                        down(u - 1, u - 1, f, ((u - 1) // NQ) % 2)
                    if rounds == ROUNDS and u * FC + f == low_parts(ROUNDS - 1).stop + 3:
                        pe.wait_ge(S4["equal_counted"], 1 + PRIME)
                        mm(bank[6][:, 0:1], before_rows[:], cnt[:, 1:2], start=True, stop=True).then_inc(S4["equal_before_made"], 1)
            with pe.Fori(0, NE // 4) as i:
                for k in range(2 * NQ):
                    u = i * (2 * NQ) + (UNITS // 2 + k)
                    for f in range(FC):
                        up(u, k, f, (k // NQ, i * 2 + (NE // 2 + k // NQ)))
                        down(u - 1, k - 1, f, ((k - 1) // NQ) % 2)
            for f in range(FC):
                down(UNITS - 1, UNITS - 1, f, 1)
            for n in range(NQ):
                pe.wait_ge(S4["result_added"], UNITS - NQ + n + 1 + PRIME)
                for t in range(QT):
                    last = t_.transpose(bank[n][0:TT, D * t:D * t + D], y_sum[:, n, TT * t:TT * t + TT], ident[:])
                last.then_inc(S4["outputs_made"], 1)


def tokens(n):
    return slice(QC * n, QC * n + QC)


def tiles(n):
    return slice(QT * n, QT * n + QT)


def low_parts(r):
    return range(EARLY + r * BETWEEN // ROUNDS, EARLY + (r + 1) * BETWEEN // ROUNDS)


def flat(t):
    return t[:].rearrange("p t e -> p (t e)")


def view3(t, cols):
    return t[:].rearrange("p (n k) -> p n k", k=cols)



_INS = ["x", "ctx_768", "L0_attn_wq", "L0_attn_wk", "L0_attn_wv", "L0_xattn_Wq", "L0_xattn_bq", "L0_xattn_Wk",
        "L0_xattn_bk", "L0_xattn_Wv", "L0_xattn_bv", "L0_xattn_Wo", "L0_xattn_bo", "L0_ffn_Wr", "L0_ffn_W1", "L0_ffn_W2"]


def kernel(**inputs):
    import numpy as np
    import concourse.bacc as bacc
    from concourse.bass_utils import run_bass_kernel_spmd

    nc = bacc.Bacc("TRN2", target_bir_lowering=False, num_devices=1)
    arrays, args = {}, []
    for name in _INS:
        a = np.ascontiguousarray(inputs[name])
        arrays[f"in_{name}"] = a
        args.append(nc.dram_tensor(f"in_{name}", a.shape, mybir.dt.from_np(a.dtype), kind="ExternalInput").ap())
    out = nc.dram_tensor("out", (B, S, D), F32, kind="ExternalOutput").ap()
    gate_rows = nc.dram_tensor("gate_rows", (NE, B * S), F32, kind="Internal").ap()
    decoder_kernel(nc, gate_rows, *args, out)
    r = run_bass_kernel_spmd(nc, [arrays], core_ids=[0])
    return r.results[0]["out"]
```
